# Optimizing a Trainium2 kernel written in Bass

```python
import numpy as np
import jax
import jax.numpy as jnp

def _softmax(x, axis=-1):
    return jax.nn.softmax(x, axis=axis)

def _gelu(x):
    return jax.nn.gelu(x, approximate=True)

def _silu(x):
    return jax.nn.silu(x)

def _sigmoid(x):
    return jax.nn.sigmoid(x)

def _layernorm(x, axis=-1, eps=1e-05):
    m = jnp.mean(x, axis=axis, keepdims=True)
    v = jnp.var(x, axis=axis, keepdims=True)
    return (x - m) / jnp.sqrt(v + eps)

def _scatter_add(tgt, idx, src, axis=0):
    return tgt.at[idx].add(src)

def _segment_sum(src, seg, n):
    return jax.ops.segment_sum(src, seg, n)
kernel_name = 'mk_gps_d1_gnn_r8_be4e38'

def setup_inputs(seed: int=0):
    np.random.seed(seed)
    _w = jnp.asarray

    def _rec_inputs():
        import jax
        import jax.numpy as jnp
        _gk = jax.random.key(seed)
        x = -0.0002117 + 1 * jax.random.normal(jax.random.fold_in(_gk, 1), (6250, 256), jnp.float32)
        _s = jax.random.randint(jax.random.fold_in(_gk, 2), (100000,), 0, 6250, jnp.int32)
        _d = jax.random.randint(jax.random.fold_in(_gk, 3), (100000,), 0, 6250, jnp.int32)
        _loop = jnp.arange(6250, dtype=jnp.int32)
        src = jnp.concatenate([_s, _d, _loop])
        dst = jnp.concatenate([_d, _s, _loop])
        _o = jnp.argsort(dst, stable=True)
        src = src[_o]
        dst = dst[_o]
        edge_attr_2 = jax.random.uniform(jax.random.fold_in(_gk, 11), (206250, 2), jnp.float32, 0.0, 1)
        return (x, src, dst, edge_attr_2)
    x, src, dst, edge_attr_2 = _rec_inputs()

    def _L0_gnn_setup():
        import jax, jax.numpy as jnp
        import numpy as np
        N_NODES = 12500
        N_EDGES = 200000
        IN_FEATS = 256
        OUT_FEATS = 64
        NUM_HEADS = 4
        key = jax.random.key(seed)
        k_h, k_adj, k_dir, k_wf, k_wr, k_af = jax.random.split(key, 6)
        h = jax.random.normal(k_h, (N_NODES, IN_FEATS), dtype=jnp.float32)
        adj = jax.random.randint(k_adj, (2, N_EDGES), 0, N_NODES, dtype=jnp.int64)
        bit = jax.random.randint(k_dir, (N_EDGES,), 0, 2).astype(jnp.float32)
        direction = jnp.stack([bit, 1.0 - bit], axis=1)
        s_w = float(np.sqrt(6.0 / (IN_FEATS + OUT_FEATS)))
        s_a = float(np.sqrt(6.0 / (NUM_HEADS + OUT_FEATS)))
        W_forward = jax.random.uniform(k_wf, (OUT_FEATS, IN_FEATS), jnp.float32, -s_w, s_w)
        W_reverse = jax.random.uniform(k_wr, (OUT_FEATS, IN_FEATS), jnp.float32, -s_w, s_w)
        attn_forward = jax.random.uniform(k_af, (1, NUM_HEADS, OUT_FEATS), jnp.float32, -s_a, s_a)
        return {'h': h, 'adj': adj, 'direction': direction, 'W_forward': W_forward, 'W_reverse': W_reverse, 'attn_forward': attn_forward}
    _L0_gnn_all = _L0_gnn_setup()
    _L0_gnn_in = {k: v for k, v in _L0_gnn_all.items() if k in ('W_forward', 'W_reverse', 'attn_forward')}
    del _L0_gnn_all

    def _L0_mix_setup():
        import jax, jax.numpy as jnp
        import numpy as np
        NHEAD = 8
        ATT_EPS = 1e-06
        LN_EPS = 1e-05

        def _layernorm(x, g, b):
            mu = jnp.mean(x, axis=-1, keepdims=True)
            var = jnp.mean(jnp.square(x - mu), axis=-1, keepdims=True)
            return (x - mu) * jax.lax.rsqrt(var + LN_EPS) * g + b
        key = jax.random.key(seed)
        ks = jax.random.split(key, 7)
        N, L, C = (4, 2048, 256)
        s = 1.0 / np.sqrt(C)
        return {'x': jax.random.normal(ks[0], (N, L, C), jnp.float32), 'Wq': jax.random.normal(ks[1], (C, C), jnp.float32) * s, 'Wk': jax.random.normal(ks[2], (C, C), jnp.float32) * s, 'Wv': jax.random.normal(ks[3], (C, C), jnp.float32) * s, 'Wm': jax.random.normal(ks[4], (C, C), jnp.float32) * s, 'W1': jax.random.normal(ks[5], (2 * C, 2 * C), jnp.float32) * (1.0 / np.sqrt(2 * C)), 'W2': jax.random.normal(ks[6], (2 * C, C), jnp.float32) * (1.0 / np.sqrt(2 * C)), 'g1': jnp.ones((C,), jnp.float32), 'b1': jnp.zeros((C,), jnp.float32), 'g2': jnp.ones((C,), jnp.float32), 'b2': jnp.zeros((C,), jnp.float32)}
    _L0_mix_all = _L0_mix_setup()
    _L0_mix_in = {k: v for k, v in _L0_mix_all.items() if k in ('Wq', 'Wk', 'Wv', 'Wm', 'W1', 'W2', 'g1', 'b1', 'g2', 'b2')}
    del _L0_mix_all

    def _L0_ffn_setup():
        import jax, jax.numpy as jnp
        import numpy as np
        B, S, D = (8, 512, 256)
        H = 4 * D
        CAPACITY = 0.5
        key = jax.random.key(seed)
        ks = jax.random.split(key, 6)
        x = jax.random.normal(ks[0], (B, S, D), dtype=jnp.float32)
        attention_mask = jnp.zeros((B, 1, 1, S), dtype=jnp.float32)
        wr = jax.random.normal(ks[1], (D, 1), dtype=jnp.float32) * 0.02
        br = jnp.zeros((1,), dtype=jnp.float32)
        w1 = jax.random.normal(ks[2], (D, H), dtype=jnp.float32) * 0.02
        b1 = jnp.zeros((H,), dtype=jnp.float32)
        w2 = jax.random.normal(ks[3], (H, D), dtype=jnp.float32) * 0.02
        b2 = jnp.zeros((D,), dtype=jnp.float32)
        return {'x': x, 'attention_mask': attention_mask, 'wr': wr, 'br': br, 'w1': w1, 'b1': b1, 'w2': w2, 'b2': b2}
    _L0_ffn_all = _L0_ffn_setup()
    _L0_ffn_in = {k: v for k, v in _L0_ffn_all.items() if k in ('attention_mask', 'wr', 'br', 'w1', 'b1', 'w2', 'b2')}
    del _L0_ffn_all
    return {'x': x, 'src': src, 'dst': dst, 'edge_attr_2': edge_attr_2, 'L0_gnn_W_forward': _L0_gnn_in['W_forward'], 'L0_gnn_W_reverse': _L0_gnn_in['W_reverse'], 'L0_gnn_attn_forward': _L0_gnn_in['attn_forward'], 'L0_mix_Wq': _L0_mix_in['Wq'], 'L0_mix_Wk': _L0_mix_in['Wk'], 'L0_mix_Wv': _L0_mix_in['Wv'], 'L0_mix_Wm': _L0_mix_in['Wm'], 'L0_mix_W1': _L0_mix_in['W1'], 'L0_mix_W2': _L0_mix_in['W2'], 'L0_mix_g1': _L0_mix_in['g1'], 'L0_mix_b1': _L0_mix_in['b1'], 'L0_mix_g2': _L0_mix_in['g2'], 'L0_mix_b2': _L0_mix_in['b2'], 'L0_ffn_attention_mask': _L0_ffn_in['attention_mask'], 'L0_ffn_wr': _L0_ffn_in['wr'], 'L0_ffn_br': _L0_ffn_in['br'], 'L0_ffn_w1': _L0_ffn_in['w1'], 'L0_ffn_b1': _L0_ffn_in['b1'], 'L0_ffn_w2': _L0_ffn_in['w2'], 'L0_ffn_b2': _L0_ffn_in['b2']}

def reference(x, src, dst, edge_attr_2, L0_gnn_W_forward, L0_gnn_W_reverse, L0_gnn_attn_forward, L0_mix_Wq, L0_mix_Wk, L0_mix_Wv, L0_mix_Wm, L0_mix_W1, L0_mix_W2, L0_mix_g1, L0_mix_b1, L0_mix_g2, L0_mix_b2, L0_ffn_attention_mask, L0_ffn_wr, L0_ffn_br, L0_ffn_w1, L0_ffn_b1, L0_ffn_w2, L0_ffn_b2):
    import jax
    import jax.numpy as jnp

    def _L0_gnn_ref(h, adj, direction, W_forward, W_reverse, attn_forward):
        import jax, jax.numpy as jnp
        import numpy as np
        N_NODES = 12500
        N_EDGES = 200000
        IN_FEATS = 256
        OUT_FEATS = 64
        NUM_HEADS = 4
        N = h.shape[0]
        H = attn_forward.shape[1]
        h_fwd = h @ W_forward.T
        h_rev = h @ W_reverse.T
        src, dst = (adj[0], adj[1])
        messages = h_fwd[src] * direction[:, 0:1] + h_rev[src] * direction[:, 1:2]
        scores = jnp.einsum('ef,hf->eh', messages, attn_forward[0])
        scores = jax.nn.leaky_relu(scores, negative_slope=0.2)
        exp_scores = jnp.exp(scores - scores.max(axis=0, keepdims=True))
        sum_exp = jax.ops.segment_sum(exp_scores, dst, num_segments=N)
        norm = exp_scores / (sum_exp[dst] + 1e-10)
        outs = [jax.ops.segment_sum(messages * norm[:, hd:hd + 1], dst, num_segments=N) for hd in range(H)]
        out = jnp.stack(outs, axis=1)
        return out.reshape(N, -1)

    def _L0_mix_ref(x, Wq, Wk, Wv, Wm, W1, W2, g1, b1, g2, b2):
        import jax, jax.numpy as jnp
        import numpy as np
        NHEAD = 8
        ATT_EPS = 1e-06
        LN_EPS = 1e-05

        def _layernorm(x, g, b):
            mu = jnp.mean(x, axis=-1, keepdims=True)
            var = jnp.mean(jnp.square(x - mu), axis=-1, keepdims=True)
            return (x - mu) * jax.lax.rsqrt(var + LN_EPS) * g + b
        N, L, C = x.shape
        H = NHEAD
        D = C // H
        q = (x @ Wq).reshape(N, L, H, D)
        k = (x @ Wk).reshape(N, L, H, D)
        v = (x @ Wv).reshape(N, L, H, D)
        Q = jax.nn.elu(q) + 1.0
        K = jax.nn.elu(k) + 1.0
        v = v / L
        KV = jnp.einsum('nshd,nshv->nhdv', K, v)
        Z = 1.0 / (jnp.einsum('nlhd,nhd->nlh', Q, K.sum(axis=1)) + ATT_EPS)
        msg = jnp.einsum('nlhd,nhdv,nlh->nlhv', Q, KV, Z) * L
        msg = msg.reshape(N, L, C) @ Wm
        msg = _layernorm(msg, g1, b1)
        h = jnp.concatenate([x, msg], axis=-1) @ W1
        h = jax.nn.relu(h) @ W2
        msg = _layernorm(h, g2, b2)
        return x + msg

    def _L0_ffn_ref(x, attention_mask, wr, br, w1, b1, w2, b2):
        import jax, jax.numpy as jnp
        import numpy as np
        B, S, D = (8, 512, 256)
        H = 4 * D
        CAPACITY = 0.5
        b, s, d = x.shape
        weights = (jnp.einsum('bsd,do->bso', x, wr) + br)[..., 0]
        k = max(1, int(CAPACITY * s))
        kk = k - 1 if k > 1 else 1
        _, idx = jax.lax.top_k(weights, k)
        sel_idx = idx[:, :kk]
        sel = jnp.take_along_axis(x, sel_idx[:, :, None], axis=1)
        h = jax.nn.gelu(jnp.einsum('bkd,dh->bkh', sel, w1) + b1)
        y = jnp.einsum('bkh,hd->bkd', h, w2) + b2
        w_sel = jnp.take_along_axis(weights, sel_idx, axis=1)
        y = y * w_sel[..., None]
        batch_idx = jnp.arange(b)[:, None]
        processed = jnp.zeros_like(x).at[batch_idx, sel_idx].set(y)
        return processed + x
    edge_index = jnp.stack([src, dst])
    xn = _layernorm(x, axis=-1)
    x = x + _L0_gnn_ref(xn, edge_index, edge_attr_2, L0_gnn_W_forward, L0_gnn_W_reverse, L0_gnn_attn_forward) + _L0_mix_ref(xn[None], L0_mix_Wq, L0_mix_Wk, L0_mix_Wv, L0_mix_Wm, L0_mix_W1, L0_mix_W2, L0_mix_g1, L0_mix_b1, L0_mix_g2, L0_mix_b2)[0]
    x = x + _L0_ffn_ref(_layernorm(x, axis=-1)[None], L0_ffn_attention_mask, L0_ffn_wr, L0_ffn_br, L0_ffn_w1, L0_ffn_b1, L0_ffn_w2, L0_ffn_b2)[0]
    return x

_drawn_inputs = setup_inputs


def setup_inputs(seed=0):
    import zlib

    import numpy as np

    out = dict(_drawn_inputs(seed))
    spreads = {'L0_mix_g1': (1.0, 0.2),
     'L0_mix_b1': (0.0, 0.273),
     'L0_mix_g2': (1.0, 0.2),
     'L0_mix_b2': (0.0, 0.1),
     'L0_ffn_b1': (0.0, 0.8),
     'L0_ffn_b2': (0.0, 0.8)}
    factors = {'L0_ffn_wr': 7.14, 'L0_ffn_w1': 8.0, 'L0_ffn_w2': 7.846}
    for name, (base, spread) in spreads.items():
        noise = np.random.default_rng([zlib.crc32(name.encode()), seed]).standard_normal(out[name].shape)
        drawn = base * np.exp(spread * noise) if base else spread * noise
        out[name] = jnp.asarray(drawn.astype(out[name].dtype))
    for name, factor in factors.items():
        out[name] = (out[name] * factor).astype(out[name].dtype)
    return out
```

```python
from contextlib import ExitStack

import concourse.bass as bass
from concourse import mybir

F32 = mybir.dt.float32
I32 = mybir.dt.int32
ALU = mybir.AluOpType
ACT = mybir.ActivationFunctionType
AX = mybir.AxisListType.X

P = 128
N = 6250
E = 206250
TOP = 3124
C = 256
KC = C // P
F = 64
H = 4
ROW = F + H
UT = 2
UN = UT * P
UNITS = -(-N // UN)
NP = UNITS * UN
NT = NP // P
LAST = N - (NP - UN)
ET = -(-E // P)
BT = 13
BLOCKS = ET // BT
GROUPS = [(0, 4), (4, 8), (8, 13)]
NG = len(GROUPS)
WIN = 32
WINS = NP // WIN
GR = BLOCKS * NG
GC = -(-GR // P)
PAD_NODE = 1.0e6
LN_EPS = 1e-5
SUM_EPS = 1e-10
ATT_EPS = 1e-6
SLOPE = 0.2
GAP_MAX = 30.0
SUM_TOL = 2.0 ** -23
LOW = -3.0e38
HD = 32
HID = 2 * C
FF = 4 * C
PRE = 5
SLOTS = 5
BODIES = BLOCKS // SLOTS
MIX_BODIES = 5
MIX_EACH = UNITS // MIX_BODIES
PAIR_BODIES = 3
STEPS = 12
OUT_CHUNKS = 5
DONE = 2 * PAIR_BODIES + (BODIES - MIX_BODIES - PAIR_BODIES) + 1
assert BLOCKS * BT == ET and BLOCKS % SLOTS and UNITS % PRE == 0 and UNITS % MIX_BODIES == 0
assert E % P and LAST <= P and 0 < UNITS - DONE and KC == 2 and UT == 2 and MIX_EACH <= SLOTS
assert UNITS % OUT_CHUNKS == 0
assert all(2 * j + 2 <= MIX_BODIES + j - 1 for j in range(PAIR_BODIES)) and DONE <= BODIES - 1


class Count:

    def __init__(self, sem, credit=0):
        self.sem, self.credit = sem, credit

    def wait(self, eng, count):
        eng.wait_ge(self.sem, count + self.credit)


class Stages:

    def __init__(self, sem, names):
        self.sem, self.names = sem, names.split()

    def open(self, eng):
        eng.sem_inc(self.sem, len(self.names))

    def wait(self, eng, name, units):
        eng.wait_ge(self.sem, units * len(self.names) + (self.names.index(name) + 1))


V_STAGES = ("m1 qmin mtop diag qt own lead gap guard zr0 zr mt stat1 mv1 rstd1 z stat2 mv2 rstd2 z2 y2 y3 ra "
            "den tol rden low gn x1 stat3 mv3 rstd3 xf dot base wcol yb yw")
A_STAGES = "qexp gexp sd1 m2t relu sd2 part sd3 xft gelu0 gelu1 gelu2 gelu3"
P_STAGES = "q m1t mall attn proj ztr hid y ptr xtr ff0 ff1 ff2 ff3 out"


def chain_counts(sem, tag):
    c = {"V": Stages(sem(f"{tag}_vector_stages"), V_STAGES), "A": Stages(sem(f"{tag}_scalar_stages"), A_STAGES),
         "P": Stages(sem(f"{tag}_tensor_stages"), P_STAGES), "before": 0}
    for name in ("x_in", "r_in", "base_out"):
        c[name] = sem(f"{tag}_{name}")
    return c


def vector_chain(dve, s, c, step, u, seen, track):
    bank = s["bank"]
    r = u + 1 + c["before"]
    if step == 0:
        s["max_seen"](dve, seen)
        dve.tensor_reduce(s["m1"], s["smax"].rearrange("p t h -> p h t"), AX, ALU.max).then_inc(c["V"].sem, 1)
    if step == 1:
        c["P"].wait(dve, "q", r)
        dve.tensor_scalar(s["T0"], bank[2][:, :], 0.0, None, ALU.min).then_inc(c["V"].sem, 1)
        c["P"].wait(dve, "m1t", r)
        dve.tensor_reduce(s["mtop"], bank[6][0:H, 0:P], AX, ALU.max).then_inc(c["V"].sem, 1)
        c["V"].wait(dve, "mtop", r)
        dve.tensor_scalar(s["diag"], s["ident"][0:H, 0:H], s["mtop"], None, ALU.mult).then_inc(c["V"].sem, 1)
    if step == 2:
        c["A"].wait(dve, "qexp", r)
        dve.scalar_tensor_tensor(out=s["T2"], in0=bank[2][:, :], scalar=0.0, in1=s["T1"], op0=ALU.max, op1=ALU.add)\
            .then_inc(c["V"].sem, 1)
        c["P"].wait(dve, "mall", r)
        dve.tensor_copy(s["mall"], bank[6][:, UN:UN + H]).then_inc(c["V"].sem, 1)
        c["V"].wait(dve, "own", r)
        dve.scalar_tensor_tensor(out=s["lead"], in0=s["mall"], scalar=SLOPE, in1=s["mall"], op0=ALU.mult, op1=ALU.max)\
            .then_inc(c["V"].sem, 1)
        c["V"].wait(dve, "lead", r)
        dve.tensor_tensor(s["gap"], s["lead"], s["bound"], ALU.subtract).then_inc(c["V"].sem, 1)
    if step == 3:
        c["A"].wait(dve, "gexp", r)
        dve.tensor_scalar(s["guard"], s["gexp"], SUM_EPS, None, ALU.mult).then_inc(c["V"].sem, 1)
        c["P"].wait(dve, "attn", r)
        dve.tensor_scalar(s["T0"], bank[3][:, :], ATT_EPS, None, ALU.add).then_inc(c["V"].sem, 1)
        c["V"].wait(dve, "zr0", r)
        dve.reciprocal(s["T0"], s["T0"]).then_inc(c["V"].sem, 1)
        c["V"].wait(dve, "zr", r)
        dve.wait_ge(c["base_out"], r * 16)
        dve.scalar_tensor_tensor(out=s["T3"], in0=bank[4][:, :], scalar=float(N), in1=s["T0"], op0=ALU.mult, op1=ALU.mult)\
            .then_inc(c["V"].sem, 1)

    def moments(n, source):
        for t in range(UT):
            ins = dve.bn_stats(s["stats"][:, t, :], source(t))
        ins.then_inc(c["V"].sem, 1)
        c["V"].wait(dve, f"stat{n}", r)
        dve.sem_inc(s["hold_v"], 1)
        for t in range(UT):
            ins = dve.bn_aggr(s["mv"][:, t, :], s["stats"][:, t, :])
        ins.then_inc(c["V"].sem, 1)

    def normal(n, dst, source):
        c["A"].wait(dve, f"sd{n}", r)
        dve.reciprocal(s["rstd"], s["sd"]).then_inc(c["V"].sem, 1)
        c["V"].wait(dve, f"rstd{n}", r)
        for t in range(UT):
            ins = dve.tensor_scalar(dst[:, t * C:(t + 1) * C], source(t), s["mv"][:, t, 0:1], s["rstd"][:, t:t + 1],
                                    ALU.subtract, ALU.mult)
        ins.then_inc(c["V"].sem, 1)

    def rows_of(tile):
        return lambda t: tile[:, t * C:(t + 1) * C]

    if step == 4:
        c["P"].wait(dve, "proj", r)
        moments(1, rows_of(bank[5]))
    if step == 5:
        normal(1, s["T0"], rows_of(bank[5]))
    if step == 6:
        c["P"].wait(dve, "y", r)
        moments(2, rows_of(bank[3]))
    if step == 7:
        normal(2, s["T2"], rows_of(bank[3]))
        t2 = s["T2"].rearrange("p (t c) -> p t c", t=UT)
        c["V"].wait(dve, "z2", r)
        dve.tensor_tensor(t2, t2, s["g2"].rearrange("p (o c) -> p o c", o=1).to_broadcast([P, UT, C]), ALU.mult)\
            .then_inc(c["V"].sem, 1)
        c["V"].wait(dve, "y2", r)
        dve.tensor_tensor(t2, t2, s["b2"].rearrange("p (o c) -> p o c", o=1).to_broadcast([P, UT, C]), ALU.add)\
            .then_inc(c["V"].sem, 1)
        c["V"].wait(dve, "y3", r)
        dve.wait_ge(c["r_in"], r * 16)
        dve.tensor_tensor(s["T5"], s["T5"], s["T2"], ALU.add).then_inc(c["V"].sem, 1)
    if step == 8:
        c["P"].wait(dve, "ptr", r)
        for t in range(UT):
            ins = dve.tensor_tensor(s["den"][:, t, :], bank[4 + t][:, 2 * P:2 * P + H], s["guard"], ALU.add)
        ins.then_inc(c["V"].sem, 1)
        for t, n in enumerate(track):
            if n:
                ins = dve.scalar_tensor_tensor(out=s["tol"][0:n, t, :], in0=bank[4 + t][0:n, 2 * P:2 * P + H], scalar=SUM_TOL,
                                               in1=s["guard"][0:n, :], op0=ALU.mult, op1=ALU.add)
        ins.then_inc(c["V"].sem, 1)
        c["V"].wait(dve, "den", r)
        dve.reciprocal(s["rden"], s["den"]).then_inc(c["V"].sem, 1)
        c["V"].wait(dve, "rden", r)
        c["V"].wait(dve, "tol", r)
        for t, n in enumerate(track):
            if n:
                low = s["low"][0:n, t, :]
                ins = dve.tensor_tensor(low, low, s["tol"][0:n, t, :], ALU.min)
        ins.then_inc(c["V"].sem, 1)
        for t in range(UT):
            ins = dve.tensor_tensor(s["T1"][:, t * C:(t + 1) * C].rearrange("p (b a f) -> p b a f", b=2, a=2),
                                    bank[4 + t][:, 0:2 * P].rearrange("p (a b f) -> p b a f", a=2, b=2),
                                    s["rden"][:, t, :].rearrange("p (b a o) -> p b a o", b=2, o=1).to_broadcast([P, 2, 2, F]),
                                    ALU.mult)
        ins.then_inc(c["V"].sem, 1)
        c["V"].wait(dve, "gn", r)
        c["V"].wait(dve, "ra", r)
        dve.tensor_tensor(s["T5"], s["T5"], s["T1"], ALU.add).then_inc(c["V"].sem, 1)
        c["V"].wait(dve, "x1", r)
        moments(3, rows_of(s["T5"]))
    if step == 9:
        normal(3, s["T2"], rows_of(s["T5"]))
        c["V"].wait(dve, "xf", r)
        for t in range(UT):
            rows = slice(t * C, (t + 1) * C)
            ins = dve.tensor_tensor_reduce(s["T1"][:, rows], s["T2"][:, rows], s["wr"], 1.0, 0.0, ALU.mult, ALU.add,
                                           s["dot"][:, t:t + 1])
        ins.then_inc(c["V"].sem, 1)
        dve.tensor_tensor(s["T3"], s["T5"], s["T2"], ALU.add).then_inc(c["V"].sem, 1)
        c["V"].wait(dve, "dot", r)
        dve.tensor_scalar(s["wcol"], s["dot"], s["br"], None, ALU.add).then_inc(c["V"].sem, 1)
    if step == 11:
        c["V"].wait(dve, "wcol", r)
        dve.tensor_copy(s["w_all"][:, bass.ds(u * UT, UT)], s["wcol"])
        c["P"].wait(dve, "out", r)
        t1 = s["T1"].rearrange("p (t c) -> p t c", t=UT)
        dve.tensor_tensor(t1, bank[3][:, :].rearrange("p (t c) -> p t c", t=UT),
                          s["fb2"].rearrange("p (o c) -> p o c", o=1).to_broadcast([P, UT, C]), ALU.add).then_inc(c["V"].sem, 1)
        c["V"].wait(dve, "yb", r)
        for t in range(UT):
            ins = dve.tensor_scalar(s["acc"][:, t, bass.ds(u * UN, C)], s["T1"][:, t * C:(t + 1) * C], s["wcol"][:, t:t + 1],
                                    None, ALU.mult)
        ins.then_inc(c["V"].sem, 1)


def scalar_chain(act, s, c, step, u, merges):
    bank = s["bank"]
    r = u + 1 + c["before"]
    if step == 0:
        act.dma_start(s["T4"], s["xnt_d"][:, :, bass.ds(u * UN, UN)]).then_inc(c["x_in"], 16)
        c["V"].wait(act, "base", r - 1)
        act.dma_start(s["T5"].rearrange("p (t c) -> p t c", t=UT),
                      s["resid_d"][bass.ds(u * UN, UN), :].rearrange("(t p) c -> p t c", p=P)).then_inc(c["r_in"], 16)
    if step == 1:
        c["V"].wait(act, "qmin", r)
        act.activation(s["T1"], s["T0"], ACT.Exp).then_inc(c["A"].sem, 1)
    if step == 2:
        c["V"].wait(act, "gap", r)
        act.activation(s["gexp"], s["gap"], ACT.Exp).then_inc(c["A"].sem, 1)

    def deviation(n):
        c["V"].wait(act, f"mv{n}", r)
        act.activation(s["sd"], s["mv"][:, :, 1], ACT.Sqrt, bias=s["eps"]).then_inc(c["A"].sem, 1)

    if step == 4:
        deviation(1)
    if step == 5:
        c["P"].wait(act, "ztr", r)
        for k in range(KC):
            ins = act.activation(s["T1"][:, k * UN:(k + 1) * UN], bank[6][:, k * UN:(k + 1) * UN], ACT.Identity,
                                 bias=s["b1"][:, k:k + 1], scale=s["g1"][:, k:k + 1])
        ins.then_inc(c["A"].sem, 1)
        c["P"].wait(act, "hid", r)
        for f, b in enumerate((7, 2)):
            ins = act.activation(s["hidden"][:, 2 * f * UN:(2 * f + 2) * UN], bank[b][:, :], ACT.Relu)
        ins.then_inc(c["A"].sem, 1)
    if step == 6:
        deviation(2)
    if step == 8:
        merges(act)
        act.activation(s["T3"].rearrange("p (a n) -> p a n", a=2), s["acc"][:, :, bass.ds(u * UN, UN)], ACT.Copy)
        act.activation(s["part_w"], s["acc_w"][:, bass.ds(u * UN, UN)], ACT.Copy).then_inc(c["A"].sem, 1)
        deviation(3)
    if step == 9:
        c["V"].wait(act, "base", r)
        act.dma_start(s["base_d"][bass.ds(u * UN, UN), :].rearrange("(t p) c -> p t c", p=P),
                      s["T3"].rearrange("p (t c) -> p t c", t=UT)).then_inc(c["base_out"], 16)
        c["P"].wait(act, "xtr", r)
        act.activation(s["T0"], bank[6][:, :], ACT.Copy).then_inc(c["A"].sem, 1)
    if step == 10:
        for f in range(4):
            c["P"].wait(act, f"ff{f}", r)
            for m in range(2):
                j = 2 * f + m
                ins = act.activation(s["hidden"][:, j * UN:(j + 1) * UN], bank[(7, 2)[f % 2]][:, m * UN:(m + 1) * UN],
                                     ACT.Gelu_apprx_tanh, bias=s["fb1"][:, j:j + 1])
            ins.then_inc(c["A"].sem, 1)


def tensor_chain(pe, s, c, step, u):
    bank, ident = s["bank"], s["ident"]
    r = u + 1 + c["before"]

    def turned(dst, tile):
        for t in range(UT):
            for k in range(KC):
                ins = pe.transpose(dst[:, k * UN + t * P:k * UN + (t + 1) * P], tile[:, t * C + k * P:t * C + (k + 1) * P], ident)
        return ins

    def by_row(dst, halves, weights, n):
        for t in range(UT):
            for k in range(n):
                ins = pe.matmul(dst[:, t * C:(t + 1) * C], halves[:, k * UN + t * P:k * UN + (t + 1) * P], weights[:, k, :],
                                start=(k == 0), stop=(k == n - 1))
        return ins

    if step == 1:
        pe.wait_ge(c["x_in"], r * 16)
        for j in range(KC):
            for k in range(KC):
                ins = pe.matmul(bank[2][:, j * UN:(j + 1) * UN], s["wq"][:, k, j * P:(j + 1) * P], s["T4"][:, k, :],
                                start=(k == 0), stop=(k == KC - 1))
        ins.then_inc(c["P"].sem, 1)
        c["V"].wait(pe, "m1", r)
        pe.transpose(bank[6][0:H, 0:P], s["m1"], ident).then_inc(c["P"].sem, 1)
    if step == 2:
        c["V"].wait(pe, "diag", r)
        pe.matmul(bank[6][:, UN:UN + H], s["ones"][0:H, :], s["diag"], start=True, stop=True).then_inc(c["P"].sem, 1)
        c["V"].wait(pe, "qt", r)
        for b, w in ((3, s["ksum"]), (4, s["kv"])):
            for j in range(KC):
                ins = pe.matmul(bank[b][:, j * UN:(j + 1) * UN], w[:, j, :], s["T2"][:, j * UN:(j + 1) * UN], start=True, stop=True)
        ins.then_inc(c["P"].sem, 1)
    if step == 3:
        c["V"].wait(pe, "mt", r)
        by_row(bank[5], s["T3"], s["wm"], KC).then_inc(c["P"].sem, 1)
    if step == 5:
        c["V"].wait(pe, "z", r)
        turned(bank[6], s["T0"]).then_inc(c["P"].sem, 1)
        c["A"].wait(pe, "m2t", r)
        for m in range(HID // P):
            dst = bank[(7, 2)[m // 2]][:, (m % 2) * UN:(m % 2 + 1) * UN]
            for k in range(2 * KC):
                rhs = s["T4"][:, k, :] if k < KC else s["T1"][:, (k - KC) * UN:(k - KC + 1) * UN]
                ins = pe.matmul(dst, s["w1"][:, k, m * P:(m + 1) * P], rhs, start=(k == 0), stop=(k == 2 * KC - 1))
        ins.then_inc(c["P"].sem, 1)
    if step == 6:
        c["A"].wait(pe, "relu", r)
        by_row(bank[3], s["hidden"], s["w2"], HID // P).then_inc(c["P"].sem, 1)
    if step == 8:
        c["A"].wait(pe, "part", r)
        for t in range(UT):
            for a in range(2):
                pe.transpose(bank[4 + t][:, a * P:(a + 1) * P], s["T3"][:, a * UN + t * P:a * UN + (t + 1) * P], ident)
            ins = pe.transpose(bank[4 + t][:, 2 * P:2 * P + H], s["part_w"][:, t * P:(t + 1) * P], ident[0:H, 0:H])
        ins.then_inc(c["P"].sem, 1)
    if step == 9:
        c["V"].wait(pe, "xf", r)
        turned(bank[6], s["T2"]).then_inc(c["P"].sem, 1)
    if step == 10:
        c["A"].wait(pe, "xft", r)
        for f in range(4):
            if f >= 2:
                c["A"].wait(pe, f"gelu{f - 2}", r)
            for m in range(2):
                j = 2 * f + m
                for k in range(KC):
                    ins = pe.matmul(bank[(7, 2)[f % 2]][:, m * UN:(m + 1) * UN], s["f1"][:, k, j * P:(j + 1) * P],
                                    s["T0"][:, k * UN:(k + 1) * UN], start=(k == 0), stop=(k == KC - 1))
            ins.then_inc(c["P"].sem, 1)
        c["A"].wait(pe, "gelu3", r)
        by_row(bank[3], s["hidden"], s["f2"], FF // P).then_inc(c["P"].sem, 1)


def body_slots(blocks, steps):
    n = 3 * blocks
    return [range(q * steps // n, (q + 1) * steps // n) for q in range(n)]


def build_program(nc, x, src_t, dst_t, attr_t, wg, wsum, attn_t, wkv_d, wq_d, wm_d, w1_d, w2_d, g1_d, b1_d, g2_d, b2_d,
                  f1_d, f2_d, fb1_d, fb2_d, wr_d, br_d, out):
    with ExitStack() as ctx:
        def sb(name, shape, dt=F32, where=ctx):
            return where.enter_context(nc.sbuf_tensor(name, shape, dt))

        def sem(name):
            return ctx.enter_context(nc.semaphore(name))

        def count(name, credit=0):
            return Count(sem(name), credit)

        table_d = nc.dram_tensor("table_d", (NP, 2 * ROW), F32, kind="Internal").ap()
        xnt_d = nc.dram_tensor("xnt_d", (P, KC, NP), F32, kind="Internal").ap()
        resid_d = nc.dram_tensor("resid_d", (NP, C), F32, kind="Internal").ap()
        base_d = nc.dram_tensor("base_d", (NP, C), F32, kind="Internal").ap()
        first_d = nc.dram_tensor("first_d", (GC * P,), F32, kind="Internal").ap()

        bank = [ctx.enter_context(nc.psum_tensor(f"bank{i}", [P, 512], F32)) for i in range(8)]

        ident = sb("ident", [P, P])
        ones = sb("ones", [P, P])
        before = sb("before", [P, P])
        heads = sb("heads", [P, P])
        iota_i = sb("iota_i", [P, WIN], I32)
        iota = sb("iota", [P, WIN])
        limit_i = sb("limit_i", [P, BODIES + 1, SLOTS * NG], I32)
        eps_col = sb("eps_col", [P, 1])
        valid = sb("valid", [P, NT])

        wq = sb("wq", [P, KC, C])
        wm = sb("wm", [P, KC, C])
        w1 = sb("w1", [P, 2 * KC, HID])
        w2 = sb("w2", [P, HID // P, C])
        f1 = sb("f1", [P, KC, FF])
        wkv = f1[:, :, 0:2 * C]
        f2 = sb("f2", [P, FF // P, C])
        g1 = sb("g1", [P, KC])
        b1 = sb("b1", [P, KC])
        fb1 = sb("fb1", [P, FF // P])
        g2 = sb("g2", [P, C])
        b2 = sb("b2", [P, C])
        fb2 = sb("fb2", [P, C])
        wr = sb("wr", [P, C])
        br = sb("br", [P, 1])

        dst_rel = sb("dst_rel", [P, ET])
        first_i = sb("first_i", [1, GC * P], I32)
        bound = sb("bound", [P, H])
        smax = sb("smax", [P, BT, H])
        acc = sb("acc", [P, 2, NP])
        acc_w = sb("acc_w", [H, NP])
        w_all = sb("w_all", [P, NT])
        low = sb("low", [P, UT, H])
        kv_sum = sb("kv_sum", [P, KC, P + 1])
        kv = sb("kv", [P, KC, P])
        ksum = sb("ksum", [P, KC, P])
        verdict = sb("verdict", [P, 4])
        flag_i = sb("flag_i", [P, 1], I32)
        v4 = sb("v4", [4, 1])
        vd = sb("vd", [4, 4])
        vb = sb("vb", [P, 4])
        v_one = sb("v_one", [P, 1])
        small = {n: sb(n, [P, H]) for n in ("m1", "mall", "lead", "gap", "gexp", "guard")}
        mtop = sb("mtop", [H, 1])
        diag = sb("diag", [H, H])
        stats_u = sb("stats_u", [P, UT, 6])
        mv_u = sb("mv_u", [P, UT, 2])
        sd_u = sb("sd_u", [P, UT])
        rstd_u = sb("rstd_u", [P, UT])
        den = sb("den", [P, UT, H])
        rden = sb("rden", [P, UT, H])
        tol = sb("tol", [P, UT, H])
        dot = sb("dot", [P, UT])
        wcol = sb("wcol", [P, UT])

        s_const = sem("s_const")
        s_zero = sem("s_zero")
        s_dv = sem("s_dv")
        s_ask = sem("s_ask")
        s_given = sem("s_given")
        hold_v = sem("hold_v"); hold_p = sem("hold_p"); hold_s = sem("hold_s"); hold_a = sem("hold_a"); hold_t = sem("hold_t")
        s_w = {k: sem(f"s_w_{k}") for k in ("wg", "wsum", "attn", "dst", "attr", "mix", "chain", "ff")}
        dve_links = [0]

        def linker(dve):
            def link(ins):
                dve_links[0] += 1
                ins.then_inc(s_dv, 1)
                dve.wait_ge(s_dv, dve_links[0])
            return link

        asked = [0]

        edge = ExitStack()
        idx = [sb(f"idx{k}", [P, BT], I32, edge) for k in range(SLOTS)]
        att = [sb(f"att{k}", [P, BT, 2], F32, edge) for k in range(SLOTS)]
        got = [sb(f"got{k}", [P, BT, 2, ROW], F32, edge) for k in range(SLOTS)]
        T4 = sb("T4", [P, KC, UN], F32, edge)
        T5 = sb("T5", [P, UT * C], F32, edge)
        lrelu = sb("lrelu", [P, BT, H], F32, edge)
        score = sb("score", [P, 2, BT, H], F32, edge)
        wgt = sb("wgt", [P, 2, BT, H], F32, edge)

        pre = ExitStack()
        x_u = sb("x_u", [P, PRE, UT, C], F32, pre)
        xn = sb("xn", [P, PRE, UT, C], F32, pre)
        xnt = sb("xnt", [P, PRE, KC, UN], F32, pre)
        rows = sb("rows", [P, PRE, UT, 2, ROW], F32, pre)
        stats = sb("stats", [P, PRE, UT, 6], F32, pre)
        mv = sb("mv", [P, PRE, UT, 2], F32, pre)
        sd = sb("sd", [P, PRE, UT], F32, pre)
        rstd = sb("rstd", [P, PRE, UT], F32, pre)
        pre.close()
        work = ExitStack()
        msg = sb("msg", [P, 2, BT, ROW], F32, work)
        onehot = sb("onehot", [P, 2, BT, WIN], F32, work)
        woh = sb("woh", [P, 2, BT, H, WIN], F32, work)
        T0 = sb("T0", [P, UT * C], F32, work)
        T1 = sb("T1", [P, UT * C], F32, work)
        T2 = sb("T2", [P, UT * C], F32, work)
        T3 = sb("T3", [P, UT * C], F32, work)
        hidden = sb("hidden", [P, FF // P * UN], F32, work)
        after = ExitStack()

        flat = acc[:, :, :].rearrange("p a n -> p (a n)")
        at = [0]

        def piece(n):
            at[0] += n
            return flat[:, at[0] - n:at[0]]

        dst_i = piece(ET).bitcast(I32)
        dst_f = piece(ET)
        attr = piece(2 * ET).rearrange("p (t d) -> p t d", d=2)
        first_bc = piece(GC * P)
        gmin = piece(GC * P)
        gmax = piece(GC * P)
        wg_s = piece(KC * 2 * ROW).rearrange("p (k d r) -> p k d r", k=KC, d=2)
        wsum_s = piece(2 * C).rearrange("p (d c) -> p d c", d=2)[0:F]
        attn_s = piece(H)[0:F]
        p_all = piece(NT * 2 * H).rearrange("p (t d h) -> p t d h", d=2, h=H)
        p_lo = piece(NT * 2 * H).rearrange("p (t d h) -> p t d h", d=2, h=H)
        ext = piece(4)
        ext_bc = piece(4)
        bcol = piece(GC)
        mcol = piece(GC)
        limit = piece((BODIES + 1) * SLOTS * NG)
        assert at[0] <= 2 * NP

        c_stats = count("c_stats"); c_mv = count("c_mv"); c_sd = count("c_sd"); c_rstd = count("c_rstd")
        c_xn = count("c_xn"); c_res = count("c_res")
        c_tr = count("c_tr"); c_xnt = count("c_xnt"); c_tab = count("c_tab"); c_rows = count("c_rows")
        c_rows_p = count("c_rows_p")
        s_x = [sem(f"s_x{j}") for j in range(PRE)]
        s_rows_out = [sem(f"s_rows_out{j}") for j in range(PRE)]
        s_xnt_out = [sem(f"s_xnt_out{j}") for j in range(PRE)]
        s_res_out = [sem(f"s_res_out{j}") for j in range(PRE)]
        s_score_w = sem("s_score_w"); s_score_c = sem("s_score_c")
        s_first_out = sem("s_first_out"); s_first_in = sem("s_first_in")
        s_first = sem("s_first")
        s_kv = sem("s_kv")
        s_begin = sem("s_begin")

        s_idx = [sem(f"s_idx{k}") for k in range(SLOTS)]
        s_att = [sem(f"s_att{k}") for k in range(SLOTS)]
        s_got = [sem(f"s_got{k}") for k in range(SLOTS)]
        e_prod = count("e_prod"); e_msg = count("e_msg", SLOTS)
        e_lrelu = count("e_lrelu"); e_score = count("e_score"); e_max = count("e_max")
        e_wgt = count("e_wgt", 1); e_onehot = count("e_onehot"); e_woh = count("e_woh")
        e_scat = count("e_scat", 1)
        e_grp = count("e_grp"); e_merge = count("e_merge", 2); e_acc = count("e_acc")
        m_x = sem("m_x")
        m_proj = count("m_proj"); m_min = count("m_min"); m_exp = count("m_exp"); m_v = count("m_v")
        m_k = count("m_k"); m_kv = count("m_kv"); m_sum = count("m_sum", 1)
        c = chain_counts(sem, "c")

        def max_seen(dve, seen):
            e_max.wait(dve, seen)

        s = dict(bank=bank, ident=ident[:, :], ones=ones[:, :], smax=smax[:, :, :], acc=acc, acc_w=acc_w, w_all=w_all,
                 T0=T0[:, :], T1=T1[:, :], T2=T2[:, :], T3=T3[:, :], T4=T4[:, :, :], T5=T5[:, :], hidden=hidden[:, :],
                 part_w=T0[0:H, 0:UN], mtop=mtop[:, :], diag=diag[:, :], bound=bound[:, :], stats=stats_u, mv=mv_u,
                 sd=sd_u[:, :], rstd=rstd_u[:, :], den=den[:, :, :], rden=rden[:, :, :], tol=tol, low=low, dot=dot[:, :],
                 wcol=wcol[:, :], g1=g1, b1=b1, g2=g2[:, :], b2=b2[:, :], fb1=fb1, fb2=fb2[:, :], wr=wr[:, :], br=br[:, 0:1],
                 eps=eps_col[:, 0:1], wq=wq, wm=wm, w1=w1, w2=w2, f1=f1, f2=f2, kv=kv, ksum=ksum, xnt_d=xnt_d,
                 resid_d=resid_d, base_d=base_d, hold_v=hold_v, max_seen=max_seen,
                 **{n: t[:, :] for n, t in small.items()})
        s_full = (P, P)
        s_last = (LAST, 0)

        def edge_bodies(eng, block_part, mix_part, chain_part):
            def body(i, blocks, kind, units):
                steps = {"mix": 3 * MIX_EACH, "chain": STEPS * len(units)}[kind]
                for q, todo in enumerate(body_slots(blocks, steps)):
                    k = q // 3
                    block_part(eng, q % 3, i, k)
                    for step in todo:
                        if kind == "mix":
                            mix_part(eng, step % 3, i * MIX_EACH + step // 3)
                        else:
                            chain_part(eng, step % STEPS, units[step // STEPS], i * SLOTS + k + 1, i * SLOTS * NG)

            with eng.Fori(0, MIX_BODIES) as i:
                body(i, SLOTS, "mix", ())
            mix_part(eng, 3, None)
            with eng.Fori(0, PAIR_BODIES) as j:
                body(j + MIX_BODIES, SLOTS, "chain", (j * 2, j * 2 + 1))
            with eng.Fori(MIX_BODIES + PAIR_BODIES, BODIES) as i:
                body(i, SLOTS, "chain", (i - (BODIES + 1 - DONE),))
            body(BODIES, BLOCKS - BODIES * SLOTS, "chain", (DONE - 1,))

        def nothing(eng, *rest):
            pass

        with nc.Block() as block:
            @block.sync
            def _(sp):
                for j in range(PRE):
                    for q in (s_xnt_out[j], s_res_out[j], s_rows_out[j]):
                        sp.sem_inc(q, 16)
                sp.sem_inc(c["base_out"], 16)

                def load_x(u, j):
                    sp.dma_start(x_u[:, j, :, :], x[bass.ds(u * UN, UN), :].rearrange("(t p) c -> p t c", p=P)).then_inc(s_x[j], 16)

                sp.dma_start(wsum_s, wsum.rearrange("d f c -> f d c")).then_inc(s_w["wsum"], 16)
                sp.dma_start(attn_s, attn_t).then_inc(s_w["attn"], 16)
                for d in range(2):
                    sp.dma_start(wg_s[:, :, d, 0:F], wg[:, d * F:(d + 1) * F].rearrange("(k p) f -> p k f", p=P)).then_inc(s_w["wg"], 16)
                for j in range(PRE):
                    load_x(j, j)

                def keep(i, j):
                    u = i * PRE + j
                    c_rows.wait(sp, u + 1)
                    sp.sem_inc(hold_s, 1)
                    sp.dma_start(table_d[bass.ds(u * UN, UN), :].rearrange("(t p) r -> p t r", p=P),
                                 rows[:, j, :, :, :].rearrange("p t d r -> p t (d r)")).then_inc(s_rows_out[j], 16)
                    c_xnt.wait(sp, u + 1)
                    sp.sem_inc(hold_s, 1)
                    sp.dma_start(xnt_d[:, :, bass.ds(u * UN, UN)], xnt[:, j, :, :]).then_inc(s_xnt_out[j], 16)
                    c_res.wait(sp, u + 1)
                    sp.sem_inc(hold_s, 1)
                    sp.dma_start(resid_d[bass.ds(u * UN, UN), :].rearrange("(t p) c -> p t c", p=P), x_u[:, j, :, :])\
                        .then_inc(s_res_out[j], 16)

                with sp.Fori(0, UNITS // PRE - 1) as i:
                    for j in range(PRE + 2):
                        if j < PRE:
                            keep(i, j)
                        if j >= 2:
                            sp.wait_ge(s_res_out[j - 2], (i + 2) * 16)
                            sp.sem_inc(hold_s, 1)
                            load_x((i + 1) * PRE + j - 2, j - 2)
                for j in range(PRE):
                    keep(UNITS // PRE - 1, j)
                for dst, src, q in ((wkv, wkv_d, "mix"), (wq, wq_d, "mix"), (wm, wm_d, "chain"), (w1, w1_d, "chain"),
                                    (w2, w2_d, "chain"), (f2, f2_d, "ff")):
                    sp.dma_start(dst if dst is wkv else dst[:, :, :], src.rearrange("(k p) c -> p k c", p=P)).then_inc(s_w[q], 16)
                for dst, src in ((g1, g1_d), (b1, b1_d), (fb1, fb1_d)):
                    sp.dma_start(dst[:, :], src).then_inc(s_w["chain"], 16)
                for dst, src in ((g2, g2_d), (b2, b2_d), (fb2, fb2_d), (wr, wr_d), (br, br_d)):
                    sp.dma_start(dst[:, :], src.rearrange("(a n) -> a n", a=1).to_broadcast([P, src.shape[0]])).then_inc(s_w["chain"], 16)

                def part(eng, third, i, k):
                    if third == 0:
                        b = i * SLOTS + k
                        e_msg.wait(sp, b - SLOTS + 1)
                        sp.sem_inc(hold_s, 1)
                        sp.dma_start(idx[k][:, :], src_t[:, bass.ds(b * BT, BT)]).then_inc(s_idx[k], 16)
                        sp.dma_start(att[k][:, :, :], attr_t[:, bass.ds(b * BT, BT), :]).then_inc(s_att[k], 16)

                edge_bodies(sp, part, nothing, nothing)
                sp.wait_ge(c["base_out"], 16 * (UNITS + 1))
                for q, n in (("mix", 2), ("chain", 11), ("ff", 2)):
                    sp.wait_ge(s_w[q], 16 * n)

            @block.gpsimd
            def _(pool):
                pool.dma_start(dst_i, dst_t).then_inc(s_w["dst"], 16)
                pool.dma_start(attr, attr_t).then_inc(s_w["attr"], 16)
                pool.memset(ident[:, :], 0.0).then_inc(s_const, 1)
                pool.memset(ones[:, :], 1.0).then_inc(s_const, 1)
                pool.memset(eps_col[:, :], LN_EPS).then_inc(s_const, 1)
                pool.iota(iota_i[:, :], pattern=[[1, WIN]], base=0, channel_multiplier=0).then_inc(s_const, 1)
                pool.memset(before[:, :], 1.0).then_inc(s_const, 1)
                pool.memset(valid[:, :], 1.0).then_inc(s_const, 1)
                pool.memset(heads[:, :], 0.0).then_inc(s_const, 1)
                pool.iota(limit_i[:, :, :], pattern=[[UN, BODIES + 1], [0, SLOTS * NG]], base=-UN, channel_multiplier=0).then_inc(s_const, 1)
                pool.wait_ge(s_const, 8)
                pool.affine_select(out=ident[:, :], in_=ident[:, :], compare_op=ALU.not_equal, fill=1.0, base=0,
                                   pattern=[[-1, P]], channel_multiplier=1).then_inc(s_const, 1)
                pool.affine_select(out=before[:, :], in_=before[:, :], compare_op=ALU.is_gt, fill=0.0, base=0,
                                   pattern=[[1, P]], channel_multiplier=-1).then_inc(s_const, 1)
                pool.affine_select(out=valid[:, :], in_=valid[:, :], compare_op=ALU.is_gt, fill=0.0, base=N,
                                   pattern=[[-P, NT]], channel_multiplier=-1).then_inc(s_const, 1)
                pool.wait_ge(s_const, 11)
                for g in range(P // HD):
                    pool.memset(heads[g * HD:(g + 1) * HD, g * HD:(g + 1) * HD], 1.0).then_inc(s_const, 1)
                pool.wait_ge(s_const, 15)
                pool.memset(acc_w[:, :], 0.0).then_inc(s_zero, 1)
                pool.memset(smax[:, :, :], LOW).then_inc(s_zero, 1)
                pool.memset(low[:, :, :], 1.0e30).then_inc(s_zero, 1)
                pool.memset(kv_sum[:, :, :], 0.0).then_inc(s_zero, 1)
                for j in range(PRE):
                    pool.wait_ge(s_rows_out[j], 16 * (UNITS // PRE + 1))

                def part(eng, third, i, k):
                    if third == 0:
                        b = i * SLOTS + k
                        pool.wait_ge(s_idx[k], (i + 1) * 16)
                        pool.sem_inc(hold_p, 1)
                        e_msg.wait(pool, b - SLOTS + 1)
                        pool.sem_inc(hold_p, 1)
                        for t in range(BT):
                            pool.indirect_dma_start(got[k][:, t, :, :].rearrange("p d r -> p (d r)"), None, table_d,
                                                    bass.IndirectOffsetOnAxis(ap=idx[k][:, t:t + 1], axis=0)).then_inc(s_got[k], 16)
                edge_bodies(pool, part, nothing, nothing)

            @block.vector
            def _(dve):
                link = linker(dve)
                dve.sem_inc(e_msg.sem, SLOTS)
                dve.sem_inc(e_merge.sem, 2)
                dve.sem_inc(m_sum.sem, 1)
                c["V"].open(dve)
                dve.wait_ge(s_w["wg"], 32)
                dve.wait_ge(s_score_w, 1)
                dve.tensor_copy(wg_s[:, :, :, F:ROW], bank[7][:, 0:KC * 2 * H].rearrange("p (k d h) -> p k d h", k=KC, d=2))\
                    .then_inc(s_score_c, 1)
                with dve.Fori(0, UNITS // PRE) as i:
                    for j in range(PRE + 2):
                        if j < PRE:
                            u = i * PRE + j
                            dve.wait_ge(s_x[j], (i + 1) * 16)
                            for t in range(UT):
                                ins = dve.bn_stats(stats[:, j, t, :], x_u[:, j, t, :])
                            ins.then_inc(c_stats.sem, 1)
                            c_stats.wait(dve, u + 1)
                            dve.sem_inc(hold_v, 1)
                            for t in range(UT):
                                ins = dve.bn_aggr(mv[:, j, t, :], stats[:, j, t, :])
                            ins.then_inc(c_mv.sem, 1)
                        if 1 <= j <= PRE:
                            n = j - 1
                            u = i * PRE + n
                            c_sd.wait(dve, u + 1)
                            dve.reciprocal(rstd[:, n, :], sd[:, n, :]).then_inc(c_rstd.sem, 1)
                            c_rstd.wait(dve, u + 1)
                            for t in range(UT):
                                ins = dve.tensor_scalar(xn[:, n, t, :], x_u[:, n, t, :], mv[:, n, t, 0:1], rstd[:, n, t:t + 1],
                                                        ALU.subtract, ALU.mult)
                            ins.then_inc(c_xn.sem, 1)
                            c_xn.wait(dve, u + 1)
                            dve.tensor_tensor(x_u[:, n, :, :], x_u[:, n, :, :], xn[:, n, :, :], ALU.add).then_inc(c_res.sem, 1)
                        if j >= 2:
                            n = j - 2
                            u = i * PRE + n
                            c_rows.wait(dve, u + 1)
                            dve.tensor_copy(p_all[:, bass.ds(u * UT, UT), :, :], rows[:, n, :, :, F:ROW]).then_inc(c_rows_p.sem, 1)
                dve.wait_ge(s_w["dst"], 16)
                link(dve.tensor_copy(dst_f, dst_i))
                link(dve.memset(gmin, PAD_NODE))
                link(dve.memset(gmax, 0.0))
                db = dst_f.rearrange("p (b t) -> p b t", t=BT)
                gv = gmin[:, 0:GR].rearrange("p (b g) -> p b g", g=NG)
                xv = gmax[:, 0:GR].rearrange("p (b g) -> p b g", g=NG)
                for g, (a, z) in enumerate(GROUPS):
                    link(dve.tensor_reduce(gv[:, :, g], db[:, :, a:z], AX, ALU.min))
                link(dve.tensor_scalar(dst_rel[:, :], dst_f, 0.5 * PAD_NODE, None, ALU.is_lt))
                link(dve.tensor_tensor(dst_rel[:, :], dst_rel[:, :], dst_f, ALU.mult))
                dr = dst_rel[:, :].rearrange("p (b t) -> p b t", t=BT)
                for g, (a, z) in enumerate(GROUPS):
                    link(dve.tensor_reduce(xv[:, :, g], dr[:, :, a:z], AX, ALU.max))
                dve.sem_inc(s_ask, 1)
                dve.wait_ge(s_given, 1)
                for k in range(GC):
                    link(dve.tensor_reduce(bcol[:, k:k + 1], bank[0][:, k * P:(k + 1) * P], AX, ALU.min))
                    link(dve.tensor_reduce(mcol[:, k:k + 1], bank[1][:, k * P:(k + 1) * P], AX, ALU.max))
                link(dve.tensor_scalar(bcol, bcol, float(NP - WIN), None, ALU.min))
                link(dve.tensor_tensor(mcol, mcol, bcol, ALU.subtract))
                link(dve.tensor_reduce(verdict[:, 0:1], mcol, AX, ALU.max))
                link(dve.tensor_scalar(verdict[:, 0:1], verdict[:, 0:1], WIN - 0.5, None, ALU.subtract))
                dve.sem_inc(s_ask, 1)
                dve.wait_ge(s_given, 2)
                link(dve.tensor_copy(gmin[0:GC, 0:P], bank[2][0:GC, 0:P]))
                dve.sem_inc(s_first, 1)

                def spread(ready, dst):
                    asked[0] += 1
                    dve.wait_ge(s_given, 1 + 2 * asked[0])
                    link(dve.tensor_reduce(v4[:, :], bank[0][0:4, 0:P], AX, ALU.max))
                    link(dve.tensor_scalar(vd[:, :], ident[0:4, 0:4], v4[:, 0:1], None, ALU.mult))
                    dve.sem_inc(s_ask, 1)
                    dve.wait_ge(s_given, 2 + 2 * asked[0])
                    link(dve.tensor_copy(dst, bank[0][:, P:P + 4]))

                dve.wait_ge(s_w["attr"], 16)
                for d in range(2):
                    link(dve.tensor_reduce(ext[:, d:d + 1], attr[:, :, d], AX, ALU.max))
                    link(dve.tensor_reduce(ext[:, 2 + d:3 + d], attr[:, :, d], AX, ALU.min))
                link(dve.tensor_scalar(ext[:, 2:4], ext[:, 2:4], -1.0, None, ALU.mult))
                dve.sem_inc(s_ask, 1)
                spread(None, ext_bc)
                link(dve.tensor_scalar(ext_bc[:, 2:4], ext_bc[:, 2:4], -1.0, None, ALU.mult))
                c_rows_p.wait(dve, UNITS)
                for d in range(2):
                    link(dve.tensor_scalar(p_lo[:, :, d, :], p_all[:, :, d, :], ext_bc[:, 2 + d:3 + d], None, ALU.mult))
                    link(dve.scalar_tensor_tensor(out=p_lo[:, :, d, :], in0=p_all[:, :, d, :], scalar=ext_bc[:, d:d + 1],
                                                  in1=p_lo[:, :, d, :], op0=ALU.mult, op1=ALU.max))
                link(dve.tensor_tensor(p_lo[:, :, 0, :], p_lo[:, :, 0, :], p_lo[:, :, 1, :], ALU.add))
                link(dve.tensor_reduce(ext, p_lo[:, :, 0, :].rearrange("p t h -> p h t"), AX, ALU.max))
                dve.sem_inc(s_ask, 1)
                spread(None, ext_bc)
                link(dve.scalar_tensor_tensor(out=bound[:, :], in0=ext_bc, scalar=SLOPE, in1=ext_bc, op0=ALU.mult, op1=ALU.max))
                dve.wait_ge(s_first_in, 16)
                lim = limit[:, 0:GR]
                link(dve.tensor_copy(lim, limit_i[:, :, :].rearrange("p b g -> p (b g)")[:, 0:GR]))
                link(dve.tensor_tensor(lim, lim, first_bc[:, 0:GR], ALU.subtract))
                link(dve.tensor_reduce(verdict[:, 1:2], lim, AX, ALU.max))
                link(dve.tensor_scalar(lim, lim, 0.0, None, ALU.max))
                link(dve.tensor_tensor(first_bc[:, 0:GR], first_bc[:, 0:GR], lim, ALU.add))
                bb = first_bc[:, 0:GR].rearrange("p (b g) -> p b g", g=NG)
                for g, (a, z) in enumerate(GROUPS):
                    link(dve.tensor_tensor(dr[:, :, a:z], db[:, :, a:z],
                                           bb[:, :, g:g + 1].to_broadcast([P, BLOCKS, z - a]), ALU.subtract))
                link(dve.tensor_copy(first_i[:, :], first_bc[0:1, :]))
                link(dve.tensor_copy(iota[:, :], iota_i[:, :]))
                dve.wait_ge(s_zero, 4)
                link(dve.memset(acc[:, :, :], 0.0))
                for j in range(PRE):
                    for q in (s_xnt_out[j], s_rows_out[j], s_res_out[j]):
                        dve.wait_ge(q, 16 * (UNITS // PRE + 1))
                dve.sem_inc(s_begin, 1)
                dve.wait_ge(s_w["chain"], 16 * 11)

                def part(eng, third, i, k):
                    b = i * SLOTS + k
                    w = k % 2
                    before_b = b if k == 0 else b - 1
                    if third == 0:
                        dve.wait_ge(s_att[k], (i + 1) * 16)
                        dve.wait_ge(s_got[k], (i + 1) * (16 * BT))
                        dve.tensor_tensor(got[k][:, :, :, :], got[k][:, :, :, :],
                                          att[k][:, :, :].rearrange("p t (d o) -> p t d o", o=1).to_broadcast([P, BT, 2, ROW]),
                                          ALU.mult).then_inc(e_prod.sem, 1)
                        e_prod.wait(dve, b + 1)
                        e_scat.wait(dve, before_b)
                        dve.tensor_tensor(msg[:, w, :, :], got[k][:, :, 0, :], got[k][:, :, 1, :], ALU.add).then_inc(e_msg.sem, 1)
                        dve.tensor_tensor(onehot[:, w, :, :],
                                          dst_rel[:, bass.ds(b * BT, BT)].rearrange("p (t o) -> p t o", o=1).to_broadcast([P, BT, WIN]),
                                          iota[:, :].rearrange("p (o w) -> p o w", o=1).to_broadcast([P, BT, WIN]),
                                          ALU.is_equal).then_inc(e_onehot.sem, 1)
                        e_msg.wait(dve, b + 1)
                        sc = msg[:, w, :, F:ROW]
                        dve.scalar_tensor_tensor(out=lrelu[:, :, :], in0=sc, scalar=SLOPE, in1=sc, op0=ALU.mult, op1=ALU.max)\
                            .then_inc(e_lrelu.sem, 1)
                        dve.tensor_tensor(smax[:, :, :], smax[:, :, :], sc, ALU.max).then_inc(e_max.sem, 1)
                        e_lrelu.wait(dve, b + 1)
                        e_wgt.wait(dve, before_b)
                        dve.tensor_tensor(score[:, w, :, :], lrelu[:, :, :],
                                          bound[:, :].rearrange("p (o h) -> p o h", o=1).to_broadcast([P, BT, H]), ALU.subtract)\
                            .then_inc(e_score.sem, 1)
                    if third == 1:
                        e_onehot.wait(dve, b + 1)
                        e_wgt.wait(dve, b + 1)
                        dve.tensor_tensor(woh[:, w, :, :, :],
                                          onehot[:, w, :, :].rearrange("p t (o w) -> p t o w", o=1).to_broadcast([P, BT, H, WIN]),
                                          wgt[:, w, :, :].rearrange("p t (h o) -> p t h o", o=1).to_broadcast([P, BT, H, WIN]),
                                          ALU.mult).then_inc(e_woh.sem, 1)
                    if third == 2:
                        e_grp.wait(dve, b + 1)
                        for g in range(NG):
                            n = i * (SLOTS * NG) + k * NG + g
                            first = dve.value_load(first_i[0:1, bass.ds(n, 1)], min_val=0, max_val=NP - WIN)
                            ps = bank[k % 2][:, g * 3 * WIN:(g + 1) * 3 * WIN]
                            e_merge.wait(dve, n)
                            a = acc[:, :, bass.ds(first, WIN)]
                            dve.tensor_tensor(a, a, ps[:, 0:2 * WIN].rearrange("p (h w) -> p h w", h=2), ALU.add).then_inc(e_acc.sem, 1)
                            a = acc_w[:, bass.ds(first, WIN)]
                            dve.tensor_tensor(a, a, ps[0:H, 2 * WIN:3 * WIN], ALU.add).then_inc(e_merge.sem, 1)

                def mix(eng, step, v):
                    if step == 1:
                        m_proj.wait(dve, v + 1)
                        for t in range(UT):
                            ins = dve.tensor_scalar(T0[:, t * C:(t + 1) * C], bank[2 + t][:, 0:C], 0.0, None, ALU.min)
                        ins.then_inc(m_min.sem, 1)
                    if step == 2:
                        m_exp.wait(dve, v + 1)
                        m_v.wait(dve, v + 1)
                        for t in range(UT):
                            ins = dve.scalar_tensor_tensor(out=T2[:, t * C:(t + 1) * C], in0=bank[2 + t][:, 0:C], scalar=0.0,
                                                           in1=T1[:, t * C:(t + 1) * C], op0=ALU.max, op1=ALU.add)
                        ins.then_inc(m_k.sem, 1)
                        m_kv.wait(dve, v + 1)
                        m_sum.wait(dve, v)
                        dve.tensor_tensor(kv_sum[:, :, :], kv_sum[:, :, :],
                                          bank[4][:, 0:KC * (P + 1)].rearrange("p (j n) -> p j n", j=KC), ALU.add).then_inc(m_sum.sem, 1)
                    if step == 3:
                        m_sum.wait(dve, UNITS)
                        for j in range(KC):
                            dve.scalar_tensor_tensor(out=kv[:, j, :], in0=kv_sum[:, j, 0:P], scalar=1.0 / N, in1=heads[:, :],
                                                     op0=ALU.mult, op1=ALU.mult)
                            ins = dve.tensor_scalar(ksum[:, j, :], heads[:, :], kv_sum[:, j, P:P + 1], None, ALU.mult)
                        ins.then_inc(s_kv, 1)

                def chain(eng, step, u, seen, groups):
                    vector_chain(dve, s, c, step, u, seen, s_full)

                edge_bodies(dve, part, mix, chain)
                for u in range(DONE, UNITS):
                    for step in range(STEPS):
                        vector_chain(dve, s, c, step, u, BLOCKS, s_full if u < UNITS - 1 else s_last)
                link(dve.tensor_tensor(verdict[:, 3:4], verdict[:, 0:1], verdict[:, 1:2], ALU.max))
                c["V"].wait(dve, "low", UNITS)
                link(dve.tensor_scalar(vb[:, :], small["gap"][:, :], -1.0, -GAP_MAX, ALU.mult, ALU.add))
                link(dve.tensor_reduce(verdict[:, 1:2], vb[:, :], AX, ALU.max))
                for t in range(UT):
                    link(dve.tensor_tensor(tol[:, t, :], small["guard"][:, :], low[:, t, :], ALU.subtract))
                link(dve.tensor_reduce(verdict[:, 2:3], tol[:, :, :].rearrange("p t h -> p (t h)"), AX, ALU.max))
                dve.sem_inc(s_ask, 1)
                spread(None, vb[:, :])
                link(dve.tensor_reduce(v_one[:, :], vb[:, :], AX, ALU.max))
                link(dve.tensor_scalar(v_one[:, :], v_one[:, :], 0.0, None, ALU.is_gt))
                link(dve.tensor_copy(flag_i[:, :], v_one[:, :]))

            @block.scalar
            def _(act):
                act.sem_inc(e_wgt.sem, 1)
                c["A"].open(act)
                act.wait_ge(s_const, 3)
                with act.Fori(0, UNITS // PRE) as i:
                    for j in range(PRE + 2):
                        if j < PRE:
                            u = i * PRE + j
                            c_mv.wait(act, u + 1)
                            act.activation(sd[:, j, :], mv[:, j, :, 1], ACT.Sqrt, bias=eps_col[:, 0:1]).then_inc(c_sd.sem, 1)
                        if 1 <= j <= PRE:
                            n = j - 1
                            u = i * PRE + n
                            c_tr.wait(act, u + 1)
                            act.wait_ge(s_xnt_out[n], (i + 1) * 16)
                            act.activation(xnt[:, n, :, :], bank[n % 3][:, :].rearrange("p (k n) -> p k n", k=KC), ACT.Copy)\
                                .then_inc(c_xnt.sem, 1)
                        if j >= 2:
                            n = j - 2
                            u = i * PRE + n
                            c_tab.wait(act, u + 1)
                            act.wait_ge(s_rows_out[n], (i + 1) * 16)
                            act.activation(rows[:, n, :, :, :],
                                           bank[4 + n % 3][:, 0:UT * 2 * ROW].rearrange("p (t d r) -> p t d r", t=UT, d=2),
                                           ACT.Copy).then_inc(c_rows.sem, 1)
                for j in range(PRE):
                    act.wait_ge(s_xnt_out[j], 16 * (UNITS // PRE + 1))
                    act.wait_ge(s_res_out[j], 16 * (UNITS // PRE + 1))
                act.wait_ge(s_first, 1)
                act.dma_start(first_d.rearrange("(c p) -> c p", c=GC), gmin[0:GC, 0:P]).then_inc(s_first_out, 16)
                act.wait_ge(s_first_out, 16)
                act.dma_start(first_bc, first_d.rearrange("(a n) -> a n", a=1).to_broadcast([P, GC * P])).then_inc(s_first_in, 16)

                def part(eng, third, i, k):
                    if third == 0:
                        b = i * SLOTS + k
                        e_score.wait(act, b + 1)
                        e_scat.wait(act, b if k == 0 else b - 1)
                        act.activation(wgt[:, k % 2, :, :], score[:, k % 2, :, :], ACT.Exp).then_inc(e_wgt.sem, 1)

                def mix(eng, step, v):
                    if step == 0:
                        act.dma_start(T4[:, :, :], xnt_d[:, :, bass.ds(v * UN, UN)]).then_inc(m_x, 16)
                    if step == 1:
                        m_min.wait(act, v + 1)
                        act.activation(T1[:, :], T0[:, :], ACT.Exp).then_inc(m_exp.sem, 1)
                        for t in range(UT):
                            ins = act.activation(T3[:, t * C:(t + 1) * C], bank[2 + t][:, C:2 * C], ACT.Copy)
                        ins.then_inc(m_v.sem, 1)
                    if step == 3:
                        m_proj.wait(act, UNITS)
                        act.dma_start(f1[:, :, :], f1_d.rearrange("(k p) c -> p k c", p=P)).then_inc(s_w["ff"], 16)

                def chain(eng, step, u, seen, groups):
                    scalar_chain(act, s, c, step, u, lambda a: e_merge.wait(a, groups))

                edge_bodies(act, part, mix, chain)
                for u in range(DONE, UNITS):
                    for step in range(STEPS):
                        scalar_chain(act, s, c, step, u, lambda a: e_merge.wait(a, GR))

            @block.tensor
            def _(pe):
                pe.sem_inc(e_scat.sem, 1)
                c["P"].open(pe)
                pe.wait_ge(s_const, 15)
                pe.wait_ge(s_w["wsum"], 16)
                pe.wait_ge(s_w["attn"], 16)
                for k in range(KC):
                    for d in range(2):
                        c0 = (k * 2 + d) * H
                        ins = pe.matmul(bank[7][:, c0:c0 + H], wsum_s[:, d, k * P:(k + 1) * P], attn_s, start=True, stop=True)
                ins.then_inc(s_score_w, 1)
                pe.wait_ge(s_score_c, 1)
                with pe.Fori(0, UNITS // PRE) as i:
                    for j in range(PRE + 1):
                        if j < PRE:
                            c_xn.wait(pe, i * PRE + j + 1)
                            for t in range(UT):
                                for k in range(KC):
                                    ins = pe.transpose(bank[j % 3][:, k * UN + t * P:k * UN + (t + 1) * P],
                                                       xn[:, j, t, k * P:(k + 1) * P], ident[:, :])
                            ins.then_inc(c_tr.sem, 1)
                        if j:
                            n = j - 1
                            c_xnt.wait(pe, i * PRE + n + 1)
                            for t in range(UT):
                                for k in range(KC):
                                    ins = pe.matmul(bank[4 + n % 3][:, t * 2 * ROW:(t + 1) * 2 * ROW], xnt[:, n, k, t * P:(t + 1) * P],
                                                    wg_s[:, k, :, :].rearrange("p d r -> p (d r)"), start=(k == 0), stop=(k == KC - 1))
                            ins.then_inc(c_tab.sem, 1)
                pe.wait_ge(s_ask, 1)
                for b, g in ((0, gmin), (1, gmax)):
                    for k in range(GC):
                        ins = pe.transpose(bank[b][:, k * P:(k + 1) * P], g[:, k * P:(k + 1) * P], ident[:, :])
                ins.then_inc(s_given, 1)
                pe.wait_ge(s_ask, 2)
                pe.transpose(bank[2][0:GC, 0:P], bcol, ident[:, :]).then_inc(s_given, 1)

                def spread(n, cols):
                    pe.wait_ge(s_ask, 1 + 2 * n)
                    pe.transpose(bank[0][0:4, 0:P], cols, ident[:, :]).then_inc(s_given, 1)
                    pe.wait_ge(s_ask, 2 + 2 * n)
                    pe.matmul(bank[0][:, P:P + 4], ones[0:4, :], vd[:, :], start=True, stop=True).then_inc(s_given, 1)

                spread(1, ext)
                spread(2, ext)
                pe.wait_ge(s_begin, 1)
                pe.wait_ge(s_w["mix"], 32)

                def part(eng, third, i, k):
                    if third != 1:
                        return
                    b = i * SLOTS + k
                    w = k % 2
                    e_woh.wait(pe, b + 1)
                    e_merge.wait(pe, (b if k == 0 else b - 1) * NG)
                    for g, (a, z) in enumerate(GROUPS):
                        ps = bank[w][:, g * 3 * WIN:(g + 1) * 3 * WIN]
                        for half in range(2):
                            for t in range(a, z):
                                pe.matmul(ps[half * F:(half + 1) * F, 0:2 * WIN], msg[:, w, t, 0:F],
                                          woh[:, w, t, 2 * half:2 * half + 2, :].rearrange("p h w -> p (h w)"),
                                          start=(t == a), stop=(t == z - 1))
                        for t in range(a, z):
                            ins = pe.matmul(ps[0:H, 2 * WIN:3 * WIN], wgt[:, w, t, :], onehot[:, w, t, :], start=(t == a), stop=(t == z - 1))
                    ins.then_inc(e_grp.sem, 1)
                    e_grp.wait(pe, b + 1)
                    pe.sem_inc(e_scat.sem, 1)

                def mix(eng, step, v):
                    if step == 1:
                        pe.wait_ge(m_x, (v + 1) * 16)
                        for t in range(UT):
                            for k in range(KC):
                                ins = pe.matmul(bank[2 + t][:, :], T4[:, k, t * P:(t + 1) * P], wkv[:, k, :], start=(k == 0), stop=(k == KC - 1))
                        ins.then_inc(m_proj.sem, 1)
                    if step == 2:
                        m_v.wait(pe, v + 1)
                        m_k.wait(pe, v + 1)
                        for j in range(KC):
                            to = j * (P + 1)
                            for t in range(UT):
                                cols = slice(t * C + j * P, t * C + (j + 1) * P)
                                pe.matmul(bank[4][:, to:to + P], T2[:, cols], T3[:, cols], start=(t == 0), stop=(t == UT - 1))
                            for t in range(UT):
                                cols = slice(t * C + j * P, t * C + (j + 1) * P)
                                ins = pe.matmul(bank[4][:, to + P:to + P + 1], T2[:, cols], valid[:, bass.ds(v * UT + t, 1)],
                                                start=(t == 0), stop=(t == UT - 1))
                        ins.then_inc(m_kv.sem, 1)
                    if step == 3:
                        pe.wait_ge(s_kv, 1)
                        pe.wait_ge(s_w["chain"], 16 * 11)
                        pe.wait_ge(s_w["ff"], 32)

                def chain(eng, step, u, seen, groups):
                    tensor_chain(pe, s, c, step, u)

                edge_bodies(pe, part, mix, chain)
                for u in range(DONE, UNITS):
                    for step in range(STEPS):
                        tensor_chain(pe, s, c, step, u)
                spread(3, verdict[:, :])

        whole = BLOCKS // SLOTS
        idx_g, dst_gi, att_g, got_g = idx[0], idx[1], att[0], got[0]
        dst_g = dst_rel[:, 0:BT]
        s_gen = sem("s_gen")
        s_gdst = sem("s_gdst")
        idx_n, att_n, got_n = (whole + 1) * 16, (whole + 1) * 16, (whole + 1) * 16 * BT
        g_prod, g_msg = Count(e_prod.sem, BLOCKS), Count(e_msg.sem, SLOTS + BLOCKS)
        g_lrelu, g_score, g_wgt = Count(e_lrelu.sem, BLOCKS), Count(e_score.sem, BLOCKS), Count(e_wgt.sem, BLOCKS + 1)
        g_onehot, g_woh = Count(e_onehot.sem, BLOCKS), Count(e_woh.sem, BLOCKS)
        g_grp, g_merge = Count(e_grp.sem, BLOCKS), Count(e_merge.sem, 2 + GR)
        g_dst = count("g_dst", 1); g_rel = count("g_rel", 1)
        g_acc = Count(e_acc.sem, GR)
        cg = dict(c, before=UNITS)

        def way(eng):
            return eng.value_load(flag_i[0:1, 0:1], min_val=0, max_val=1)

        def again(eng, chain):
            with eng.Fori(0, UNITS) as u:
                for step in range(STEPS):
                    chain(step, u)

        with nc.Block() as block:
            @block.sync
            def _(sp):
                with sp.If(way(sp) > 0):
                    with sp.Fori(0, BLOCKS) as b:
                        g_merge.wait(sp, b * WINS)
                        sp.sem_inc(hold_s, 1)
                        sp.dma_start(idx_g[:, :], src_t[:, bass.ds(b * BT, BT)]).then_inc(s_idx[0], 16)
                        sp.dma_start(att_g[:, :, :], attr_t[:, bass.ds(b * BT, BT), :]).then_inc(s_att[0], 16)
                        sp.dma_start(dst_gi[:, :], dst_t[:, bass.ds(b * BT, BT)]).then_inc(s_gdst, 16)
                    sp.sem_inc(hold_s, 1)

            @block.gpsimd
            def _(pool):
                with pool.If(way(pool) > 0):
                    pool.memset(acc[:, :, :], 0.0).then_inc(s_zero, 1)
                    pool.wait_ge(s_zero, 5)
                    pool.memset(acc_w[:, :], 0.0).then_inc(s_zero, 1)
                    with pool.Fori(0, BLOCKS) as b:
                        pool.wait_ge(s_idx[0], b * 16 + (idx_n + 16))
                        pool.sem_inc(hold_p, 1)
                        g_merge.wait(pool, b * WINS)
                        pool.sem_inc(hold_p, 1)
                        for t in range(BT):
                            pool.indirect_dma_start(got_g[:, t, :, :].rearrange("p d r -> p (d r)"), None, table_d,
                                                    bass.IndirectOffsetOnAxis(ap=idx_g[:, t:t + 1], axis=0)).then_inc(s_got[0], 16)
                    pool.sem_inc(hold_p, 1)

            @block.vector
            def _(dve):
                with dve.If(way(dve) > 0):
                    dve.sem_inc(g_dst.sem, 1)
                    dve.sem_inc(g_rel.sem, 1)
                    dve.tensor_copy(bound[:, :], small["lead"][:, :]).then_inc(s_gen, 1)
                    dve.wait_ge(s_gen, 1)
                    dve.wait_ge(s_zero, 6)
                    with dve.Fori(0, BLOCKS) as b:
                        dve.wait_ge(s_gdst, (b + 1) * 16)
                        g_rel.wait(dve, b * WINS)
                        dve.tensor_scalar(dst_g, dst_gi[:, :], 1.0, float(WIN), ALU.mult, ALU.add).then_inc(g_dst.sem, 1)
                        dve.wait_ge(s_att[0], b * 16 + (att_n + 16))
                        dve.wait_ge(s_got[0], b * (16 * BT) + (got_n + 16 * BT))
                        dve.tensor_tensor(got_g[:, :, :, :], got_g[:, :, :, :],
                                          att_g[:, :, :].rearrange("p t (d o) -> p t d o", o=1).to_broadcast([P, BT, 2, ROW]),
                                          ALU.mult).then_inc(g_prod.sem, 1)
                        g_prod.wait(dve, b + 1)
                        g_grp.wait(dve, b * WINS)
                        dve.tensor_tensor(msg[:, 0, :, :], got_g[:, :, 0, :], got_g[:, :, 1, :], ALU.add).then_inc(g_msg.sem, 1)
                        g_msg.wait(dve, b + 1)
                        sc = msg[:, 0, :, F:ROW]
                        dve.scalar_tensor_tensor(out=lrelu[:, :, :], in0=sc, scalar=SLOPE, in1=sc, op0=ALU.mult, op1=ALU.max)\
                            .then_inc(g_lrelu.sem, 1)
                        g_lrelu.wait(dve, b + 1)
                        dve.tensor_tensor(score[:, 0, :, :], lrelu[:, :, :],
                                          bound[:, :].rearrange("p (o h) -> p o h", o=1).to_broadcast([P, BT, H]), ALU.subtract)\
                            .then_inc(g_score.sem, 1)
                        g_dst.wait(dve, b + 1)
                        g_wgt.wait(dve, b + 1)
                        dve.sem_inc(hold_v, 1)
                        with dve.Fori(0, WINS) as w:
                            n = b * WINS + w
                            g_onehot.wait(dve, n)
                            dve.tensor_scalar(dst_g, dst_g, float(WIN), None, ALU.subtract).then_inc(g_rel.sem, 1)
                            g_rel.wait(dve, n + 1)
                            g_grp.wait(dve, n)
                            dve.tensor_tensor(onehot[:, 0, :, :],
                                              dst_g.rearrange("p (t o) -> p t o", o=1).to_broadcast([P, BT, WIN]),
                                              iota[:, :].rearrange("p (o w) -> p o w", o=1).to_broadcast([P, BT, WIN]),
                                              ALU.is_equal).then_inc(g_onehot.sem, 1)
                            g_onehot.wait(dve, n + 1)
                            dve.tensor_tensor(woh[:, 0, :, :, :],
                                              onehot[:, 0, :, :].rearrange("p t (o w) -> p t o w", o=1).to_broadcast([P, BT, H, WIN]),
                                              wgt[:, 0, :, :].rearrange("p t (h o) -> p t h o", o=1).to_broadcast([P, BT, H, WIN]),
                                              ALU.mult).then_inc(g_woh.sem, 1)
                            g_grp.wait(dve, n + 1)
                            g_merge.wait(dve, n)
                            a = acc[:, :, bass.ds(w * WIN, WIN)]
                            dve.tensor_tensor(a, a, bank[0][:, 0:2 * WIN].rearrange("p (h w) -> p h w", h=2), ALU.add).then_inc(g_acc.sem, 1)
                            a = acc_w[:, bass.ds(w * WIN, WIN)]
                            dve.tensor_tensor(a, a, bank[0][0:H, 2 * WIN:3 * WIN], ALU.add).then_inc(g_merge.sem, 1)
                        dve.sem_inc(hold_v, 1)
                    dve.sem_inc(hold_v, 1)
                    again(dve, lambda step, u: vector_chain(dve, s, cg, step, u, BLOCKS, s_full))
                    dve.sem_inc(hold_v, 1)

            @block.scalar
            def _(act):
                with act.If(way(act) > 0):
                    with act.Fori(0, BLOCKS) as b:
                        g_score.wait(act, b + 1)
                        g_grp.wait(act, b * WINS)
                        act.activation(wgt[:, 0, :, :], score[:, 0, :, :], ACT.Exp).then_inc(g_wgt.sem, 1)
                    act.sem_inc(hold_a, 1)
                    again(act, lambda step, u: scalar_chain(act, s, cg, step, u, lambda a: g_merge.wait(a, BLOCKS * WINS)))
                    act.wait_ge(c["base_out"], 16 * (2 * UNITS + 1))

            @block.tensor
            def _(pe):
                with pe.If(way(pe) > 0):
                    with pe.Fori(0, BLOCKS) as b:
                        with pe.Fori(0, WINS) as w:
                            n = b * WINS + w
                            g_woh.wait(pe, n + 1)
                            g_merge.wait(pe, n)
                            for half in range(2):
                                for t in range(BT):
                                    pe.matmul(bank[0][half * F:(half + 1) * F, 0:2 * WIN], msg[:, 0, t, 0:F],
                                              woh[:, 0, t, 2 * half:2 * half + 2, :].rearrange("p h w -> p (h w)"),
                                              start=(t == 0), stop=(t == BT - 1))
                            for t in range(BT):
                                ins = pe.matmul(bank[0][0:H, 2 * WIN:3 * WIN], wgt[:, 0, t, :], onehot[:, 0, t, :],
                                                start=(t == 0), stop=(t == BT - 1))
                            ins.then_inc(g_grp.sem, 1)
                        pe.sem_inc(hold_t, 1)
                    pe.sem_inc(hold_t, 1)
                    again(pe, lambda step, u: tensor_chain(pe, s, cg, step, u))
                    pe.sem_inc(hold_t, 1)

        work.close()
        edge.close()

        last = ExitStack()
        base = sb("base", [P, NT, C], F32, last)
        wv = sb("wv", [P, NT], F32, last)
        hit = sb("hit", [P, NT], F32, last)
        above = sb("above", [P, NT], F32, last)
        level = sb("level", [P, NT], F32, last)
        pick = sb("pick", [P, NT], F32, last)
        cnt = sb("cnt", [P, 1], F32, last)
        need = sb("need", [P, 1], F32, last)
        by_tile_sum = sb("by_tile_sum", [NT, P], F32, last)
        key = {n: sb(f"key_{n}", [P, 1], I32, last) for n in ("found", "bit", "try", "a", "b", "code", "yes", "sign", "minus", "c31", "c1")}
        l_in = [sem(f"l_in{j}") for j in range(OUT_CHUNKS)]
        l_out = sem("l_out"); l_key = sem("l_key"); l_step = sem("l_step"); l_v = sem("l_v"); l_p = sem("l_p"); l_tail = sem("l_tail")
        l_done = sem("l_done")
        l_try = count("l_try"); l_a = count("l_a"); l_b = count("l_b"); l_code = count("l_code"); l_cnt = count("l_cnt")
        l_sum = count("l_sum"); l_yes = count("l_yes"); l_add = count("l_add"); l_found = count("l_found", 1)
        CT = NT // OUT_CHUNKS

        with nc.Block() as block:
            @block.sync
            def _(sp):
                for j in range(OUT_CHUNKS):
                    sp.dma_start(base[:, j * CT:(j + 1) * CT, :], base_d[j * CT * P:(j + 1) * CT * P, :].rearrange("(t p) c -> p t c", p=P))\
                        .then_inc(l_in[j], 16)
                for j in range(OUT_CHUNKS):
                    full = min((j + 1) * CT, N // P)
                    sp.wait_ge(l_done, j + 1)
                    sp.dma_start(out[j * CT * P:full * P, :].rearrange("(t p) c -> p t c", p=P), base[:, j * CT:full, :]).then_inc(l_out, 16)
                sp.dma_start(out[N // P * P:N, :], base[0:N % P, N // P, :]).then_inc(l_out, 16)
                sp.wait_ge(l_out, 16 * (OUT_CHUNKS + 1))

            @block.gpsimd
            def _(pool):
                for name, value in (("found", 0), ("bit", -2 ** 31), ("sign", -2 ** 31), ("minus", -1), ("c31", 31), ("c1", 1)):
                    pool.iota(key[name][:, :], pattern=[[0, 1]], base=value, channel_multiplier=0).then_inc(l_key, 1)

            @block.vector
            def _(dve):
                n = [0]

                def link(ins):
                    n[0] += 1
                    ins.then_inc(l_v, 1)
                    dve.wait_ge(l_v, n[0])

                dve.sem_inc(l_found.sem, 1)
                link(dve.tensor_scalar(level[:, :], valid[:, :], 1.0, -LOW, ALU.subtract, ALU.mult))
                link(dve.tensor_tensor(wv[:, :], w_all[:, :], valid[:, :], ALU.mult))
                link(dve.tensor_tensor(wv[:, :], wv[:, :], level[:, :], ALU.add))
                dve.wait_ge(l_key, 6)
                k = {name: tile[:, :] for name, tile in key.items()}

                def code_of(source, r):
                    dve.tensor_scalar(k["a"], source, k["c31"], k["minus"], ALU.arith_shift_right, ALU.bitwise_xor).then_inc(l_a.sem, 1)
                    l_a.wait(dve, r)
                    dve.tensor_tensor(k["b"], k["a"], k["sign"], ALU.bitwise_or).then_inc(l_b.sem, 1)
                    l_b.wait(dve, r)
                    dve.tensor_tensor(k["code"], k["b"], source, ALU.bitwise_xor).then_inc(l_code.sem, 1)
                    l_code.wait(dve, r)

                with dve.Fori(0, 32) as i:
                    l_found.wait(dve, i)
                    dve.tensor_tensor(k["try"], k["found"], k["bit"], ALU.bitwise_or).then_inc(l_try.sem, 1)
                    l_try.wait(dve, i + 1)
                    code_of(k["try"], i + 1)
                    dve.tensor_scalar(hit[:, :], wv[:, :], k["code"].bitcast(F32), None, ALU.is_ge, ALU.add, accum_out=cnt[:, :])\
                        .then_inc(l_cnt.sem, 1)
                    l_sum.wait(dve, i + 1)
                    dve.tensor_scalar(k["yes"], bank[0][:, 0:1], TOP - 0.5, None, ALU.is_gt).then_inc(l_yes.sem, 1)
                    l_yes.wait(dve, i + 1)
                    dve.tensor_tensor(k["a"], k["yes"], k["bit"], ALU.mult).then_inc(l_add.sem, 1)
                    l_add.wait(dve, i + 1)
                    dve.tensor_tensor(k["found"], k["found"], k["a"], ALU.bitwise_or)
                    dve.tensor_tensor(k["bit"], k["bit"], k["c1"], ALU.logical_shift_right).then_inc(l_found.sem, 1)
                l_found.wait(dve, 32)
                code_of(k["found"], 33)
                thr = k["code"].bitcast(F32)
                link(dve.tensor_scalar(above[:, :], wv[:, :], thr, None, ALU.is_gt, ALU.add, accum_out=cnt[:, :]))
                link(dve.tensor_scalar(level[:, :], wv[:, :], thr, None, ALU.is_equal))
                dve.sem_inc(l_step, 1)
                dve.wait_ge(l_p, 1)
                link(dve.tensor_copy(by_tile_sum[:, :], bank[1][0:NT, 0:P]))
                link(dve.tensor_scalar(need[:, :], bank[2][:, 0:1], -1.0, float(TOP), ALU.mult, ALU.add))
                dve.sem_inc(l_step, 1)
                dve.wait_ge(l_p, 2)
                link(dve.tensor_scalar(pick[:, :], bank[3][:, 0:NT], need[:, 0:1], None, ALU.is_lt))
                link(dve.tensor_tensor(pick[:, :], pick[:, :], level[:, :], ALU.mult))
                link(dve.tensor_tensor(pick[:, :], pick[:, :], above[:, :], ALU.add))
                for j in range(OUT_CHUNKS):
                    dve.wait_ge(l_in[j], 16)
                    for t in range(j * CT, (j + 1) * CT):
                        ins = dve.scalar_tensor_tensor(out=base[:, t, :], in0=acc[:, t % UT, t // UT * UN:t // UT * UN + C],
                                                       scalar=pick[:, t:t + 1], in1=base[:, t, :], op0=ALU.mult, op1=ALU.add)
                    ins.then_inc(l_done, 1)

            @block.tensor
            def _(pe):
                with pe.Fori(0, 32) as i:
                    l_cnt.wait(pe, i + 1)
                    pe.matmul(bank[0][:, 0:1], ones[:, :], cnt[:, :], start=True, stop=True).then_inc(l_sum.sem, 1)
                pe.wait_ge(l_step, 1)
                pe.matmul(bank[1][0:NT, 0:P], level[:, :], ones[:, :], start=True, stop=True)
                pe.matmul(bank[2][:, 0:1], ones[:, :], cnt[:, :], start=True, stop=True).then_inc(l_p, 1)
                pe.wait_ge(l_step, 2)
                pe.matmul(bank[3][:, 0:NT], before[:, :], level[:, :], start=True, stop=False)
                pe.matmul(bank[3][:, 0:NT], by_tile_sum[:, :], before[0:NT, 0:NT], start=False, stop=True).then_inc(l_p, 1)
        last.close()


def kernel(**inputs):
    import numpy as np
    import concourse.bacc as bacc
    from concourse.bass_utils import run_bass_kernel_spmd

    def by_tile(a, fill):
        a = np.concatenate([a, fill[:ET * P - E]], axis=0)
        return np.ascontiguousarray(np.moveaxis(a.reshape((ET, P) + a.shape[1:]), 0, 1))

    def by_partition(a):
        return np.ascontiguousarray(a.reshape(-1, P).T)

    a = {k: np.asarray(v) for k, v in inputs.items()}
    x, src, dst, attr = a["x"], a["src"], a["dst"], a["edge_attr_2"]
    wf, wr = a["L0_gnn_W_forward"], a["L0_gnn_W_reverse"]
    arrays = {
        "x": np.concatenate([x, np.zeros((NP - N, C), x.dtype)], axis=0),
        "src_t": by_tile(src, src),
        "dst_t": by_tile(dst, np.full((P,), int(PAD_NODE), dst.dtype)),
        "attr_t": by_tile(attr, attr),
        "wg": np.ascontiguousarray(np.concatenate([wf.T, wr.T], axis=1)),
        "wsum": np.stack([wf, wr]),
        "attn_t": np.ascontiguousarray(a["L0_gnn_attn_forward"][0].T),
        "wkv_d": np.concatenate([a["L0_mix_Wk"], a["L0_mix_Wv"]], axis=1),
        "wq_d": a["L0_mix_Wq"],
        "wm_d": a["L0_mix_Wm"],
        "w1_d": a["L0_mix_W1"],
        "w2_d": a["L0_mix_W2"],
        "g1_d": by_partition(a["L0_mix_g1"]),
        "b1_d": by_partition(a["L0_mix_b1"]),
        "g2_d": a["L0_mix_g2"],
        "b2_d": a["L0_mix_b2"],
        "f1_d": a["L0_ffn_w1"],
        "f2_d": a["L0_ffn_w2"],
        "fb1_d": by_partition(a["L0_ffn_b1"]),
        "fb2_d": a["L0_ffn_b2"],
        "wr_d": np.ascontiguousarray(a["L0_ffn_wr"][:, 0]),
        "br_d": a["L0_ffn_br"],
    }
    nc = bacc.Bacc("TRN2", target_bir_lowering=False, num_devices=1)
    args = {k: nc.dram_tensor(f"in_{k}", v.shape, mybir.dt.from_np(v.dtype), kind="ExternalInput").ap() for k, v in arrays.items()}
    out = nc.dram_tensor("out_0", (N, C), F32, kind="ExternalOutput").ap()
    build_program(nc, out=out, **args)
    r = run_bass_kernel_spmd(nc, [{f"in_{k}": v for k, v in arrays.items()}], core_ids=[0])
    return r.results[0]["out_0"]
```

```python
from contextlib import ExitStack

import concourse.bass as bass
from concourse import mybir

F32 = mybir.dt.float32
I32 = mybir.dt.int32
ALU = mybir.AluOpType
ACT = mybir.ActivationFunctionType
AX = mybir.AxisListType.X

P = 128
N = 6250
E = 206250
TOP = 3124
C = 256
KC = C // P
F = 64
H = 4
ROW = F + H
UT = 2
UN = UT * P
UNITS = -(-N // UN)
NP = UNITS * UN
NT = NP // P
LAST = N - (NP - UN)
ET = -(-E // P)
BT = 13
BLOCKS = ET // BT
GROUPS = [(0, 4), (4, 8), (8, 13)]
NG = len(GROUPS)
WIN = 32
WINS = NP // WIN
GR = BLOCKS * NG
GC = -(-GR // P)
PAD_NODE = 1.0e6
LN_EPS = 1e-5
SUM_EPS = 1e-10
ATT_EPS = 1e-6
SLOPE = 0.2
GAP_MAX = 30.0
SUM_TOL = 2.0 ** -23
LOW = -3.0e38
HD = 32
HID = 2 * C
FF = 4 * C
PRE = 5
SLOTS = 4
BODIES = BLOCKS // SLOTS
MIX_BODIES = 5
MIX_EACH = UNITS // MIX_BODIES
GAP_BODY = BODIES - 6
STEPS = 15
OUT_CHUNKS = 5
ROUNDS = UNITS + 2
assert BLOCKS * BT == ET and BLOCKS % SLOTS == 0 and UNITS % PRE == 0 and UNITS % MIX_BODIES == 0
assert E % P and LAST <= P and KC == 2 and UT == 2
assert UNITS % OUT_CHUNKS == 0
assert MIX_BODIES + 2 < GAP_BODY and BODIES - MIX_BODIES - 2 < UNITS


class Count:

    def __init__(self, sem, credit=0):
        self.sem, self.credit = sem, credit

    def wait(self, eng, count):
        eng.wait_ge(self.sem, count + self.credit)


class Stages:

    AHEAD = 3

    def __init__(self, sem, names, before=0):
        self.sem, self.names, self.before = sem, names.split(), before

    def open(self, eng):
        eng.sem_inc(self.sem, self.AHEAD * len(self.names))

    def wait(self, eng, name, units):
        if isinstance(units, int):
            units = min(units, UNITS)
        eng.wait_ge(self.sem, units * len(self.names) + (self.names.index(name) + 1 + (self.before + self.AHEAD - 1) * len(self.names)))


STAGES = {
    "V0": "qmin qt zr0 zr mt stat1 mv1 rstd1 z",
    "V1": "stat2 mv2 rstd2 z2 y2 y3 m1 mtop diag top lead gap guard",
    "V2": "den tol rden low gn ra x1 stat3 mv3 rstd3 xf dot base wcol yb yw",
    "A0": "qexp sd1 m2t",
    "A1": "relu sd2 gexp",
    "A2": "part sd3 xft gelu0 gelu1 gelu2 gelu3",
    "P0": "q attn proj ztr own",
    "P1": "hid y m1t mall",
    "P2": "ptr xtr ff0 ff1 ff2 ff3 out",
}


def chain_counts(sem):
    c = {name: Stages(sem(f"stages_{name}"), names) for name, names in STAGES.items()}
    for name in ("x_in", "r_in", "base_out"):
        c[name] = sem(f"c_{name}")
    return c


def once_more(c):
    return {name: Stages(q.sem, " ".join(q.names), UNITS) if isinstance(q, Stages) else q for name, q in c.items()}


def units_done(c, v):
    return v + 1, v, v - 1, c["V0"].before


def vector_round(dve, s, c, step, v, parts, seen, track):
    bank = s["bank"]
    r0, r1, r2, before = units_done(c, v)
    V0, V1, V2 = c["V0"], c["V1"], c["V2"]

    def moments(count, n, r, source):
        k = n - 1
        for t in range(UT):
            ins = dve.bn_stats(s["stats"][:, k, t, :], source(t))
        ins.then_inc(count.sem, 1)
        count.wait(dve, f"stat{n}", r)
        dve.sem_inc(s["hold_v"], 1)
        for t in range(UT):
            ins = dve.bn_aggr(s["mv"][:, k, t, :], s["stats"][:, k, t, :])
        ins.then_inc(count.sem, 1)

    def normal(count, scalar_count, n, r, dst, source):
        k = n - 1
        scalar_count.wait(dve, f"sd{n}", r)
        dve.reciprocal(s["rstd"][:, k, :], s["sd"][:, k, :]).then_inc(count.sem, 1)
        count.wait(dve, f"rstd{n}", r)
        for t in range(UT):
            ins = dve.tensor_scalar(dst[:, t * C:(t + 1) * C], source(t), s["mv"][:, k, t, 0:1], s["rstd"][:, k, t:t + 1],
                                    ALU.subtract, ALU.mult)
        ins.then_inc(count.sem, 1)

    def rows_of(tile):
        return lambda t: tile[:, t * C:(t + 1) * C]

    def by_tile(row):
        return row.rearrange("p (o c) -> p o c", o=1).to_broadcast([P, UT, C])

    if 0 in parts:
        if step == 2:
            c["P0"].wait(dve, "q", r0)
            c["P2"].wait(dve, "ptr", r2)
            dve.tensor_scalar(s["T0"], bank[3][:, :], 0.0, None, ALU.min).then_inc(V0.sem, 1)
        if step == 4:
            c["A0"].wait(dve, "qexp", r0)
            dve.scalar_tensor_tensor(out=s["T2"], in0=bank[3][:, :], scalar=0.0, in1=s["T1"], op0=ALU.max, op1=ALU.add)\
                .then_inc(V0.sem, 1)
        if step == 6:
            c["P0"].wait(dve, "attn", r0)
            c["P2"].wait(dve, "xtr", r2)
            dve.tensor_scalar(s["T0"], bank[2][:, :], ATT_EPS, None, ALU.add).then_inc(V0.sem, 1)
            V0.wait(dve, "zr0", r0)
            dve.reciprocal(s["T0"], s["T0"]).then_inc(V0.sem, 1)
            V0.wait(dve, "zr", r0)
            dve.scalar_tensor_tensor(out=s["T3"], in0=bank[4][:, :], scalar=float(N), in1=s["T0"], op0=ALU.mult, op1=ALU.mult)\
                .then_inc(V0.sem, 1)
        if step == 8:
            c["P0"].wait(dve, "proj", r0)
            moments(V0, 1, r0, rows_of(bank[3]))
        if step == 10:
            normal(V0, c["A0"], 1, r0, s["T0"], rows_of(bank[3]))
    if 1 in parts:
        if step == 3:
            c["P1"].wait(dve, "y", r1)
            moments(V1, 2, r1, rows_of(bank[7]))
        if step == 5:
            normal(V1, c["A1"], 2, r1, s["Y"], rows_of(bank[7]))
        if step == 6:
            y = s["Y"].rearrange("p (t c) -> p t c", t=UT)
            V1.wait(dve, "z2", r1)
            dve.tensor_tensor(y, y, by_tile(s["g2"]), ALU.mult).then_inc(V1.sem, 1)
            V1.wait(dve, "y2", r1)
            dve.tensor_tensor(y, y, by_tile(s["b2"]), ALU.add).then_inc(V1.sem, 1)
            s["max_seen"](dve, seen)
            dve.tensor_reduce(s["m1"], s["smax"].rearrange("p t h -> p h t"), AX, ALU.max).then_inc(V1.sem, 1)
        if step == 8:
            c["P1"].wait(dve, "m1t", r1)
            dve.tensor_reduce(s["mtop"], bank[2][0:H, 0:P], AX, ALU.max).then_inc(V1.sem, 1)
            V1.wait(dve, "mtop", r1)
            dve.tensor_scalar(s["diag"], s["ident"][0:H, 0:H], s["mtop"], None, ALU.mult).then_inc(V1.sem, 1)
        if step == 10:
            c["P1"].wait(dve, "mall", r1)
            dve.tensor_copy(s["top"], bank[2][:, UN:UN + H]).then_inc(V1.sem, 1)
            V1.wait(dve, "top", r1)
            dve.scalar_tensor_tensor(out=s["lead"], in0=s["top"], scalar=SLOPE, in1=s["top"], op0=ALU.mult, op1=ALU.max).then_inc(V1.sem, 1)
            V1.wait(dve, "lead", r1)
            dve.tensor_tensor(s["gap"], s["lead"], s["bound"], ALU.subtract).then_inc(V1.sem, 1)
        if step == 12:
            c["A1"].wait(dve, "gexp", r1)
            dve.tensor_scalar(s["guard"], s["gexp"], SUM_EPS, None, ALU.mult).then_inc(V1.sem, 1)
    if 2 in parts:
        u = v - 2
        if step == 2:
            c["P2"].wait(dve, "ptr", r2)
            V1.wait(dve, "guard", r2)
            for t in range(UT):
                ins = dve.tensor_tensor(s["den"][:, t, :], bank[5 + t][:, 2 * P:2 * P + H], s["guard"], ALU.add)
            ins.then_inc(V2.sem, 1)
            for t, n in enumerate(track):
                if n:
                    ins = dve.scalar_tensor_tensor(out=s["tol"][0:n, t, :], in0=bank[5 + t][0:n, 2 * P:2 * P + H], scalar=SUM_TOL,
                                                   in1=s["guard"][0:n, :], op0=ALU.mult, op1=ALU.add)
            ins.then_inc(V2.sem, 1)
            V2.wait(dve, "den", r2)
            dve.reciprocal(s["rden"], s["den"]).then_inc(V2.sem, 1)
            V2.wait(dve, "rden", r2)
            for t, n in enumerate(track):
                if n:
                    low = s["low"][0:n, t, :]
                    ins = dve.tensor_tensor(low, low, s["tol"][0:n, t, :], ALU.min)
            ins.then_inc(V2.sem, 1)
            for t in range(UT):
                ins = dve.tensor_tensor(s["T2"][:, t * C:(t + 1) * C].rearrange("p (b a f) -> p b a f", b=2, a=2),
                                        bank[5 + t][:, 0:2 * P].rearrange("p (a b f) -> p b a f", a=2, b=2),
                                        s["rden"][:, t, :].rearrange("p (b a o) -> p b a o", b=2, o=1).to_broadcast([P, 2, 2, F]),
                                        ALU.mult)
            ins.then_inc(V2.sem, 1)
            dve.wait_ge(c["r_in"], (r2 + before) * 16)
            dve.tensor_tensor(s["T5"], s["T5"], s["Y"], ALU.add).then_inc(V2.sem, 1)
            V2.wait(dve, "ra", r2)
            dve.tensor_tensor(s["T5"], s["T5"], s["T2"], ALU.add).then_inc(V2.sem, 1)
            V2.wait(dve, "x1", r2)
            moments(V2, 3, r2, rows_of(s["T5"]))
        if step == 4:
            c["A0"].wait(dve, "qexp", r0)
            normal(V2, c["A2"], 3, r2, s["T0"], rows_of(s["T5"]))
            V2.wait(dve, "xf", r2)
            for t in range(UT):
                rows = slice(t * C, (t + 1) * C)
                ins = dve.tensor_tensor_reduce(s["T3"][:, rows], s["T0"][:, rows], s["wr"], 1.0, 0.0, ALU.mult, ALU.add,
                                               s["dot"][:, t:t + 1])
            ins.then_inc(V2.sem, 1)
            dve.wait_ge(c["base_out"], (r2 + before) * 16)
            dve.tensor_tensor(s["base"], s["T5"], s["T0"], ALU.add).then_inc(V2.sem, 1)
            V2.wait(dve, "dot", r2)
            dve.tensor_scalar(s["wcol"], s["dot"], s["br"], None, ALU.add).then_inc(V2.sem, 1)
        if step == 14:
            V2.wait(dve, "wcol", r2)
            dve.tensor_copy(s["w_all"][:, bass.ds(u * UT, UT)], s["wcol"])
            c["P2"].wait(dve, "out", r2)
            t2 = s["T2"].rearrange("p (t c) -> p t c", t=UT)
            dve.tensor_tensor(t2, bank[5][:, :].rearrange("p (t c) -> p t c", t=UT), by_tile(s["fb2"]), ALU.add).then_inc(V2.sem, 1)
            V2.wait(dve, "yb", r2)
            for t in range(UT):
                ins = dve.tensor_scalar(s["acc"][:, t, bass.ds(u * UN, C)], s["T2"][:, t * C:(t + 1) * C], s["wcol"][:, t:t + 1],
                                        None, ALU.mult)
            ins.then_inc(V2.sem, 1)


def scalar_round(act, s, c, step, v, parts, merges):
    bank = s["bank"]
    r0, r1, r2, before = units_done(c, v)
    A0, A1, A2 = c["A0"], c["A1"], c["A2"]

    def deviation(vector_count, count, n, r):
        vector_count.wait(act, f"mv{n}", r)
        act.activation(s["sd"][:, n - 1, :], s["mv"][:, n - 1, :, 1], ACT.Sqrt, bias=s["eps"]).then_inc(count.sem, 1)

    if isinstance(v, int) and v == 0 and step == 0:
        act.dma_start(s["T4"], s["xnt_d"][:, :, 0:UN]).then_inc(c["x_in"], 16)
    if step == 12 and (not isinstance(v, int) or v + 1 < UNITS):
        c["P0"].wait(act, "own", r0)
        act.dma_start(s["T4"], s["xnt_d"][:, :, bass.ds((v + 1) * UN, UN)]).then_inc(c["x_in"], 16)
    if 0 in parts and step == 3:
        c["V0"].wait(act, "qmin", r0)
        act.activation(s["T1"], s["T0"], ACT.Exp).then_inc(A0.sem, 1)
    if 2 in parts:
        u = v - 2
        if step == 0:
            merges(act)
            c["P0"].wait(act, "ztr", r0 - 1)
            act.activation(s["T3"].rearrange("p (a n) -> p a n", a=2), s["acc"][:, :, bass.ds(u * UN, UN)], ACT.Copy)
            act.activation(s["part_w"], s["acc_w"][:, bass.ds(u * UN, UN)], ACT.Copy).then_inc(A2.sem, 1)
        if step == 3:
            deviation(c["V2"], A2, 3, r2)
        if step == 5:
            c["V2"].wait(act, "base", r2)
            act.dma_start(s["base_d"][bass.ds(u * UN, UN), :].rearrange("(t p) c -> p t c", p=P),
                          s["base"].rearrange("p (t c) -> p t c", t=UT)).then_inc(c["base_out"], 16)
        if step == 6:
            c["P2"].wait(act, "xtr", r2)
            c["V0"].wait(act, "qt", r0)
            act.activation(s["T1"], bank[5][:, :], ACT.Copy).then_inc(A2.sem, 1)
        if step in (8, 10):
            for f in ((0, 1) if step == 8 else (2, 3)):
                c["P2"].wait(act, f"ff{f}", r2)
                for m in range(2):
                    j = 2 * f + m
                    ins = act.activation(s["hidden"][:, j * UN:(j + 1) * UN], bank[6 + f % 2][:, m * UN:(m + 1) * UN],
                                         ACT.Gelu_apprx_tanh, bias=s["fb1"][:, j:j + 1])
                ins.then_inc(A2.sem, 1)
    if 1 in parts:
        if step == 1:
            c["P1"].wait(act, "hid", r1)
            c["P2"].wait(act, "out", r2 - 1)
            for f, b in enumerate((2, 4)):
                ins = act.activation(s["hidden"][:, 2 * f * UN:(2 * f + 2) * UN], bank[b][:, :], ACT.Relu)
            ins.then_inc(A1.sem, 1)
        if step == 4:
            deviation(c["V1"], A1, 2, r1)
        if step == 11:
            c["V1"].wait(act, "gap", r1)
            act.activation(s["gexp"], s["gap"], ACT.Exp).then_inc(A1.sem, 1)
        if step == 13:
            c["V2"].wait(act, "base", r2)
            act.dma_start(s["T5"].rearrange("p (t c) -> p t c", t=UT),
                          s["resid_d"][bass.ds((v - 1) * UN, UN), :].rearrange("(t p) c -> p t c", p=P)).then_inc(c["r_in"], 16)
    if 0 in parts:
        if step == 9:
            deviation(c["V0"], A0, 1, r0)
        if step == 12:
            c["P0"].wait(act, "ztr", r0)
            c["P2"].wait(act, "ff3", r2)
            for k in range(KC):
                ins = act.activation(s["T1"][:, k * UN:(k + 1) * UN], bank[3][:, k * UN:(k + 1) * UN], ACT.Identity,
                                     bias=s["b1"][:, k:k + 1], scale=s["g1"][:, k:k + 1])
            ins.then_inc(A0.sem, 1)


def tensor_round(pe, s, c, step, v, parts):
    bank, ident = s["bank"], s["ident"]
    r0, r1, r2, before = units_done(c, v)
    P0, P1, P2 = c["P0"], c["P1"], c["P2"]

    def turned(dst, tile):
        for t in range(UT):
            for k in range(KC):
                ins = pe.transpose(dst[:, k * UN + t * P:k * UN + (t + 1) * P], tile[:, t * C + k * P:t * C + (k + 1) * P], ident)
        return ins

    def by_row(dst, halves, weights, n, tiles=range(UT)):
        for t in tiles:
            for k in range(n):
                ins = pe.matmul(dst[:, t * C:(t + 1) * C], halves[:, k * UN + t * P:k * UN + (t + 1) * P], weights[:, k, :],
                                start=(k == 0), stop=(k == n - 1))
        return ins

    def hidden_half(f, ks):
        for m in (2 * f, 2 * f + 1):
            for k in ks:
                rhs = s["T4"][:, k, :] if k < KC else s["T1"][:, (k - KC) * UN:(k - KC + 1) * UN]
                ins = pe.matmul(bank[(2, 4)[f]][:, (m % 2) * UN:(m % 2 + 1) * UN], s["w1"][:, k, m * P:(m + 1) * P], rhs,
                                start=(k == 0 and m % 2 == 0), stop=(k == 2 * KC - 1 and m % 2 == 1))
        return ins

    if 2 in parts:
        if step == 1:
            c["A2"].wait(pe, "part", r2)
            c["V2"].wait(pe, "yb", r2 - 1)
            for t in range(UT):
                for a in range(2):
                    pe.transpose(bank[5 + t][:, a * P:(a + 1) * P], s["T3"][:, a * UN + t * P:a * UN + (t + 1) * P], ident)
                ins = pe.transpose(bank[5 + t][:, 2 * P:2 * P + H], s["part_w"][:, t * P:(t + 1) * P], ident[0:H, 0:H])
            ins.then_inc(P2.sem, 1)
        if step == 5:
            c["V2"].wait(pe, "xf", r2)
            turned(bank[5], s["T0"]).then_inc(P2.sem, 1)
        if step in (7, 9):
            c["A2"].wait(pe, "xft", r2)
            for f in ((0, 1) if step == 7 else (2, 3)):
                if f == 1:
                    c["V1"].wait(pe, "z2", r1)
                if f >= 2:
                    c["A2"].wait(pe, f"gelu{f - 2}", r2)
                for m in range(2):
                    j = 2 * f + m
                    for k in range(KC):
                        ins = pe.matmul(bank[6 + f % 2][:, m * UN:(m + 1) * UN], s["f1"][:, k, j * P:(j + 1) * P],
                                        s["T1"][:, k * UN:(k + 1) * UN], start=(k == 0), stop=(k == KC - 1))
                ins.then_inc(P2.sem, 1)
        if step == 11:
            c["A2"].wait(pe, "gelu3", r2)
            by_row(bank[5], s["hidden"], s["f2"], FF // P, (0,))
        if step == 12:
            by_row(bank[5], s["hidden"], s["f2"], FF // P, (1,)).then_inc(P2.sem, 1)
    if 1 in parts:
        if step == 0:
            c["A0"].wait(pe, "m2t", r1)
            hidden_half(0, (2, 3))
            hidden_half(1, (2, 3)).then_inc(P1.sem, 1)
        if step == 2:
            c["A1"].wait(pe, "relu", r1)
            by_row(bank[7], s["hidden"], s["w2"], HID // P).then_inc(P1.sem, 1)
        if step == 7:
            c["V1"].wait(pe, "m1", r1)
            c["V0"].wait(pe, "mt", r0)
            pe.transpose(bank[2][0:H, 0:P], s["m1"], ident).then_inc(P1.sem, 1)
        if step == 9:
            c["V1"].wait(pe, "diag", r1)
            pe.matmul(bank[2][:, UN:UN + H], s["ones"][0:H, :], s["diag"], start=True, stop=True).then_inc(P1.sem, 1)
    if 0 in parts:
        if step == 1:
            pe.wait_ge(c["x_in"], (r0 + before) * 16)
            for j in range(KC):
                for k in range(KC):
                    ins = pe.matmul(bank[3][:, j * UN:(j + 1) * UN], s["wq"][:, k, j * P:(j + 1) * P], s["T4"][:, k, :],
                                    start=(k == 0), stop=(k == KC - 1))
            ins.then_inc(P0.sem, 1)
        if step == 5:
            c["V0"].wait(pe, "qt", r0)
            c["A1"].wait(pe, "relu", r1)
            for b, w in ((2, s["ksum"]), (4, s["kv"])):
                for j in range(KC):
                    ins = pe.matmul(bank[b][:, j * UN:(j + 1) * UN], w[:, j, :], s["T2"][:, j * UN:(j + 1) * UN], start=True, stop=True)
            ins.then_inc(P0.sem, 1)
        if step == 7:
            c["V0"].wait(pe, "mt", r0)
            by_row(bank[3], s["T3"], s["wm"], KC).then_inc(P0.sem, 1)
        if step == 8:
            hidden_half(1, (0, 1))
        if step == 11:
            c["V0"].wait(pe, "z", r0)
            c["V1"].wait(pe, "top", r1)
            turned(bank[3], s["T0"]).then_inc(P0.sem, 1)
            hidden_half(0, (0, 1)).then_inc(P0.sem, 1)


def parts_of(v):
    return tuple(k for k in range(3) if 0 <= v - k < UNITS) if isinstance(v, int) else (0, 1, 2)


def body_slots(steps):
    n = 3 * SLOTS
    return [range(q * steps // n, (q + 1) * steps // n) for q in range(n)]


def build_program(nc, x, src_t, dst_t, attr_t, wg, wsum, attn_t, wkv_d, wq_d, wm_d, w1_d, w2_d, g1_d, b1_d, g2_d, b2_d,
                  f1_d, f2_d, fb1_d, fb2_d, wr_d, br_d, out):
    with ExitStack() as ctx:
        def sb(name, shape, dt=F32, where=ctx):
            return where.enter_context(nc.sbuf_tensor(name, shape, dt))

        def sem(name):
            return ctx.enter_context(nc.semaphore(name))

        def count(name, credit=0):
            return Count(sem(name), credit)

        table_d = nc.dram_tensor("table_d", (NP, 2 * ROW), F32, kind="Internal").ap()
        xnt_d = nc.dram_tensor("xnt_d", (P, KC, NP), F32, kind="Internal").ap()
        resid_d = nc.dram_tensor("resid_d", (NP, C), F32, kind="Internal").ap()
        base_d = nc.dram_tensor("base_d", (NP, C), F32, kind="Internal").ap()
        first_d = nc.dram_tensor("first_d", (GC * P,), F32, kind="Internal").ap()

        bank = [ctx.enter_context(nc.psum_tensor(f"bank{i}", [P, 512], F32)) for i in range(8)]

        ident = sb("ident", [P, P])
        ones = sb("ones", [P, P])
        iota_i = sb("iota_i", [P, WIN], I32)
        iota = sb("iota", [P, WIN])
        eps_col = sb("eps_col", [P, 1])
        valid = sb("valid", [P, NT])

        wq = sb("wq", [P, KC, C])
        wm = sb("wm", [P, KC, C])
        w1 = sb("w1", [P, 2 * KC, HID])
        w2 = sb("w2", [P, HID // P, C])
        f1 = sb("f1", [P, KC, FF])
        wkv = f1[:, :, 0:2 * C]
        f2 = sb("f2", [P, FF // P, C])
        g1 = sb("g1", [P, KC])
        b1 = sb("b1", [P, KC])
        fb1 = sb("fb1", [P, FF // P])
        g2 = sb("g2", [P, C])
        b2 = sb("b2", [P, C])
        fb2 = sb("fb2", [P, C])
        wr = sb("wr", [P, C])
        br = sb("br", [P, 1])

        dst_rel = sb("dst_rel", [P, ET])
        first_i = sb("first_i", [1, GC * P], I32)
        bound = sb("bound", [P, H])
        smax = sb("smax", [P, BT, H])
        acc = sb("acc", [P, 2, NP])
        acc_w = sb("acc_w", [H, NP])
        w_all = sb("w_all", [P, NT])
        low = sb("low", [P, UT, H])
        kv = sb("kv", [P, KC, P])
        ksum = sb("ksum", [P, KC, P])
        verdict = sb("verdict", [P, 4])
        flag_i = sb("flag_i", [P, 1], I32)
        v4 = sb("v4", [4, 1])
        vd = sb("vd", [4, 4])
        vb = sb("vb", [P, 4])
        v_one = sb("v_one", [P, 1])
        small = {n: sb(n, [P, H]) for n in ("m1", "top", "lead", "gap", "gexp", "guard")}
        mtop = sb("mtop", [H, 1])
        diag = sb("diag", [H, H])
        stats_u = sb("stats_u", [P, 3, UT, 6])
        mv_u = sb("mv_u", [P, 3, UT, 2])
        sd_u = sb("sd_u", [P, 3, UT])
        rstd_u = sb("rstd_u", [P, 3, UT])
        den = sb("den", [P, UT, H])
        rden = sb("rden", [P, UT, H])
        tol = sb("tol", [P, UT, H])
        dot = sb("dot", [P, UT])
        wcol = sb("wcol", [P, UT])

        s_const = sem("s_const")
        s_zero = sem("s_zero")
        s_dv = sem("s_dv")
        s_ask = sem("s_ask")
        s_given = sem("s_given")
        hold_v = sem("hold_v"); hold_p = sem("hold_p"); hold_s = sem("hold_s"); hold_a = sem("hold_a"); hold_t = sem("hold_t")
        s_w = {k: sem(f"s_w_{k}") for k in ("wg", "wsum", "attn", "dst", "attr", "mix", "chain", "ff")}
        dve_links = [0]

        def linker(dve):
            def link(ins):
                dve_links[0] += 1
                ins.then_inc(s_dv, 1)
                dve.wait_ge(s_dv, dve_links[0])
            return link

        asked = [0]

        edge = ExitStack()
        idx = [sb(f"idx{k}", [P, BT], I32, edge) for k in range(SLOTS)]
        att = [sb(f"att{k}", [P, BT, 2], F32, edge) for k in range(SLOTS)]
        got = [sb(f"got{k}", [P, BT, 2, ROW], F32, edge) for k in range(SLOTS)]
        T4 = sb("T4", [P, KC, UN], F32, edge)
        T5 = sb("T5", [P, UT * C], F32, edge)
        Y = sb("Y", [P, UT * C], F32, edge)
        base_u = sb("base_u", [P, UT * C], F32, edge)
        kv_sum = Y[:, 0:KC * (P + 1)].rearrange("p (k n) -> p k n", k=KC)
        heads = T5[:, 0:P]
        limit_i = base_u[:, 0:(BODIES + 1) * SLOTS * NG].bitcast(I32)
        early = (GAP_BODY + 1) * SLOTS * NG
        lrelu = sb("lrelu", [P, BT, H], F32, edge)
        score = sb("score", [P, 2, BT, H], F32, edge)
        wgt = sb("wgt", [P, 2, BT, H], F32, edge)

        pre = ExitStack()
        x_u = sb("x_u", [P, PRE, UT, C], F32, pre)
        xn = sb("xn", [P, PRE, UT, C], F32, pre)
        xnt = sb("xnt", [P, PRE, KC, UN], F32, pre)
        rows = sb("rows", [P, PRE, UT, 2, ROW], F32, pre)
        stats = sb("stats", [P, PRE, UT, 6], F32, pre)
        mv = sb("mv", [P, PRE, UT, 2], F32, pre)
        sd = sb("sd", [P, PRE, UT], F32, pre)
        rstd = sb("rstd", [P, PRE, UT], F32, pre)
        pre.close()
        work = ExitStack()
        msg = sb("msg", [P, 2, BT, ROW], F32, work)
        onehot = sb("onehot", [P, 2, BT, WIN], F32, work)
        woh = sb("woh", [P, 2, BT, H, WIN], F32, work)
        T0 = sb("T0", [P, UT * C], F32, work)
        T1 = sb("T1", [P, UT * C], F32, work)
        T2 = sb("T2", [P, UT * C], F32, work)
        T3 = sb("T3", [P, UT * C], F32, work)
        hidden = sb("hidden", [P, FF // P * UN], F32, work)
        after = ExitStack()

        flat = acc[:, :, :].rearrange("p a n -> p (a n)")
        at = [0]

        def piece(n):
            at[0] += n
            return flat[:, at[0] - n:at[0]]

        dst_i = piece(ET).bitcast(I32)
        dst_f = piece(ET)
        attr = piece(2 * ET).rearrange("p (t d) -> p t d", d=2)
        first_bc = piece(GC * P)
        gmin = piece(GC * P)
        gmax = piece(GC * P)
        wg_s = piece(KC * 2 * ROW).rearrange("p (k d r) -> p k d r", k=KC, d=2)
        wsum_s = piece(2 * C).rearrange("p (d c) -> p d c", d=2)[0:F]
        attn_s = piece(H)[0:F]
        p_all = piece(NT * 2 * H).rearrange("p (t d h) -> p t d h", d=2, h=H)
        p_lo = piece(NT * 2 * H).rearrange("p (t d h) -> p t d h", d=2, h=H)
        ext = piece(4)
        ext_bc = piece(4)
        bcol = piece(GC)
        mcol = piece(GC)
        limit = piece((BODIES + 1) * SLOTS * NG)
        assert at[0] <= 2 * NP

        c_stats = count("c_stats"); c_mv = count("c_mv"); c_sd = count("c_sd"); c_rstd = count("c_rstd")
        c_xn = count("c_xn"); c_res = count("c_res")
        c_tr = count("c_tr"); c_xnt = count("c_xnt"); c_tab = count("c_tab"); c_rows = count("c_rows")
        c_rows_p = count("c_rows_p")
        s_x = [sem(f"s_x{j}") for j in range(PRE)]
        s_rows_out = [sem(f"s_rows_out{j}") for j in range(PRE)]
        s_xnt_out = [sem(f"s_xnt_out{j}") for j in range(PRE)]
        s_res_out = [sem(f"s_res_out{j}") for j in range(PRE)]
        s_score_w = sem("s_score_w"); s_score_c = sem("s_score_c")
        s_first_out = sem("s_first_out"); s_first_in = sem("s_first_in")
        s_first = sem("s_first")
        s_kv = sem("s_kv")
        s_begin = sem("s_begin")

        s_idx = [sem(f"s_idx{k}") for k in range(SLOTS)]
        s_att = [sem(f"s_att{k}") for k in range(SLOTS)]
        s_got = [sem(f"s_got{k}") for k in range(SLOTS)]
        e_prod = count("e_prod"); e_msg = count("e_msg", SLOTS)
        e_lrelu = count("e_lrelu"); e_score = count("e_score"); e_max = count("e_max")
        e_wgt = count("e_wgt", 2); e_onehot = count("e_onehot"); e_woh = count("e_woh")
        e_scat = count("e_scat", 2)
        e_grp = count("e_grp"); e_merge = count("e_merge", NG + 1); e_acc = count("e_acc")
        m_x = sem("m_x")
        m_proj = count("m_proj"); m_min = count("m_min"); m_exp = count("m_exp"); m_v = count("m_v")
        m_k = count("m_k"); m_kv = count("m_kv"); m_sum = count("m_sum", 1)
        c = chain_counts(sem)

        def max_seen(dve, seen):
            e_max.wait(dve, seen)

        s = dict(bank=bank, ident=ident[:, :], ones=ones[:, :], smax=smax[:, :, :], acc=acc, acc_w=acc_w, w_all=w_all,
                 T0=T0[:, :], T1=T1[:, :], T2=T2[:, :], T3=T3[:, :], T4=T4[:, :, :], T5=T5[:, :], Y=Y[:, :], base=base_u[:, :], hidden=hidden[:, :],
                 part_w=T0[0:H, 0:UN], mtop=mtop[:, :], diag=diag[:, :], bound=bound[:, :], stats=stats_u, mv=mv_u,
                 sd=sd_u, rstd=rstd_u, den=den[:, :, :], rden=rden[:, :, :], tol=tol, low=low, dot=dot[:, :],
                 wcol=wcol[:, :], g1=g1, b1=b1, g2=g2[:, :], b2=b2[:, :], fb1=fb1, fb2=fb2[:, :], wr=wr[:, :], br=br[:, 0:1],
                 eps=eps_col[:, 0:1], wq=wq, wm=wm, w1=w1, w2=w2, f1=f1, f2=f2, kv=kv, ksum=ksum, xnt_d=xnt_d,
                 resid_d=resid_d, base_d=base_d, hold_v=hold_v, max_seen=max_seen,
                 **{n: t[:, :] for n, t in small.items()})
        s_full = (P, P)
        s_last = (LAST, 0)

        def edge_bodies(eng, block_part, mix_part, chain_part):
            def body(i, kind, v=None):
                steps = {"mix": 3 * MIX_EACH, "chain": STEPS, "plain": 0}[kind]
                for q, todo in enumerate(body_slots(steps)):
                    k = q // 3
                    block_part(eng, q % 3, i, k)
                    for step in todo:
                        if kind == "mix":
                            mix_part(eng, step % 3, i * MIX_EACH + step // 3)
                        else:
                            chain_part(eng, step, v, parts_of(v), i * SLOTS + k + 1, i * (SLOTS * NG) - NG)

            body(0, "mix")
            with eng.Fori(1, MIX_BODIES) as i:
                body(i, "mix")
            mix_part(eng, 3, None)
            body(MIX_BODIES, "chain", 0)
            body(MIX_BODIES + 1, "chain", 1)
            with eng.Fori(MIX_BODIES + 2, GAP_BODY) as i:
                body(i, "chain", i - MIX_BODIES)
            body(GAP_BODY, "plain")
            with eng.Fori(GAP_BODY + 1, BODIES - 1) as i:
                body(i, "chain", i - MIX_BODIES - 1)
            body(BODIES - 1, "chain", BODIES - MIX_BODIES - 2)
            block_part(eng, 3, None, None)
            for v in range(BODIES - MIX_BODIES - 1, ROUNDS):
                for step in range(STEPS):
                    chain_part(eng, step, v, parts_of(v), BLOCKS, GR)

        def nothing(eng, *rest):
            pass

        with nc.Block() as block:
            @block.sync
            def _(sp):
                for j in range(PRE):
                    for q in (s_xnt_out[j], s_res_out[j], s_rows_out[j]):
                        sp.sem_inc(q, 16)
                sp.sem_inc(c["base_out"], 16)

                def load_x(u, j):
                    sp.dma_start(x_u[:, j, :, :], x[bass.ds(u * UN, UN), :].rearrange("(t p) c -> p t c", p=P)).then_inc(s_x[j], 16)

                sp.dma_start(wsum_s, wsum.rearrange("d f c -> f d c")).then_inc(s_w["wsum"], 16)
                sp.dma_start(attn_s, attn_t).then_inc(s_w["attn"], 16)
                for d in range(2):
                    sp.dma_start(wg_s[:, :, d, 0:F], wg[:, d * F:(d + 1) * F].rearrange("(k p) f -> p k f", p=P)).then_inc(s_w["wg"], 16)
                for j in range(PRE):
                    load_x(j, j)

                def keep(i, j):
                    u = i * PRE + j
                    c_rows.wait(sp, u + 1)
                    sp.sem_inc(hold_s, 1)
                    sp.dma_start(table_d[bass.ds(u * UN, UN), :].rearrange("(t p) r -> p t r", p=P),
                                 rows[:, j, :, :, :].rearrange("p t d r -> p t (d r)")).then_inc(s_rows_out[j], 16)
                    c_xnt.wait(sp, u + 1)
                    sp.sem_inc(hold_s, 1)
                    sp.dma_start(xnt_d[:, :, bass.ds(u * UN, UN)], xnt[:, j, :, :]).then_inc(s_xnt_out[j], 16)
                    c_res.wait(sp, u + 1)
                    sp.sem_inc(hold_s, 1)
                    sp.dma_start(resid_d[bass.ds(u * UN, UN), :].rearrange("(t p) c -> p t c", p=P), x_u[:, j, :, :])\
                        .then_inc(s_res_out[j], 16)

                with sp.Fori(0, UNITS // PRE - 1) as i:
                    for j in range(PRE + 2):
                        if j < PRE:
                            keep(i, j)
                        if j >= 2:
                            sp.wait_ge(s_res_out[j - 2], (i + 2) * 16)
                            sp.sem_inc(hold_s, 1)
                            load_x((i + 1) * PRE + j - 2, j - 2)
                for j in range(PRE):
                    keep(UNITS // PRE - 1, j)
                for dst, src, q in ((wkv, wkv_d, "mix"), (wq, wq_d, "mix"), (wm, wm_d, "chain"), (w1, w1_d, "chain"),
                                    (w2, w2_d, "chain"), (f2, f2_d, "ff")):
                    sp.dma_start(dst if dst is wkv else dst[:, :, :], src.rearrange("(k p) c -> p k c", p=P)).then_inc(s_w[q], 16)
                for dst, src in ((g1, g1_d), (b1, b1_d), (fb1, fb1_d)):
                    sp.dma_start(dst[:, :], src).then_inc(s_w["chain"], 16)
                for dst, src in ((g2, g2_d), (b2, b2_d), (fb2, fb2_d), (wr, wr_d), (br, br_d)):
                    sp.dma_start(dst[:, :], src.rearrange("(a n) -> a n", a=1).to_broadcast([P, src.shape[0]])).then_inc(s_w["chain"], 16)

                def part(eng, third, i, k):
                    if third == 0:
                        b = i * SLOTS + k
                        e_msg.wait(sp, b - SLOTS + 1)
                        sp.sem_inc(hold_s, 1)
                        sp.dma_start(idx[k][:, :], src_t[:, bass.ds(b * BT, BT)]).then_inc(s_idx[k], 16)
                        sp.dma_start(att[k][:, :, :], attr_t[:, bass.ds(b * BT, BT), :]).then_inc(s_att[k], 16)

                edge_bodies(sp, part, nothing, nothing)
                sp.wait_ge(c["base_out"], 16 * (UNITS + 1))
                for q, n in (("mix", 2), ("chain", 11), ("ff", 2)):
                    sp.wait_ge(s_w[q], 16 * n)

            @block.gpsimd
            def _(pool):
                pool.dma_start(dst_i, dst_t).then_inc(s_w["dst"], 16)
                pool.dma_start(attr, attr_t).then_inc(s_w["attr"], 16)
                pool.memset(ident[:, :], 0.0).then_inc(s_const, 1)
                pool.memset(ones[:, :], 1.0).then_inc(s_const, 1)
                pool.memset(eps_col[:, :], LN_EPS).then_inc(s_const, 1)
                pool.iota(iota_i[:, :], pattern=[[1, WIN]], base=0, channel_multiplier=0).then_inc(s_const, 1)
                pool.memset(valid[:, :], 1.0).then_inc(s_const, 1)
                pool.memset(heads, 0.0).then_inc(s_const, 1)
                for part, first, n, done in ((limit_i[:, 0:early], 0, GAP_BODY + 1, -MIX_BODIES - 1),
                                             (limit_i[:, early:], GAP_BODY + 1, BODIES - GAP_BODY, -MIX_BODIES - 2)):
                    pool.iota(part.rearrange("p (b g) -> p b g", g=SLOTS * NG), pattern=[[UN, n], [0, SLOTS * NG]],
                              base=UN * (first + done), channel_multiplier=0).then_inc(s_const, 1)
                pool.wait_ge(s_const, 8)
                pool.affine_select(out=ident[:, :], in_=ident[:, :], compare_op=ALU.not_equal, fill=1.0, base=0,
                                   pattern=[[-1, P]], channel_multiplier=1).then_inc(s_const, 1)
                pool.affine_select(out=valid[:, :], in_=valid[:, :], compare_op=ALU.is_gt, fill=0.0, base=N,
                                   pattern=[[-P, NT]], channel_multiplier=-1).then_inc(s_const, 1)
                pool.wait_ge(s_const, 10)
                for g in range(P // HD):
                    pool.memset(heads[g * HD:(g + 1) * HD, g * HD:(g + 1) * HD], 1.0).then_inc(s_const, 1)
                pool.wait_ge(s_const, 14)
                pool.memset(acc_w[:, :], 0.0).then_inc(s_zero, 1)
                pool.memset(smax[:, :, :], LOW).then_inc(s_zero, 1)
                pool.memset(low[:, :, :], 1.0e30).then_inc(s_zero, 1)
                pool.memset(kv_sum, 0.0).then_inc(s_zero, 1)
                for j in range(PRE):
                    pool.wait_ge(s_rows_out[j], 16 * (UNITS // PRE + 1))

                def part(eng, third, i, k):
                    if third == 0:
                        b = i * SLOTS + k
                        pool.wait_ge(s_idx[k], (i + 1) * 16)
                        pool.sem_inc(hold_p, 1)
                        e_msg.wait(pool, b - SLOTS + 1)
                        pool.sem_inc(hold_p, 1)
                        for t in range(BT):
                            pool.indirect_dma_start(got[k][:, t, :, :].rearrange("p d r -> p (d r)"), None, table_d,
                                                    bass.IndirectOffsetOnAxis(ap=idx[k][:, t:t + 1], axis=0)).then_inc(s_got[k], 16)
                edge_bodies(pool, part, nothing, nothing)

            @block.vector
            def _(dve):
                link = linker(dve)
                dve.sem_inc(e_msg.sem, SLOTS)
                dve.sem_inc(e_merge.sem, NG + 1)
                dve.sem_inc(m_sum.sem, 1)
                for k in range(3):
                    c[f"V{k}"].open(dve)
                dve.wait_ge(s_w["wg"], 32)
                dve.wait_ge(s_score_w, 1)
                dve.tensor_copy(wg_s[:, :, :, F:ROW], bank[7][:, 0:KC * 2 * H].rearrange("p (k d h) -> p k d h", k=KC, d=2))\
                    .then_inc(s_score_c, 1)
                with dve.Fori(0, UNITS // PRE) as i:
                    for j in range(PRE + 2):
                        if j < PRE:
                            u = i * PRE + j
                            dve.wait_ge(s_x[j], (i + 1) * 16)
                            for t in range(UT):
                                ins = dve.bn_stats(stats[:, j, t, :], x_u[:, j, t, :])
                            ins.then_inc(c_stats.sem, 1)
                            c_stats.wait(dve, u + 1)
                            dve.sem_inc(hold_v, 1)
                            for t in range(UT):
                                ins = dve.bn_aggr(mv[:, j, t, :], stats[:, j, t, :])
                            ins.then_inc(c_mv.sem, 1)
                        if 1 <= j <= PRE:
                            n = j - 1
                            u = i * PRE + n
                            c_sd.wait(dve, u + 1)
                            dve.reciprocal(rstd[:, n, :], sd[:, n, :]).then_inc(c_rstd.sem, 1)
                            c_rstd.wait(dve, u + 1)
                            for t in range(UT):
                                ins = dve.tensor_scalar(xn[:, n, t, :], x_u[:, n, t, :], mv[:, n, t, 0:1], rstd[:, n, t:t + 1],
                                                        ALU.subtract, ALU.mult)
                            ins.then_inc(c_xn.sem, 1)
                            c_xn.wait(dve, u + 1)
                            dve.tensor_tensor(x_u[:, n, :, :], x_u[:, n, :, :], xn[:, n, :, :], ALU.add).then_inc(c_res.sem, 1)
                        if j >= 2:
                            n = j - 2
                            u = i * PRE + n
                            c_rows.wait(dve, u + 1)
                            dve.tensor_copy(p_all[:, bass.ds(u * UT, UT), :, :], rows[:, n, :, :, F:ROW]).then_inc(c_rows_p.sem, 1)
                dve.wait_ge(s_w["dst"], 16)
                link(dve.tensor_copy(dst_f, dst_i))
                link(dve.memset(gmin, PAD_NODE))
                link(dve.memset(gmax, 0.0))
                db = dst_f.rearrange("p (b t) -> p b t", t=BT)
                gv = gmin[:, 0:GR].rearrange("p (b g) -> p b g", g=NG)
                xv = gmax[:, 0:GR].rearrange("p (b g) -> p b g", g=NG)
                for g, (a, z) in enumerate(GROUPS):
                    link(dve.tensor_reduce(gv[:, :, g], db[:, :, a:z], AX, ALU.min))
                link(dve.tensor_scalar(dst_rel[:, :], dst_f, 0.5 * PAD_NODE, None, ALU.is_lt))
                link(dve.tensor_tensor(dst_rel[:, :], dst_rel[:, :], dst_f, ALU.mult))
                dr = dst_rel[:, :].rearrange("p (b t) -> p b t", t=BT)
                for g, (a, z) in enumerate(GROUPS):
                    link(dve.tensor_reduce(xv[:, :, g], dr[:, :, a:z], AX, ALU.max))
                dve.sem_inc(s_ask, 1)
                dve.wait_ge(s_given, 1)
                for k in range(GC):
                    link(dve.tensor_reduce(bcol[:, k:k + 1], bank[0][:, k * P:(k + 1) * P], AX, ALU.min))
                    link(dve.tensor_reduce(mcol[:, k:k + 1], bank[1][:, k * P:(k + 1) * P], AX, ALU.max))
                link(dve.tensor_scalar(bcol, bcol, float(NP - WIN), None, ALU.min))
                link(dve.tensor_tensor(mcol, mcol, bcol, ALU.subtract))
                link(dve.tensor_reduce(verdict[:, 0:1], mcol, AX, ALU.max))
                link(dve.tensor_scalar(verdict[:, 0:1], verdict[:, 0:1], WIN - 0.5, None, ALU.subtract))
                dve.sem_inc(s_ask, 1)
                dve.wait_ge(s_given, 2)
                link(dve.tensor_copy(gmin[0:GC, 0:P], bank[2][0:GC, 0:P]))
                dve.sem_inc(s_first, 1)

                def spread(ready, dst):
                    asked[0] += 1
                    dve.wait_ge(s_given, 1 + 2 * asked[0])
                    link(dve.tensor_reduce(v4[:, :], bank[0][0:4, 0:P], AX, ALU.max))
                    link(dve.tensor_scalar(vd[:, :], ident[0:4, 0:4], v4[:, 0:1], None, ALU.mult))
                    dve.sem_inc(s_ask, 1)
                    dve.wait_ge(s_given, 2 + 2 * asked[0])
                    link(dve.tensor_copy(dst, bank[0][:, P:P + 4]))

                dve.wait_ge(s_w["attr"], 16)
                for d in range(2):
                    link(dve.tensor_reduce(ext[:, d:d + 1], attr[:, :, d], AX, ALU.max))
                    link(dve.tensor_reduce(ext[:, 2 + d:3 + d], attr[:, :, d], AX, ALU.min))
                link(dve.tensor_scalar(ext[:, 2:4], ext[:, 2:4], -1.0, None, ALU.mult))
                dve.sem_inc(s_ask, 1)
                spread(None, ext_bc)
                link(dve.tensor_scalar(ext_bc[:, 2:4], ext_bc[:, 2:4], -1.0, None, ALU.mult))
                c_rows_p.wait(dve, UNITS)
                for d in range(2):
                    link(dve.tensor_scalar(p_lo[:, :, d, :], p_all[:, :, d, :], ext_bc[:, 2 + d:3 + d], None, ALU.mult))
                    link(dve.scalar_tensor_tensor(out=p_lo[:, :, d, :], in0=p_all[:, :, d, :], scalar=ext_bc[:, d:d + 1],
                                                  in1=p_lo[:, :, d, :], op0=ALU.mult, op1=ALU.max))
                link(dve.tensor_tensor(p_lo[:, :, 0, :], p_lo[:, :, 0, :], p_lo[:, :, 1, :], ALU.add))
                link(dve.tensor_reduce(ext, p_lo[:, :, 0, :].rearrange("p t h -> p h t"), AX, ALU.max))
                dve.sem_inc(s_ask, 1)
                spread(None, ext_bc)
                link(dve.scalar_tensor_tensor(out=bound[:, :], in0=ext_bc, scalar=SLOPE, in1=ext_bc, op0=ALU.mult, op1=ALU.max))
                dve.wait_ge(s_first_in, 16)
                lim = limit[:, 0:GR]
                link(dve.tensor_copy(lim, limit_i[:, NG:GR + NG]))
                link(dve.tensor_tensor(lim, lim, first_bc[:, 0:GR], ALU.subtract))
                link(dve.tensor_reduce(verdict[:, 1:2], lim, AX, ALU.max))
                link(dve.tensor_scalar(lim, lim, 0.0, None, ALU.max))
                link(dve.tensor_tensor(first_bc[:, 0:GR], first_bc[:, 0:GR], lim, ALU.add))
                bb = first_bc[:, 0:GR].rearrange("p (b g) -> p b g", g=NG)
                for g, (a, z) in enumerate(GROUPS):
                    link(dve.tensor_tensor(dr[:, :, a:z], db[:, :, a:z],
                                           bb[:, :, g:g + 1].to_broadcast([P, BLOCKS, z - a]), ALU.subtract))
                link(dve.tensor_copy(first_i[:, :], first_bc[0:1, :]))
                link(dve.tensor_copy(iota[:, :], iota_i[:, :]))
                dve.wait_ge(s_zero, 4)
                link(dve.memset(acc[:, :, :], 0.0))
                for j in range(PRE):
                    for q in (s_xnt_out[j], s_rows_out[j], s_res_out[j]):
                        dve.wait_ge(q, 16 * (UNITS // PRE + 1))
                dve.sem_inc(s_begin, 1)
                dve.wait_ge(s_w["chain"], 16 * 11)

                def merge(n, w, blocks):
                    firsts = [dve.value_load(first_i[0:1, bass.ds(n + g, 1)], min_val=0, max_val=NP - WIN) for g in range(NG)]
                    e_grp.wait(dve, blocks)
                    for g, first in enumerate(firsts):
                        ps = bank[w][:, g * 3 * WIN:(g + 1) * 3 * WIN]
                        e_merge.wait(dve, n + g)
                        a = acc[:, :, bass.ds(first, WIN)]
                        dve.tensor_tensor(a, a, ps[:, 0:2 * WIN].rearrange("p (h w) -> p h w", h=2), ALU.add).then_inc(e_acc.sem, 1)
                        a = acc_w[:, bass.ds(first, WIN)]
                        dve.tensor_tensor(a, a, ps[0:H, 2 * WIN:3 * WIN], ALU.add).then_inc(e_merge.sem, 1)

                def part(eng, third, i, k):
                    if third == 3:
                        merge((BLOCKS - 1) * NG, (BLOCKS - 1) % 2, BLOCKS)
                        return
                    b = i * SLOTS + k
                    w = k % 2
                    if third == 0:
                        dve.wait_ge(s_att[k], (i + 1) * 16)
                        dve.wait_ge(s_got[k], (i + 1) * (16 * BT))
                        dve.tensor_tensor(got[k][:, :, :, :], got[k][:, :, :, :],
                                          att[k][:, :, :].rearrange("p t (d o) -> p t d o", o=1).to_broadcast([P, BT, 2, ROW]),
                                          ALU.mult).then_inc(e_prod.sem, 1)
                        e_prod.wait(dve, b + 1)
                        e_scat.wait(dve, b - 1)
                        dve.tensor_tensor(msg[:, w, :, :], got[k][:, :, 0, :], got[k][:, :, 1, :], ALU.add).then_inc(e_msg.sem, 1)
                        dve.tensor_tensor(onehot[:, w, :, :],
                                          dst_rel[:, bass.ds(b * BT, BT)].rearrange("p (t o) -> p t o", o=1).to_broadcast([P, BT, WIN]),
                                          iota[:, :].rearrange("p (o w) -> p o w", o=1).to_broadcast([P, BT, WIN]),
                                          ALU.is_equal).then_inc(e_onehot.sem, 1)
                        e_msg.wait(dve, b + 1)
                        sc = msg[:, w, :, F:ROW]
                        dve.scalar_tensor_tensor(out=lrelu[:, :, :], in0=sc, scalar=SLOPE, in1=sc, op0=ALU.mult, op1=ALU.max)\
                            .then_inc(e_lrelu.sem, 1)
                        dve.tensor_tensor(smax[:, :, :], smax[:, :, :], sc, ALU.max).then_inc(e_max.sem, 1)
                        e_lrelu.wait(dve, b + 1)
                        e_wgt.wait(dve, b - 1)
                        dve.tensor_tensor(score[:, w, :, :], lrelu[:, :, :],
                                          bound[:, :].rearrange("p (o h) -> p o h", o=1).to_broadcast([P, BT, H]), ALU.subtract)\
                            .then_inc(e_score.sem, 1)
                    if third == 1:
                        e_onehot.wait(dve, b + 1)
                        e_wgt.wait(dve, b + 1)
                        dve.tensor_tensor(woh[:, w, :, :, :],
                                          onehot[:, w, :, :].rearrange("p t (o w) -> p t o w", o=1).to_broadcast([P, BT, H, WIN]),
                                          wgt[:, w, :, :].rearrange("p t (h o) -> p t h o", o=1).to_broadcast([P, BT, H, WIN]),
                                          ALU.mult).then_inc(e_woh.sem, 1)
                        if k or not isinstance(i, int) or i:
                            merge(i * (SLOTS * NG) + (k - 1) * NG, (k - 1) % 2, b)

                def key_features(v):
                    m_exp.wait(dve, v + 1)
                    m_v.wait(dve, v + 1)
                    for t in range(UT):
                        ins = dve.scalar_tensor_tensor(out=T2[:, t * C:(t + 1) * C], in0=bank[2 + t][:, 0:C], scalar=0.0,
                                                       in1=T1[:, t * C:(t + 1) * C], op0=ALU.max, op1=ALU.add)
                    ins.then_inc(m_k.sem, 1)

                def add_unit(v):
                    m_kv.wait(dve, v + 1)
                    m_sum.wait(dve, v)
                    dve.tensor_tensor(kv_sum, kv_sum, bank[4][:, 0:KC * (P + 1)].rearrange("p (j n) -> p j n", j=KC), ALU.add)\
                        .then_inc(m_sum.sem, 1)

                def mix(eng, step, v):
                    later = not isinstance(v, int) or v > 0
                    if step == 0 and later:
                        key_features(v - 1)
                    if step == 2:
                        if later:
                            add_unit(v - 1)
                        m_proj.wait(dve, v + 1)
                        for t in range(UT):
                            ins = dve.tensor_scalar(T0[:, t * C:(t + 1) * C], bank[2 + t][:, 0:C], 0.0, None, ALU.min)
                        ins.then_inc(m_min.sem, 1)
                    if step == 3:
                        key_features(UNITS - 1)
                        add_unit(UNITS - 1)
                        m_sum.wait(dve, UNITS)
                        for j in range(KC):
                            dve.scalar_tensor_tensor(out=kv[:, j, :], in0=kv_sum[:, j, 0:P], scalar=1.0 / N, in1=heads,
                                                     op0=ALU.mult, op1=ALU.mult)
                            ins = dve.tensor_scalar(ksum[:, j, :], heads, kv_sum[:, j, P:P + 1], None, ALU.mult)
                        ins.then_inc(s_kv, 1)

                def chain(eng, step, v, parts, seen, groups):
                    vector_round(dve, s, c, step, v, parts, seen, s_last if isinstance(v, int) and v == ROUNDS - 1 else s_full)

                edge_bodies(dve, part, mix, chain)
                link(dve.tensor_tensor(verdict[:, 3:4], verdict[:, 0:1], verdict[:, 1:2], ALU.max))
                c["V2"].wait(dve, "low", UNITS)
                link(dve.tensor_scalar(vb[:, :], small["gap"][:, :], -1.0, -GAP_MAX, ALU.mult, ALU.add))
                link(dve.tensor_reduce(verdict[:, 1:2], vb[:, :], AX, ALU.max))
                for t in range(UT):
                    link(dve.tensor_tensor(tol[:, t, :], small["guard"][:, :], low[:, t, :], ALU.subtract))
                link(dve.tensor_reduce(verdict[:, 2:3], tol[:, :, :].rearrange("p t h -> p (t h)"), AX, ALU.max))
                dve.sem_inc(s_ask, 1)
                spread(None, vb[:, :])
                link(dve.tensor_reduce(v_one[:, :], vb[:, :], AX, ALU.max))
                link(dve.tensor_scalar(v_one[:, :], v_one[:, :], 0.0, None, ALU.is_gt))
                link(dve.tensor_copy(flag_i[:, :], v_one[:, :]))

            @block.scalar
            def _(act):
                act.sem_inc(e_wgt.sem, 2)
                for k in range(3):
                    c[f"A{k}"].open(act)
                act.wait_ge(s_const, 3)
                with act.Fori(0, UNITS // PRE) as i:
                    for j in range(PRE + 2):
                        if j < PRE:
                            u = i * PRE + j
                            c_mv.wait(act, u + 1)
                            act.activation(sd[:, j, :], mv[:, j, :, 1], ACT.Sqrt, bias=eps_col[:, 0:1]).then_inc(c_sd.sem, 1)
                        if 1 <= j <= PRE:
                            n = j - 1
                            u = i * PRE + n
                            c_tr.wait(act, u + 1)
                            act.wait_ge(s_xnt_out[n], (i + 1) * 16)
                            act.activation(xnt[:, n, :, :], bank[n % 3][:, :].rearrange("p (k n) -> p k n", k=KC), ACT.Copy)\
                                .then_inc(c_xnt.sem, 1)
                        if j >= 2:
                            n = j - 2
                            u = i * PRE + n
                            c_tab.wait(act, u + 1)
                            act.wait_ge(s_rows_out[n], (i + 1) * 16)
                            act.activation(rows[:, n, :, :, :],
                                           bank[4 + n % 3][:, 0:UT * 2 * ROW].rearrange("p (t d r) -> p t d r", t=UT, d=2),
                                           ACT.Copy).then_inc(c_rows.sem, 1)
                for j in range(PRE):
                    act.wait_ge(s_xnt_out[j], 16 * (UNITS // PRE + 1))
                    act.wait_ge(s_res_out[j], 16 * (UNITS // PRE + 1))
                act.wait_ge(s_first, 1)
                act.dma_start(first_d.rearrange("(c p) -> c p", c=GC), gmin[0:GC, 0:P]).then_inc(s_first_out, 16)
                act.wait_ge(s_first_out, 16)
                act.dma_start(first_bc, first_d.rearrange("(a n) -> a n", a=1).to_broadcast([P, GC * P])).then_inc(s_first_in, 16)

                def part(eng, third, i, k):
                    if third == 0:
                        b = i * SLOTS + k
                        e_score.wait(act, b + 1)
                        e_scat.wait(act, b - 1)
                        act.activation(wgt[:, k % 2, :, :], score[:, k % 2, :, :], ACT.Exp).then_inc(e_wgt.sem, 1)

                def mix(eng, step, v):
                    later = not isinstance(v, int) or v > 0
                    if step == 0:
                        if later:
                            m_proj.wait(act, v)
                        act.dma_start(T4[:, :, :], xnt_d[:, :, bass.ds(v * UN, UN)]).then_inc(m_x, 16)
                    if step == 2:
                        if later:
                            m_k.wait(act, v)
                        m_min.wait(act, v + 1)
                        act.activation(T1[:, :], T0[:, :], ACT.Exp).then_inc(m_exp.sem, 1)
                        if later:
                            m_kv.wait(act, v)
                        for t in range(UT):
                            ins = act.activation(T3[:, t * C:(t + 1) * C], bank[2 + t][:, C:2 * C], ACT.Copy)
                        ins.then_inc(m_v.sem, 1)
                    if step == 3:
                        m_proj.wait(act, UNITS)
                        act.dma_start(f1[:, :, :], f1_d.rearrange("(k p) c -> p k c", p=P)).then_inc(s_w["ff"], 16)

                def chain(eng, step, v, parts, seen, groups):
                    scalar_round(act, s, c, step, v, parts, lambda a: e_merge.wait(a, groups))

                edge_bodies(act, part, mix, chain)

            @block.tensor
            def _(pe):
                pe.sem_inc(e_scat.sem, 2)
                for k in range(3):
                    c[f"P{k}"].open(pe)
                pe.wait_ge(s_const, 14)
                pe.wait_ge(s_w["wsum"], 16)
                pe.wait_ge(s_w["attn"], 16)
                for k in range(KC):
                    for d in range(2):
                        c0 = (k * 2 + d) * H
                        ins = pe.matmul(bank[7][:, c0:c0 + H], wsum_s[:, d, k * P:(k + 1) * P], attn_s, start=True, stop=True)
                ins.then_inc(s_score_w, 1)
                pe.wait_ge(s_score_c, 1)
                with pe.Fori(0, UNITS // PRE) as i:
                    for j in range(PRE + 1):
                        if j < PRE:
                            c_xn.wait(pe, i * PRE + j + 1)
                            for t in range(UT):
                                for k in range(KC):
                                    ins = pe.transpose(bank[j % 3][:, k * UN + t * P:k * UN + (t + 1) * P],
                                                       xn[:, j, t, k * P:(k + 1) * P], ident[:, :])
                            ins.then_inc(c_tr.sem, 1)
                        if j:
                            n = j - 1
                            c_xnt.wait(pe, i * PRE + n + 1)
                            for t in range(UT):
                                for k in range(KC):
                                    ins = pe.matmul(bank[4 + n % 3][:, t * 2 * ROW:(t + 1) * 2 * ROW], xnt[:, n, k, t * P:(t + 1) * P],
                                                    wg_s[:, k, :, :].rearrange("p d r -> p (d r)"), start=(k == 0), stop=(k == KC - 1))
                            ins.then_inc(c_tab.sem, 1)
                pe.wait_ge(s_ask, 1)
                for b, g in ((0, gmin), (1, gmax)):
                    for k in range(GC):
                        ins = pe.transpose(bank[b][:, k * P:(k + 1) * P], g[:, k * P:(k + 1) * P], ident[:, :])
                ins.then_inc(s_given, 1)
                pe.wait_ge(s_ask, 2)
                pe.transpose(bank[2][0:GC, 0:P], bcol, ident[:, :]).then_inc(s_given, 1)

                def spread(n, cols):
                    pe.wait_ge(s_ask, 1 + 2 * n)
                    pe.transpose(bank[0][0:4, 0:P], cols, ident[:, :]).then_inc(s_given, 1)
                    pe.wait_ge(s_ask, 2 + 2 * n)
                    pe.matmul(bank[0][:, P:P + 4], ones[0:4, :], vd[:, :], start=True, stop=True).then_inc(s_given, 1)

                spread(1, ext)
                spread(2, ext)
                pe.wait_ge(s_begin, 1)
                pe.wait_ge(s_w["mix"], 32)

                def part(eng, third, i, k):
                    if third != 2:
                        return
                    b = i * SLOTS + k
                    w = k % 2
                    e_woh.wait(pe, b + 1)
                    e_merge.wait(pe, (b - 1) * NG)
                    for g, (a, z) in enumerate(GROUPS):
                        ps = bank[w][:, g * 3 * WIN:(g + 1) * 3 * WIN]
                        for half in range(2):
                            for t in range(a, z):
                                pe.matmul(ps[half * F:(half + 1) * F, 0:2 * WIN], msg[:, w, t, 0:F],
                                          woh[:, w, t, 2 * half:2 * half + 2, :].rearrange("p h w -> p (h w)"),
                                          start=(t == a), stop=(t == z - 1))
                        for t in range(a, z):
                            ins = pe.matmul(ps[0:H, 2 * WIN:3 * WIN], wgt[:, w, t, :], onehot[:, w, t, :], start=(t == a), stop=(t == z - 1))
                    ins.then_inc(e_grp.sem, 1)
                    e_grp.wait(pe, b + 1)
                    pe.sem_inc(e_scat.sem, 1)

                def keys_by_values(v):
                    m_v.wait(pe, v + 1)
                    m_k.wait(pe, v + 1)
                    m_sum.wait(pe, v)
                    for j in range(KC):
                        to = j * (P + 1)
                        for t in range(UT):
                            cols = slice(t * C + j * P, t * C + (j + 1) * P)
                            pe.matmul(bank[4][:, to:to + P], T2[:, cols], T3[:, cols], start=(t == 0), stop=(t == UT - 1))
                        for t in range(UT):
                            cols = slice(t * C + j * P, t * C + (j + 1) * P)
                            ins = pe.matmul(bank[4][:, to + P:to + P + 1], T2[:, cols], valid[:, bass.ds(v * UT + t, 1)],
                                            start=(t == 0), stop=(t == UT - 1))
                    ins.then_inc(m_kv.sem, 1)

                def mix(eng, step, v):
                    if step == 1:
                        if not isinstance(v, int) or v > 0:
                            keys_by_values(v - 1)
                        pe.wait_ge(m_x, (v + 1) * 16)
                        for t in range(UT):
                            for k in range(KC):
                                ins = pe.matmul(bank[2 + t][:, :], T4[:, k, t * P:(t + 1) * P], wkv[:, k, :], start=(k == 0), stop=(k == KC - 1))
                        ins.then_inc(m_proj.sem, 1)
                    if step == 3:
                        keys_by_values(UNITS - 1)
                        pe.wait_ge(s_kv, 1)
                        pe.wait_ge(s_w["chain"], 16 * 11)
                        pe.wait_ge(s_w["ff"], 32)

                def chain(eng, step, v, parts, seen, groups):
                    tensor_round(pe, s, c, step, v, parts)

                edge_bodies(pe, part, mix, chain)
                spread(3, verdict[:, :])

        idx_g, dst_gi, att_g, got_g = idx[0], idx[1], att[0], got[0]
        dst_g = dst_rel[:, 0:BT]
        s_gen = sem("s_gen")
        s_gdst = sem("s_gdst")
        idx_n, att_n, got_n = BODIES * 16, BODIES * 16, BODIES * 16 * BT
        g_prod, g_msg = Count(e_prod.sem, BLOCKS), Count(e_msg.sem, SLOTS + BLOCKS)
        g_lrelu, g_score, g_wgt = Count(e_lrelu.sem, BLOCKS), Count(e_score.sem, BLOCKS), Count(e_wgt.sem, BLOCKS + e_wgt.credit)
        g_onehot, g_woh = Count(e_onehot.sem, BLOCKS), Count(e_woh.sem, BLOCKS)
        g_grp, g_merge = Count(e_grp.sem, BLOCKS), Count(e_merge.sem, GR + e_merge.credit)
        g_dst = count("g_dst", 1); g_rel = count("g_rel", 1)
        g_acc = Count(e_acc.sem, GR)
        cg = once_more(c)

        def way(eng):
            return eng.value_load(flag_i[0:1, 0:1], min_val=0, max_val=1)

        def again(eng, chain):
            def run(v):
                for step in range(STEPS):
                    chain(step, v, parts_of(v))

            run(0)
            run(1)
            with eng.Fori(2, UNITS - 1) as v:
                run(v)
            run(UNITS - 1)
            run(UNITS)
            run(UNITS + 1)

        with nc.Block() as block:
            @block.sync
            def _(sp):
                with sp.If(way(sp) > 0):
                    with sp.Fori(0, BLOCKS) as b:
                        g_merge.wait(sp, b * WINS)
                        sp.sem_inc(hold_s, 1)
                        sp.dma_start(idx_g[:, :], src_t[:, bass.ds(b * BT, BT)]).then_inc(s_idx[0], 16)
                        sp.dma_start(att_g[:, :, :], attr_t[:, bass.ds(b * BT, BT), :]).then_inc(s_att[0], 16)
                        sp.dma_start(dst_gi[:, :], dst_t[:, bass.ds(b * BT, BT)]).then_inc(s_gdst, 16)
                    sp.sem_inc(hold_s, 1)

            @block.gpsimd
            def _(pool):
                with pool.If(way(pool) > 0):
                    pool.memset(acc[:, :, :], 0.0).then_inc(s_zero, 1)
                    pool.wait_ge(s_zero, 5)
                    pool.memset(acc_w[:, :], 0.0).then_inc(s_zero, 1)
                    with pool.Fori(0, BLOCKS) as b:
                        pool.wait_ge(s_idx[0], b * 16 + (idx_n + 16))
                        pool.sem_inc(hold_p, 1)
                        g_merge.wait(pool, b * WINS)
                        pool.sem_inc(hold_p, 1)
                        for t in range(BT):
                            pool.indirect_dma_start(got_g[:, t, :, :].rearrange("p d r -> p (d r)"), None, table_d,
                                                    bass.IndirectOffsetOnAxis(ap=idx_g[:, t:t + 1], axis=0)).then_inc(s_got[0], 16)
                    pool.sem_inc(hold_p, 1)

            @block.vector
            def _(dve):
                with dve.If(way(dve) > 0):
                    dve.sem_inc(g_dst.sem, 1)
                    dve.sem_inc(g_rel.sem, 1)
                    dve.tensor_copy(bound[:, :], small["lead"][:, :]).then_inc(s_gen, 1)
                    dve.wait_ge(s_gen, 1)
                    dve.wait_ge(s_zero, 6)
                    with dve.Fori(0, BLOCKS) as b:
                        dve.wait_ge(s_gdst, (b + 1) * 16)
                        g_rel.wait(dve, b * WINS)
                        dve.tensor_scalar(dst_g, dst_gi[:, :], 1.0, float(WIN), ALU.mult, ALU.add).then_inc(g_dst.sem, 1)
                        dve.wait_ge(s_att[0], b * 16 + (att_n + 16))
                        dve.wait_ge(s_got[0], b * (16 * BT) + (got_n + 16 * BT))
                        dve.tensor_tensor(got_g[:, :, :, :], got_g[:, :, :, :],
                                          att_g[:, :, :].rearrange("p t (d o) -> p t d o", o=1).to_broadcast([P, BT, 2, ROW]),
                                          ALU.mult).then_inc(g_prod.sem, 1)
                        g_prod.wait(dve, b + 1)
                        g_grp.wait(dve, b * WINS)
                        dve.tensor_tensor(msg[:, 0, :, :], got_g[:, :, 0, :], got_g[:, :, 1, :], ALU.add).then_inc(g_msg.sem, 1)
                        g_msg.wait(dve, b + 1)
                        sc = msg[:, 0, :, F:ROW]
                        dve.scalar_tensor_tensor(out=lrelu[:, :, :], in0=sc, scalar=SLOPE, in1=sc, op0=ALU.mult, op1=ALU.max)\
                            .then_inc(g_lrelu.sem, 1)
                        g_lrelu.wait(dve, b + 1)
                        dve.tensor_tensor(score[:, 0, :, :], lrelu[:, :, :],
                                          bound[:, :].rearrange("p (o h) -> p o h", o=1).to_broadcast([P, BT, H]), ALU.subtract)\
                            .then_inc(g_score.sem, 1)
                        g_dst.wait(dve, b + 1)
                        g_wgt.wait(dve, b + 1)
                        dve.sem_inc(hold_v, 1)
                        with dve.Fori(0, WINS) as w:
                            n = b * WINS + w
                            g_onehot.wait(dve, n)
                            dve.tensor_scalar(dst_g, dst_g, float(WIN), None, ALU.subtract).then_inc(g_rel.sem, 1)
                            g_rel.wait(dve, n + 1)
                            g_grp.wait(dve, n)
                            dve.tensor_tensor(onehot[:, 0, :, :],
                                              dst_g.rearrange("p (t o) -> p t o", o=1).to_broadcast([P, BT, WIN]),
                                              iota[:, :].rearrange("p (o w) -> p o w", o=1).to_broadcast([P, BT, WIN]),
                                              ALU.is_equal).then_inc(g_onehot.sem, 1)
                            g_onehot.wait(dve, n + 1)
                            dve.tensor_tensor(woh[:, 0, :, :, :],
                                              onehot[:, 0, :, :].rearrange("p t (o w) -> p t o w", o=1).to_broadcast([P, BT, H, WIN]),
                                              wgt[:, 0, :, :].rearrange("p t (h o) -> p t h o", o=1).to_broadcast([P, BT, H, WIN]),
                                              ALU.mult).then_inc(g_woh.sem, 1)
                            g_grp.wait(dve, n + 1)
                            g_merge.wait(dve, n)
                            a = acc[:, :, bass.ds(w * WIN, WIN)]
                            dve.tensor_tensor(a, a, bank[0][:, 0:2 * WIN].rearrange("p (h w) -> p h w", h=2), ALU.add).then_inc(g_acc.sem, 1)
                            a = acc_w[:, bass.ds(w * WIN, WIN)]
                            dve.tensor_tensor(a, a, bank[0][0:H, 2 * WIN:3 * WIN], ALU.add).then_inc(g_merge.sem, 1)
                        dve.sem_inc(hold_v, 1)
                    dve.sem_inc(hold_v, 1)
                    again(dve, lambda step, v, parts: vector_round(dve, s, cg, step, v, parts, BLOCKS, s_full))
                    dve.sem_inc(hold_v, 1)

            @block.scalar
            def _(act):
                with act.If(way(act) > 0):
                    with act.Fori(0, BLOCKS) as b:
                        g_score.wait(act, b + 1)
                        g_grp.wait(act, b * WINS)
                        act.activation(wgt[:, 0, :, :], score[:, 0, :, :], ACT.Exp).then_inc(g_wgt.sem, 1)
                    act.sem_inc(hold_a, 1)
                    again(act, lambda step, v, parts: scalar_round(act, s, cg, step, v, parts, lambda a: g_merge.wait(a, BLOCKS * WINS)))
                    act.wait_ge(c["base_out"], 16 * (2 * UNITS + 1))

            @block.tensor
            def _(pe):
                with pe.If(way(pe) > 0):
                    with pe.Fori(0, BLOCKS) as b:
                        with pe.Fori(0, WINS) as w:
                            n = b * WINS + w
                            g_woh.wait(pe, n + 1)
                            g_merge.wait(pe, n)
                            for half in range(2):
                                for t in range(BT):
                                    pe.matmul(bank[0][half * F:(half + 1) * F, 0:2 * WIN], msg[:, 0, t, 0:F],
                                              woh[:, 0, t, 2 * half:2 * half + 2, :].rearrange("p h w -> p (h w)"),
                                              start=(t == 0), stop=(t == BT - 1))
                            for t in range(BT):
                                ins = pe.matmul(bank[0][0:H, 2 * WIN:3 * WIN], wgt[:, 0, t, :], onehot[:, 0, t, :],
                                                start=(t == 0), stop=(t == BT - 1))
                            ins.then_inc(g_grp.sem, 1)
                        pe.sem_inc(hold_t, 1)
                    pe.sem_inc(hold_t, 1)
                    again(pe, lambda step, v, parts: tensor_round(pe, s, cg, step, v, parts))
                    pe.sem_inc(hold_t, 1)

        work.close()
        edge.close()

        last = ExitStack()
        base = sb("base", [P, NT, C], F32, last)
        before = sb("before", [P, P], F32, last)
        wv = sb("wv", [P, NT], F32, last)
        hit = sb("hit", [P, NT], F32, last)
        above = sb("above", [P, NT], F32, last)
        level = sb("level", [P, NT], F32, last)
        pick = sb("pick", [P, NT], F32, last)
        cnt = sb("cnt", [P, 1], F32, last)
        need = sb("need", [P, 1], F32, last)
        by_tile_sum = sb("by_tile_sum", [NT, P], F32, last)
        key = {n: sb(f"key_{n}", [P, 1], I32, last) for n in ("found", "bit", "try", "a", "b", "code", "yes", "sign", "minus", "c31", "c1")}
        l_in = [sem(f"l_in{j}") for j in range(OUT_CHUNKS)]
        l_out = sem("l_out"); l_key = sem("l_key"); l_step = sem("l_step"); l_v = sem("l_v"); l_p = sem("l_p"); l_tail = sem("l_tail")
        l_done = sem("l_done"); l_before = sem("l_before")
        l_try = count("l_try"); l_a = count("l_a"); l_b = count("l_b"); l_code = count("l_code"); l_cnt = count("l_cnt")
        l_sum = count("l_sum"); l_yes = count("l_yes"); l_add = count("l_add"); l_found = count("l_found", 1)
        CT = NT // OUT_CHUNKS

        with nc.Block() as block:
            @block.sync
            def _(sp):
                for j in range(OUT_CHUNKS):
                    sp.dma_start(base[:, j * CT:(j + 1) * CT, :], base_d[j * CT * P:(j + 1) * CT * P, :].rearrange("(t p) c -> p t c", p=P))\
                        .then_inc(l_in[j], 16)
                for j in range(OUT_CHUNKS):
                    full = min((j + 1) * CT, N // P)
                    sp.wait_ge(l_done, j + 1)
                    sp.dma_start(out[j * CT * P:full * P, :].rearrange("(t p) c -> p t c", p=P), base[:, j * CT:full, :]).then_inc(l_out, 16)
                sp.dma_start(out[N // P * P:N, :], base[0:N % P, N // P, :]).then_inc(l_out, 16)
                sp.wait_ge(l_out, 16 * (OUT_CHUNKS + 1))

            @block.gpsimd
            def _(pool):
                for name, value in (("found", 0), ("bit", -2 ** 31), ("sign", -2 ** 31), ("minus", -1), ("c31", 31), ("c1", 1)):
                    pool.iota(key[name][:, :], pattern=[[0, 1]], base=value, channel_multiplier=0).then_inc(l_key, 1)
                pool.memset(before[:, :], 1.0).then_inc(l_before, 1)
                pool.wait_ge(l_before, 1)
                pool.affine_select(out=before[:, :], in_=before[:, :], compare_op=ALU.is_gt, fill=0.0, base=0,
                                   pattern=[[1, P]], channel_multiplier=-1).then_inc(l_before, 1)

            @block.vector
            def _(dve):
                n = [0]

                def link(ins):
                    n[0] += 1
                    ins.then_inc(l_v, 1)
                    dve.wait_ge(l_v, n[0])

                dve.sem_inc(l_found.sem, 1)
                link(dve.tensor_scalar(level[:, :], valid[:, :], 1.0, -LOW, ALU.subtract, ALU.mult))
                link(dve.tensor_tensor(wv[:, :], w_all[:, :], valid[:, :], ALU.mult))
                link(dve.tensor_tensor(wv[:, :], wv[:, :], level[:, :], ALU.add))
                dve.wait_ge(l_key, 6)
                k = {name: tile[:, :] for name, tile in key.items()}

                def code_of(source, r):
                    dve.tensor_scalar(k["a"], source, k["c31"], k["minus"], ALU.arith_shift_right, ALU.bitwise_xor).then_inc(l_a.sem, 1)
                    l_a.wait(dve, r)
                    dve.tensor_tensor(k["b"], k["a"], k["sign"], ALU.bitwise_or).then_inc(l_b.sem, 1)
                    l_b.wait(dve, r)
                    dve.tensor_tensor(k["code"], k["b"], source, ALU.bitwise_xor).then_inc(l_code.sem, 1)
                    l_code.wait(dve, r)

                with dve.Fori(0, 32) as i:
                    l_found.wait(dve, i)
                    dve.tensor_tensor(k["try"], k["found"], k["bit"], ALU.bitwise_or).then_inc(l_try.sem, 1)
                    l_try.wait(dve, i + 1)
                    code_of(k["try"], i + 1)
                    dve.tensor_scalar(hit[:, :], wv[:, :], k["code"].bitcast(F32), None, ALU.is_ge, ALU.add, accum_out=cnt[:, :])\
                        .then_inc(l_cnt.sem, 1)
                    l_sum.wait(dve, i + 1)
                    dve.tensor_scalar(k["yes"], bank[0][:, 0:1], TOP - 0.5, None, ALU.is_gt).then_inc(l_yes.sem, 1)
                    l_yes.wait(dve, i + 1)
                    dve.tensor_tensor(k["a"], k["yes"], k["bit"], ALU.mult).then_inc(l_add.sem, 1)
                    l_add.wait(dve, i + 1)
                    dve.tensor_tensor(k["found"], k["found"], k["a"], ALU.bitwise_or)
                    dve.tensor_tensor(k["bit"], k["bit"], k["c1"], ALU.logical_shift_right).then_inc(l_found.sem, 1)
                l_found.wait(dve, 32)
                code_of(k["found"], 33)
                thr = k["code"].bitcast(F32)
                link(dve.tensor_scalar(above[:, :], wv[:, :], thr, None, ALU.is_gt, ALU.add, accum_out=cnt[:, :]))
                link(dve.tensor_scalar(level[:, :], wv[:, :], thr, None, ALU.is_equal))
                dve.sem_inc(l_step, 1)
                dve.wait_ge(l_p, 1)
                link(dve.tensor_copy(by_tile_sum[:, :], bank[1][0:NT, 0:P]))
                link(dve.tensor_scalar(need[:, :], bank[2][:, 0:1], -1.0, float(TOP), ALU.mult, ALU.add))
                dve.sem_inc(l_step, 1)
                dve.wait_ge(l_p, 2)
                link(dve.tensor_scalar(pick[:, :], bank[3][:, 0:NT], need[:, 0:1], None, ALU.is_lt))
                link(dve.tensor_tensor(pick[:, :], pick[:, :], level[:, :], ALU.mult))
                link(dve.tensor_tensor(pick[:, :], pick[:, :], above[:, :], ALU.add))
                for j in range(OUT_CHUNKS):
                    dve.wait_ge(l_in[j], 16)
                    for t in range(j * CT, (j + 1) * CT):
                        ins = dve.scalar_tensor_tensor(out=base[:, t, :], in0=acc[:, t % UT, t // UT * UN:t // UT * UN + C],
                                                       scalar=pick[:, t:t + 1], in1=base[:, t, :], op0=ALU.mult, op1=ALU.add)
                    ins.then_inc(l_done, 1)

            @block.tensor
            def _(pe):
                with pe.Fori(0, 32) as i:
                    l_cnt.wait(pe, i + 1)
                    pe.matmul(bank[0][:, 0:1], ones[:, :], cnt[:, :], start=True, stop=True).then_inc(l_sum.sem, 1)
                pe.wait_ge(l_step, 1)
                pe.matmul(bank[1][0:NT, 0:P], level[:, :], ones[:, :], start=True, stop=True)
                pe.matmul(bank[2][:, 0:1], ones[:, :], cnt[:, :], start=True, stop=True).then_inc(l_p, 1)
                pe.wait_ge(l_step, 2)
                pe.wait_ge(l_before, 2)
                pe.matmul(bank[3][:, 0:NT], before[:, :], level[:, :], start=True, stop=False)
                pe.matmul(bank[3][:, 0:NT], by_tile_sum[:, :], before[0:NT, 0:NT], start=False, stop=True).then_inc(l_p, 1)
        last.close()


def kernel(**inputs):
    import numpy as np
    import concourse.bacc as bacc
    from concourse.bass_utils import run_bass_kernel_spmd

    def by_tile(a, fill):
        a = np.concatenate([a, fill[:ET * P - E]], axis=0)
        return np.ascontiguousarray(np.moveaxis(a.reshape((ET, P) + a.shape[1:]), 0, 1))

    def by_partition(a):
        return np.ascontiguousarray(a.reshape(-1, P).T)

    a = {k: np.asarray(v) for k, v in inputs.items()}
    x, src, dst, attr = a["x"], a["src"], a["dst"], a["edge_attr_2"]
    wf, wr = a["L0_gnn_W_forward"], a["L0_gnn_W_reverse"]
    arrays = {
        "x": np.concatenate([x, np.zeros((NP - N, C), x.dtype)], axis=0),
        "src_t": by_tile(src, src),
        "dst_t": by_tile(dst, np.full((P,), int(PAD_NODE), dst.dtype)),
        "attr_t": by_tile(attr, attr),
        "wg": np.ascontiguousarray(np.concatenate([wf.T, wr.T], axis=1)),
        "wsum": np.stack([wf, wr]),
        "attn_t": np.ascontiguousarray(a["L0_gnn_attn_forward"][0].T),
        "wkv_d": np.concatenate([a["L0_mix_Wk"], a["L0_mix_Wv"]], axis=1),
        "wq_d": a["L0_mix_Wq"],
        "wm_d": a["L0_mix_Wm"],
        "w1_d": a["L0_mix_W1"],
        "w2_d": a["L0_mix_W2"],
        "g1_d": by_partition(a["L0_mix_g1"]),
        "b1_d": by_partition(a["L0_mix_b1"]),
        "g2_d": a["L0_mix_g2"],
        "b2_d": a["L0_mix_b2"],
        "f1_d": a["L0_ffn_w1"],
        "f2_d": a["L0_ffn_w2"],
        "fb1_d": by_partition(a["L0_ffn_b1"]),
        "fb2_d": a["L0_ffn_b2"],
        "wr_d": np.ascontiguousarray(a["L0_ffn_wr"][:, 0]),
        "br_d": a["L0_ffn_br"],
    }
    nc = bacc.Bacc("TRN2", target_bir_lowering=False, num_devices=1)
    args = {k: nc.dram_tensor(f"in_{k}", v.shape, mybir.dt.from_np(v.dtype), kind="ExternalInput").ap() for k, v in arrays.items()}
    out = nc.dram_tensor("out_0", (N, C), F32, kind="ExternalOutput").ap()
    build_program(nc, out=out, **args)
    r = run_bass_kernel_spmd(nc, [{f"in_{k}": v for k, v in arrays.items()}], core_ids=[0])
    return r.results[0]["out_0"]
```

```python
from contextlib import ExitStack

import concourse.bass as bass
from concourse import mybir

F32 = mybir.dt.float32
I32 = mybir.dt.int32
ALU = mybir.AluOpType
ACT = mybir.ActivationFunctionType
AX = mybir.AxisListType.X

P = 128
N = 6250
E = 206250
TOP = 3124
BITS = 4
DIGIT = 2 ** BITS
C = 256
KC = C // P
F = 64
H = 4
ROW = F + H
UT = 2
UN = UT * P
UNITS = -(-N // UN)
NP = UNITS * UN
NT = NP // P
LAST = N - (NP - UN)
ET = -(-E // P)
BT = 13
BLOCKS = ET // BT
GROUPS = [(0, 4), (4, 8), (8, 13)]
NG = len(GROUPS)
WIN = 32
WINS = NP // WIN
GR = BLOCKS * NG
GC = -(-GR // P)
PAD_NODE = 1.0e6
LN_EPS = 1e-5
SUM_EPS = 1e-10
ATT_EPS = 1e-6
SLOPE = 0.2
GAP_MAX = 30.0
SUM_TOL = 2.0 ** -23
LOW = -3.0e38
HD = 32
HID = 2 * C
FF = 4 * C
PRE = 5
SLOTS = 4
BODIES = BLOCKS // SLOTS
MIX_BODIES = 5
MIX_EACH = UNITS // MIX_BODIES
GAP_BODY = BODIES - 6
STEPS = 15
OUT_CHUNKS = 10
ROUNDS = UNITS + 3
assert BLOCKS * BT == ET and BLOCKS % SLOTS == 0 and UNITS % PRE == 0 and UNITS % MIX_BODIES == 0
assert E % P and LAST <= P and KC == 2 and UT == 2
assert NT % OUT_CHUNKS == 0 and N // P > NT - NT // OUT_CHUNKS
assert MIX_BODIES + 3 < GAP_BODY and BODIES - MIX_BODIES - 2 < UNITS


class Count:

    def __init__(self, sem, credit=0):
        self.sem, self.credit = sem, credit

    def wait(self, eng, count):
        eng.wait_ge(self.sem, count + self.credit)


class Stages:

    AHEAD = 3

    def __init__(self, sem, names, before=0):
        self.sem, self.names, self.before = sem, names.split(), before

    def open(self, eng):
        eng.sem_inc(self.sem, self.AHEAD * len(self.names))

    def wait(self, eng, name, units):
        if isinstance(units, int):
            units = min(units, UNITS)
        eng.wait_ge(self.sem, units * len(self.names) + (self.names.index(name) + 1 + (self.before + self.AHEAD - 1) * len(self.names)))


STAGES = {
    "V0": "qmin qt zr0 zr mt stat1 mv1 rstd1 z",
    "V1": "stat2 mv2 m1 rstd2 z2 y2 y3 mtop diag top lead gap guard",
    "V2": "den tol rden low gn ra x1 stat3 mv3 rstd3 xf dot base wcol yb yw",
    "A0": "qexp sd1 m2t",
    "A1": "relu sd2 gexp",
    "A2": "part res sd3 xft gelu0 gelu1 gelu2 gelu3",
    "P0": "q attn proj ztr own",
    "P1": "hid y m1t mall",
    "P2": "ptr xtr ff0 ff1 ff2 ff3 out",
}


def chain_counts(sem):
    c = {name: Stages(sem(f"stages_{name}"), names) for name, names in STAGES.items()}
    for name in ("x_in", "r_in", "base_out"):
        c[name] = sem(f"c_{name}")
    return c


def once_more(c):
    return {name: Stages(q.sem, " ".join(q.names), UNITS) if isinstance(q, Stages) else q for name, q in c.items()}


def units_done(c, v):
    return v + 1, v, v - 1, c["V0"].before


def real_tiles(u):
    return 1 if isinstance(u, int) and u == UNITS - 1 else UT


def vector_round(dve, s, c, step, v, parts, seen, track):
    bank = s["bank"]
    r0, r1, r2, before = units_done(c, v)
    V0, V1, V2 = c["V0"], c["V1"], c["V2"]

    def moments(count, n, r, source):
        k = n - 1
        for t in range(UT):
            ins = dve.bn_stats(s["stats"][:, k, t, :], source(t))
        ins.then_inc(count.sem, 1)
        count.wait(dve, f"stat{n}", r)
        dve.sem_inc(s["hold_v"], 1)
        for t in range(UT):
            ins = dve.bn_aggr(s["mv"][:, k, t, :], s["stats"][:, k, t, :])
        ins.then_inc(count.sem, 1)

    def normal(count, scalar_count, n, r, dst, source):
        k = n - 1
        scalar_count.wait(dve, f"sd{n}", r)
        dve.reciprocal(s["rstd"][:, k, :], s["sd"][:, k, :]).then_inc(count.sem, 1)
        count.wait(dve, f"rstd{n}", r)
        for t in range(UT):
            ins = dve.tensor_scalar(dst[:, t * C:(t + 1) * C], source(t), s["mv"][:, k, t, 0:1], s["rstd"][:, k, t:t + 1],
                                    ALU.subtract, ALU.mult)
        ins.then_inc(count.sem, 1)

    def rows_of(tile):
        return lambda t: tile[:, t * C:(t + 1) * C]

    def by_tile(row):
        return row.rearrange("p (o c) -> p o c", o=1).to_broadcast([P, UT, C])

    if 3 in parts and step == 0:
        u = v - 3
        V2.wait(dve, "wcol", r2 - 1)
        dve.tensor_copy(s["w_all"][:, bass.ds(u * UT, UT)], s["wcol"])
        c["P2"].wait(dve, "out", r2 - 1)
        t2 = s["T2"].rearrange("p (t c) -> p t c", t=UT)
        dve.tensor_tensor(t2, bank[5][:, :].rearrange("p (t c) -> p t c", t=UT), by_tile(s["fb2"]), ALU.add).then_inc(V2.sem, 1)
        V2.wait(dve, "yb", r2 - 1)
        for t in range(UT):
            ins = dve.tensor_scalar(s["acc"][:, t, bass.ds(u * UN, C)], s["T2"][:, t * C:(t + 1) * C], s["wcol"][:, t:t + 1],
                                    None, ALU.mult)
        ins.then_inc(V2.sem, 1)
    if 0 in parts:
        if step == 2:
            c["P0"].wait(dve, "q", r0)
            c["P2"].wait(dve, "ptr", r2)
            dve.tensor_scalar(s["T0"], bank[3][:, :], 0.0, None, ALU.min).then_inc(V0.sem, 1)
        if step == 4:
            c["A0"].wait(dve, "qexp", r0)
            dve.scalar_tensor_tensor(out=s["T2"], in0=bank[3][:, :], scalar=0.0, in1=s["T1"], op0=ALU.max, op1=ALU.add)\
                .then_inc(V0.sem, 1)
        if step == 6:
            c["P0"].wait(dve, "attn", r0)
            c["P2"].wait(dve, "xtr", r2)
            dve.tensor_scalar(s["T0"], bank[2][:, :], ATT_EPS, None, ALU.add).then_inc(V0.sem, 1)
            V0.wait(dve, "zr0", r0)
            dve.reciprocal(s["T0"], s["T0"]).then_inc(V0.sem, 1)
            V0.wait(dve, "zr", r0)
            dve.scalar_tensor_tensor(out=s["T3"], in0=bank[4][:, :], scalar=float(N), in1=s["T0"], op0=ALU.mult, op1=ALU.mult)\
                .then_inc(V0.sem, 1)
        if step == 8:
            c["P0"].wait(dve, "proj", r0)
            moments(V0, 1, r0, rows_of(bank[3]))
        if step == 10:
            normal(V0, c["A0"], 1, r0, s["T0"], rows_of(bank[3]))
    if 1 in parts:
        if step == 5:
            c["P1"].wait(dve, "y", r1)
            moments(V1, 2, r1, rows_of(bank[7]))
        if step == 6:
            s["max_seen"](dve, seen)
            dve.tensor_reduce(s["m1"], s["smax"].rearrange("p t h -> p h t"), AX, ALU.max).then_inc(V1.sem, 1)
        if step == 7:
            normal(V1, c["A1"], 2, r1, s["Y"], rows_of(bank[7]))
            y = s["Y"].rearrange("p (t c) -> p t c", t=UT)
            V1.wait(dve, "z2", r1)
            dve.tensor_tensor(y, y, by_tile(s["g2"]), ALU.mult).then_inc(V1.sem, 1)
            V1.wait(dve, "y2", r1)
            dve.tensor_tensor(y, y, by_tile(s["b2"]), ALU.add).then_inc(V1.sem, 1)
        if step == 8:
            c["P1"].wait(dve, "m1t", r1)
            dve.tensor_reduce(s["mtop"], bank[2][0:H, 0:P], AX, ALU.max).then_inc(V1.sem, 1)
            V1.wait(dve, "mtop", r1)
            dve.tensor_scalar(s["diag"], s["ident"][0:H, 0:H], s["mtop"], None, ALU.mult).then_inc(V1.sem, 1)
        if step == 10:
            c["P1"].wait(dve, "mall", r1)
            dve.tensor_copy(s["top"], bank[2][:, UN:UN + H]).then_inc(V1.sem, 1)
            V1.wait(dve, "top", r1)
            dve.scalar_tensor_tensor(out=s["lead"], in0=s["top"], scalar=SLOPE, in1=s["top"], op0=ALU.mult, op1=ALU.max).then_inc(V1.sem, 1)
            V1.wait(dve, "lead", r1)
            dve.tensor_tensor(s["gap"], s["lead"], s["bound"], ALU.subtract).then_inc(V1.sem, 1)
        if step == 12:
            c["A1"].wait(dve, "gexp", r1)
            dve.tensor_scalar(s["guard"], s["gexp"], SUM_EPS, None, ALU.mult).then_inc(V1.sem, 1)
    if 2 in parts:
        u = v - 2
        if step == 2:
            c["P2"].wait(dve, "ptr", r2)
            V1.wait(dve, "guard", r2)
            for t in range(UT):
                ins = dve.tensor_tensor(s["den"][:, t, :], bank[5 + t][:, 2 * P:2 * P + H], s["guard"], ALU.add)
            ins.then_inc(V2.sem, 1)
            for t, n in enumerate(track):
                if n:
                    ins = dve.scalar_tensor_tensor(out=s["tol"][0:n, t, :], in0=bank[5 + t][0:n, 2 * P:2 * P + H], scalar=SUM_TOL,
                                                   in1=s["guard"][0:n, :], op0=ALU.mult, op1=ALU.add)
            ins.then_inc(V2.sem, 1)
            V2.wait(dve, "den", r2)
            dve.reciprocal(s["rden"], s["den"]).then_inc(V2.sem, 1)
            V2.wait(dve, "rden", r2)
            for t, n in enumerate(track):
                if n:
                    low = s["low"][0:n, t, :]
                    ins = dve.tensor_tensor(low, low, s["tol"][0:n, t, :], ALU.min)
            ins.then_inc(V2.sem, 1)
            for t in range(UT):
                ins = dve.tensor_tensor(s["T2"][:, t * C:(t + 1) * C].rearrange("p (b a f) -> p b a f", b=2, a=2),
                                        bank[5 + t][:, 0:2 * P].rearrange("p (a b f) -> p b a f", a=2, b=2),
                                        s["rden"][:, t, :].rearrange("p (b a o) -> p b a o", b=2, o=1).to_broadcast([P, 2, 2, F]),
                                        ALU.mult)
            ins.then_inc(V2.sem, 1)
            c["A2"].wait(dve, "res", r2)
            dve.tensor_tensor(s["T5"], s["T5"], s["Y"], ALU.add).then_inc(V2.sem, 1)
            V2.wait(dve, "ra", r2)
            dve.tensor_tensor(s["T5"], s["T5"], s["T2"], ALU.add).then_inc(V2.sem, 1)
            V2.wait(dve, "x1", r2)
            moments(V2, 3, r2, rows_of(s["T5"]))
        if step == 4:
            c["A0"].wait(dve, "qexp", r0)
            normal(V2, c["A2"], 3, r2, s["T0"], rows_of(s["T5"]))
            V2.wait(dve, "xf", r2)
            for t in range(UT):
                rows = slice(t * C, (t + 1) * C)
                ins = dve.tensor_tensor_reduce(s["T3"][:, rows], s["T0"][:, rows], s["wr"], 1.0, 0.0, ALU.mult, ALU.add,
                                               s["dot"][:, t:t + 1])
            ins.then_inc(V2.sem, 1)
            dve.wait_ge(c["base_out"], (r2 + before) * 16)
            dve.tensor_tensor(s["base"], s["T5"], s["T0"], ALU.add).then_inc(V2.sem, 1)
            V2.wait(dve, "dot", r2)
            dve.tensor_scalar(s["wcol"], s["dot"], s["br"], None, ALU.add).then_inc(V2.sem, 1)


def scalar_round(act, s, c, step, v, parts, merges):
    bank = s["bank"]
    r0, r1, r2, before = units_done(c, v)
    A0, A1, A2 = c["A0"], c["A1"], c["A2"]

    def deviation(vector_count, count, n, r):
        vector_count.wait(act, f"mv{n}", r)
        act.activation(s["sd"][:, n - 1, :], s["mv"][:, n - 1, :, 1], ACT.Sqrt, bias=s["eps"]).then_inc(count.sem, 1)

    if isinstance(v, int) and v == 0 and step == 0:
        act.dma_start(s["T4"], s["xnt_d"][:, :, 0:UN]).then_inc(c["x_in"], 16)
    if step == 12 and (not isinstance(v, int) or v + 1 < UNITS):
        c["P0"].wait(act, "own", r0)
        act.dma_start(s["T4"], s["xnt_d"][:, :, bass.ds((v + 1) * UN, UN)]).then_inc(c["x_in"], 16)
    if 0 in parts and step == 3:
        c["V0"].wait(act, "qmin", r0)
        act.activation(s["T1"], s["T0"], ACT.Exp).then_inc(A0.sem, 1)
    if 2 in parts:
        u = v - 2
        if step == 0:
            merges(act)
            c["P0"].wait(act, "ztr", r0 - 1)
            act.activation(s["T3"].rearrange("p (a n) -> p a n", a=2), s["acc"][:, :, bass.ds(u * UN, UN)], ACT.Copy)
            act.activation(s["part_w"], s["acc_w"][:, bass.ds(u * UN, UN)], ACT.Copy).then_inc(A2.sem, 1)
            act.wait_ge(c["r_in"], (r2 + before) * 16)
            for t in range(UT):
                rows = s["T5"][:, t * C:(t + 1) * C]
                ins = act.activation(rows, rows, ACT.Identity, bias=s["res_offset"][:, bass.ds(u * UT + t, 1)],
                                     scale=s["res_scale"][:, bass.ds(u * UT + t, 1)])
            ins.then_inc(A2.sem, 1)
        if step == 3:
            deviation(c["V2"], A2, 3, r2)
        if step == 5:
            c["V2"].wait(act, "base", r2)
            act.dma_start(s["base_d"][bass.ds(u * UN, UN), :].rearrange("(t p) c -> p t c", p=P),
                          s["base"].rearrange("p (t c) -> p t c", t=UT)).then_inc(c["base_out"], 16)
        if step == 6:
            c["P2"].wait(act, "xtr", r2)
            c["V0"].wait(act, "qt", r0)
            act.activation(s["T1"], bank[5][:, :], ACT.Copy).then_inc(A2.sem, 1)
        if step in (8, 10):
            for f in ((0, 1) if step == 8 else (2, 3)):
                c["P2"].wait(act, f"ff{f}", r2)
                for m in range(2):
                    j = 2 * f + m
                    n = real_tiles(u) * P
                    ins = act.activation(s["hidden"][:, j * UN:j * UN + n], bank[6 + f % 2][:, m * UN:m * UN + n],
                                         ACT.Gelu_apprx_tanh, bias=s["fb1"][:, j:j + 1])
                ins.then_inc(A2.sem, 1)
    if 1 in parts:
        if step == 2:
            c["P1"].wait(act, "hid", r1)
            c["P2"].wait(act, "out", r2 - 1)
            for f, b in enumerate((2, 4)):
                ins = act.activation(s["hidden"][:, 2 * f * UN:(2 * f + 2) * UN], bank[b][:, :], ACT.Relu)
            ins.then_inc(A1.sem, 1)
        if step == 6:
            deviation(c["V1"], A1, 2, r1)
        if step == 11:
            c["V1"].wait(act, "gap", r1)
            act.activation(s["gexp"], s["gap"], ACT.Exp).then_inc(A1.sem, 1)
        if step == 13:
            c["V2"].wait(act, "base", r2)
            act.dma_start(s["T5"].rearrange("p (t c) -> p t c", t=UT),
                          s["x"][bass.ds((v - 1) * UN, UN), :].rearrange("(t p) c -> p t c", p=P)).then_inc(c["r_in"], 16)
    if 0 in parts:
        if step == 9:
            deviation(c["V0"], A0, 1, r0)
        if step == 12:
            c["P0"].wait(act, "ztr", r0)
            c["P2"].wait(act, "ff3", r2)
            for k in range(KC):
                ins = act.activation(s["T1"][:, k * UN:(k + 1) * UN], bank[3][:, k * UN:(k + 1) * UN], ACT.Identity,
                                     bias=s["b1"][:, k:k + 1], scale=s["g1"][:, k:k + 1])
            ins.then_inc(A0.sem, 1)


def tensor_round(pe, s, c, step, v, parts):
    bank, ident = s["bank"], s["ident"]
    r0, r1, r2, before = units_done(c, v)
    P0, P1, P2 = c["P0"], c["P1"], c["P2"]

    def turned(dst, tile):
        for t in range(UT):
            for k in range(KC):
                ins = pe.transpose(dst[:, k * UN + t * P:k * UN + (t + 1) * P], tile[:, t * C + k * P:t * C + (k + 1) * P], ident)
        return ins

    def by_row(dst, halves, weights, n, tiles=range(UT)):
        for t in tiles:
            for k in range(n):
                ins = pe.matmul(dst[:, t * C:(t + 1) * C], halves[:, k * UN + t * P:k * UN + (t + 1) * P], weights[:, k, :],
                                start=(k == 0), stop=(k == n - 1))
        return ins

    def hidden_half(f, ks, n=UN):
        for m in (2 * f, 2 * f + 1):
            for k in ks:
                rhs = s["T4"][:, k, 0:n] if k < KC else s["T1"][:, (k - KC) * UN:(k - KC) * UN + n]
                ins = pe.matmul(bank[(2, 4)[f]][:, (m % 2) * UN:(m % 2) * UN + n], s["w1"][:, k, m * P:(m + 1) * P], rhs,
                                start=(k == 0 and m % 2 == 0), stop=(k == 2 * KC - 1 and m % 2 == 1))
        return ins

    if 2 in parts:
        if step == 1:
            c["A2"].wait(pe, "part", r2)
            c["V2"].wait(pe, "yb", r2 - 1)
            for t in range(UT):
                for a in range(2):
                    pe.transpose(bank[5 + t][:, a * P:(a + 1) * P], s["T3"][:, a * UN + t * P:a * UN + (t + 1) * P], ident)
                ins = pe.transpose(bank[5 + t][:, 2 * P:2 * P + H], s["part_w"][:, t * P:(t + 1) * P], ident[0:H, 0:H])
            ins.then_inc(P2.sem, 1)
        if step == 5:
            c["V2"].wait(pe, "xf", r2)
            turned(bank[5], s["T0"]).then_inc(P2.sem, 1)
        if step in (7, 8, 9):
            c["A2"].wait(pe, "xft", r2)
            for f in ((0,), (1,), (2, 3))[step - 7]:
                if f == 1:
                    c["V1"].wait(pe, "z2", r1)
                if f >= 2:
                    c["A2"].wait(pe, f"gelu{f - 2}", r2)
                for m in range(2):
                    j = 2 * f + m
                    for k in range(KC):
                        n = real_tiles(v - 2) * P
                        ins = pe.matmul(bank[6 + f % 2][:, m * UN:m * UN + n], s["f1"][:, k, j * P:(j + 1) * P],
                                        s["T1"][:, k * UN:k * UN + n], start=(k == 0), stop=(k == KC - 1))
                ins.then_inc(P2.sem, 1)
        if step == 11:
            c["A2"].wait(pe, "gelu3", r2)
            ins = by_row(bank[5], s["hidden"], s["f2"], FF // P, (0,))
            if real_tiles(v - 2) == 1:
                ins.then_inc(P2.sem, 1)
        if step == 12 and real_tiles(v - 2) == UT:
            by_row(bank[5], s["hidden"], s["f2"], FF // P, (1,)).then_inc(P2.sem, 1)
    if 1 in parts:
        if step == 1:
            c["A0"].wait(pe, "m2t", r1)
            n = real_tiles(v - 1) * P
            hidden_half(0, (2, 3), n)
            hidden_half(1, (2, 3), n).then_inc(P1.sem, 1)
        if step == 3:
            c["A1"].wait(pe, "relu", r1)
            by_row(bank[7], s["hidden"], s["w2"], HID // P, range(real_tiles(v - 1))).then_inc(P1.sem, 1)
        if step == 7:
            c["V1"].wait(pe, "m1", r1)
            c["V0"].wait(pe, "mt", r0)
            pe.transpose(bank[2][0:H, 0:P], s["m1"], ident).then_inc(P1.sem, 1)
        if step == 9:
            c["V1"].wait(pe, "diag", r1)
            pe.matmul(bank[2][:, UN:UN + H], s["ones"][0:H, :], s["diag"], start=True, stop=True).then_inc(P1.sem, 1)
    if 0 in parts:
        if step == 0:
            pe.wait_ge(c["x_in"], (r0 + before) * 16)
            c["A0"].wait(pe, "m2t", r0 - 1)
            for j in range(KC):
                for k in range(KC):
                    ins = pe.matmul(bank[3][:, j * UN:(j + 1) * UN], s["wq"][:, k, j * P:(j + 1) * P], s["T4"][:, k, :],
                                    start=(k == 0), stop=(k == KC - 1))
            ins.then_inc(P0.sem, 1)
        if step == 5:
            c["V0"].wait(pe, "qt", r0)
            c["A1"].wait(pe, "relu", r1)
            for b, w in ((2, s["ksum"]), (4, s["kv"])):
                for j in range(KC):
                    ins = pe.matmul(bank[b][:, j * UN:(j + 1) * UN], w[:, j, :], s["T2"][:, j * UN:(j + 1) * UN], start=True, stop=True)
            ins.then_inc(P0.sem, 1)
        if step == 7:
            c["V0"].wait(pe, "mt", r0)
            by_row(bank[3], s["T3"], s["wm"], KC).then_inc(P0.sem, 1)
        if step == 8:
            hidden_half(1, (0, 1))
        if step == 11:
            c["V0"].wait(pe, "z", r0)
            c["V1"].wait(pe, "top", r1)
            turned(bank[3], s["T0"]).then_inc(P0.sem, 1)
            hidden_half(0, (0, 1)).then_inc(P0.sem, 1)


def parts_of(v):
    return tuple(k for k in range(4) if 0 <= v - k < UNITS) if isinstance(v, int) else (0, 1, 2, 3)


def body_slots(steps):
    n = 3 * SLOTS
    return [range(q * steps // n, (q + 1) * steps // n) for q in range(n)]


def build_program(nc, x, src_t, dst_t, attr_t, wg, wsum, attn_t, wkv_d, wq_d, wm_d, w1_d, w2_d, g1_d, b1_d, g2_d, b2_d,
                  f1_d, f2_d, fb1_d, fb2_d, wr_d, br_d, out):
    with ExitStack() as ctx:
        def sb(name, shape, dt=F32, where=ctx):
            return where.enter_context(nc.sbuf_tensor(name, shape, dt))

        def sem(name):
            return ctx.enter_context(nc.semaphore(name))

        def count(name, credit=0):
            return Count(sem(name), credit)

        table_d = nc.dram_tensor("table_d", (NP, 2 * ROW), F32, kind="Internal").ap()
        xnt_d = nc.dram_tensor("xnt_d", (P, KC, NP), F32, kind="Internal").ap()
        base_d = nc.dram_tensor("base_d", (NP, C), F32, kind="Internal").ap()
        first_d = nc.dram_tensor("first_d", (GC * P,), F32, kind="Internal").ap()

        bank = [ctx.enter_context(nc.psum_tensor(f"bank{i}", [P, 512], F32)) for i in range(8)]

        ident = sb("ident", [P, P])
        ones = sb("ones", [P, P])
        iota_i = sb("iota_i", [P, WIN], I32)
        iota = sb("iota", [P, WIN])
        eps_col = sb("eps_col", [P, 1])
        valid = sb("valid", [P, NT])

        wq = sb("wq", [P, KC, C])
        wm = sb("wm", [P, KC, C])
        w1 = sb("w1", [P, 2 * KC, HID])
        w2 = sb("w2", [P, HID // P, C])
        f1 = sb("f1", [P, KC, FF])
        wkv = f1[:, :, 0:2 * C]
        f2 = sb("f2", [P, FF // P, C])
        g1 = sb("g1", [P, KC])
        b1 = sb("b1", [P, KC])
        fb1 = sb("fb1", [P, FF // P])
        g2 = sb("g2", [P, C])
        b2 = sb("b2", [P, C])
        fb2 = sb("fb2", [P, C])
        wr = sb("wr", [P, C])
        br = sb("br", [P, 1])

        dst_rel = sb("dst_rel", [P, ET])
        first_i = sb("first_i", [1, GC * P], I32)
        bound = sb("bound", [P, H])
        smax = sb("smax", [P, BT, H])
        acc = sb("acc", [P, 2, NP])
        acc_w = sb("acc_w", [H, NP])
        w_all = sb("w_all", [P, NT])
        low = sb("low", [P, UT, H])
        kv = sb("kv", [P, KC, P])
        ksum = sb("ksum", [P, KC, P])
        verdict = sb("verdict", [P, 4])
        flag_i = sb("flag_i", [P, 1], I32)
        v4 = sb("v4", [4, 1])
        vd = sb("vd", [4, 4])
        vb = sb("vb", [P, 4])
        v_one = sb("v_one", [P, 1])
        small = {n: sb(n, [P, H]) for n in ("m1", "top", "lead", "gap", "gexp", "guard")}
        mtop = sb("mtop", [H, 1])
        diag = sb("diag", [H, H])
        stats_u = sb("stats_u", [P, 3, UT, 6])
        mv_u = sb("mv_u", [P, 3, UT, 2])
        sd_u = sb("sd_u", [P, 3, UT])
        rstd_u = sb("rstd_u", [P, 3, UT])
        res_scale = sb("res_scale", [P, NT])
        res_offset = sb("res_offset", [P, NT])
        den = sb("den", [P, UT, H])
        rden = sb("rden", [P, UT, H])
        tol = sb("tol", [P, UT, H])
        dot = sb("dot", [P, UT])
        wcol = sb("wcol", [P, UT])

        s_const = sem("s_const")
        s_zero = sem("s_zero")
        s_dv = sem("s_dv")
        s_found = sem("s_found")
        s_ask = sem("s_ask")
        s_given = sem("s_given")
        hold_v = sem("hold_v"); hold_p = sem("hold_p"); hold_s = sem("hold_s"); hold_a = sem("hold_a"); hold_t = sem("hold_t")
        s_w = {k: sem(f"s_w_{k}") for k in ("wg", "wsum", "attn", "dst", "attr", "mix", "chain", "ff")}

        def linker(eng, count):
            links = [0]

            def link(ins):
                links[0] += 1
                ins.then_inc(count, 1)
                eng.wait_ge(count, links[0])
            return link

        edge = ExitStack()
        idx = [sb(f"idx{k}", [P, BT], I32, edge) for k in range(SLOTS)]
        att = [sb(f"att{k}", [P, BT, 2], F32, edge) for k in range(SLOTS)]
        got = [sb(f"got{k}", [P, BT, 2, ROW], F32, edge) for k in range(SLOTS)]
        T4 = sb("T4", [P, KC, UN], F32, edge)
        T5 = sb("T5", [P, UT * C], F32, edge)
        Y = sb("Y", [P, UT * C], F32, edge)
        base_u = sb("base_u", [P, UT * C], F32, edge)
        kv_sum = Y[:, 0:KC * (P + 1)].rearrange("p (k n) -> p k n", k=KC)
        heads = T5[:, 0:P]
        limit_i = base_u[:, 0:(BODIES + 1) * SLOTS * NG].bitcast(I32)
        early = (GAP_BODY + 1) * SLOTS * NG
        lrelu = sb("lrelu", [P, BT, H], F32, edge)
        score = sb("score", [P, 2, BT, H], F32, edge)
        wgt = sb("wgt", [P, 2, BT, H], F32, edge)

        pre = ExitStack()
        x_u = sb("x_u", [P, PRE, UT, C], F32, pre)
        xn = sb("xn", [P, PRE, UT, C], F32, pre)
        xnt = sb("xnt", [P, PRE, KC, UN], F32, pre)
        rows = sb("rows", [P, PRE, UT, 2, ROW], F32, pre)
        stats = sb("stats", [P, PRE, UT, 6], F32, pre)
        mv = sb("mv", [P, PRE, UT, 2], F32, pre)
        sd = sb("sd", [P, PRE, UT], F32, pre)
        rstd = sb("rstd", [P, PRE, UT], F32, pre)
        pre.close()
        work = ExitStack()
        msg = sb("msg", [P, 2, BT, ROW], F32, work)
        onehot = sb("onehot", [P, 2, BT, WIN], F32, work)
        woh = sb("woh", [P, 2, BT, H, WIN], F32, work)
        T0 = sb("T0", [P, UT * C], F32, work)
        T1 = sb("T1", [P, UT * C], F32, work)
        T2 = sb("T2", [P, UT * C], F32, work)
        T3 = sb("T3", [P, UT * C], F32, work)
        hidden = sb("hidden", [P, FF // P * UN], F32, work)

        slot_of = [g[:, :, :, :].rearrange("p t d r -> p (t d r)") for g in got]
        dst_i = slot_of[0][:, 0:ET].bitcast(I32)
        dst_real = slot_of[1][:, 0:ET]
        flat = acc[:, :, :].rearrange("p a n -> p (a n)")
        at = [0]

        def piece(n):
            at[0] += n
            return flat[:, at[0] - n:at[0]]

        attr = piece(2 * ET).rearrange("p (t d) -> p t d", d=2)
        first_bc = piece(GC * P)
        gmin = piece(GC * P)
        gmax = piece(GC * P)
        wg_s = piece(KC * 2 * ROW).rearrange("p (k d r) -> p k d r", k=KC, d=2)
        wsum_s = piece(2 * C).rearrange("p (d c) -> p d c", d=2)[0:F]
        attn_s = piece(H)[0:F]
        p_all = piece(NT * 2 * H).rearrange("p (t d h) -> p t d h", d=2, h=H)
        p_lo = piece(NT * 2 * H).rearrange("p (t d h) -> p t d h", d=2, h=H)
        ext = piece(4)
        ext_bc = piece(4)
        bcol = piece(GC)
        mcol = piece(GC)
        limit = piece((BODIES + 1) * SLOTS * NG)
        scratch = at[0]
        assert scratch <= 2 * NP

        c_stats = count("c_stats"); c_mv = count("c_mv"); c_sd = count("c_sd"); c_rstd = count("c_rstd")
        c_xn = count("c_xn"); c_res = count("c_res")
        c_tr = count("c_tr"); c_xnt = count("c_xnt"); c_tab = count("c_tab"); c_rows = count("c_rows")
        c_scores = count("c_scores")
        s_x = [sem(f"s_x{j}") for j in range(PRE)]
        s_rows_out = [sem(f"s_rows_out{j}") for j in range(PRE)]
        s_xnt_out = [sem(f"s_xnt_out{j}") for j in range(PRE)]
        s_score_w = sem("s_score_w"); s_score_c = sem("s_score_c")
        s_first_out = sem("s_first_out"); s_first_in = sem("s_first_in")
        s_first = sem("s_first")
        s_kv = sem("s_kv")
        s_begin = sem("s_begin")

        s_idx = [sem(f"s_idx{k}") for k in range(SLOTS)]
        s_att = [sem(f"s_att{k}") for k in range(SLOTS)]
        s_got = [sem(f"s_got{k}") for k in range(SLOTS)]
        e_prod = count("e_prod"); e_msg = count("e_msg", SLOTS)
        e_lrelu = count("e_lrelu"); e_score = count("e_score"); e_max = count("e_max")
        e_wgt = count("e_wgt", 2); e_onehot = count("e_onehot"); e_woh = count("e_woh")
        e_scat = count("e_scat", 2)
        e_grp = count("e_grp"); e_merge = count("e_merge", NG + 1); e_acc = count("e_acc")
        m_x = sem("m_x")
        m_proj = count("m_proj"); m_min = count("m_min"); m_exp = count("m_exp"); m_v = count("m_v")
        m_k = count("m_k"); m_kv = count("m_kv"); m_sum = count("m_sum", 1)
        c = chain_counts(sem)

        def max_seen(dve, seen):
            e_max.wait(dve, seen)

        s = dict(bank=bank, ident=ident[:, :], ones=ones[:, :], smax=smax[:, :, :], acc=acc, acc_w=acc_w, w_all=w_all,
                 T0=T0[:, :], T1=T1[:, :], T2=T2[:, :], T3=T3[:, :], T4=T4[:, :, :], T5=T5[:, :], Y=Y[:, :], base=base_u[:, :], hidden=hidden[:, :],
                 part_w=T0[0:H, 0:UN], mtop=mtop[:, :], diag=diag[:, :], bound=bound[:, :], stats=stats_u, mv=mv_u,
                 sd=sd_u, rstd=rstd_u, den=den[:, :, :], rden=rden[:, :, :], tol=tol, low=low, dot=dot[:, :],
                 wcol=wcol[:, :], g1=g1, b1=b1, g2=g2[:, :], b2=b2[:, :], fb1=fb1, fb2=fb2[:, :], wr=wr[:, :], br=br[:, 0:1],
                 eps=eps_col[:, 0:1], wq=wq, wm=wm, w1=w1, w2=w2, f1=f1, f2=f2, kv=kv, ksum=ksum, xnt_d=xnt_d,
                 x=x, res_scale=res_scale, res_offset=res_offset, base_d=base_d, hold_v=hold_v, max_seen=max_seen,
                 **{n: t[:, :] for n, t in small.items()})
        s_full = (P, P)
        s_last = (LAST, 0)

        def edge_bodies(eng, block_part, mix_part, chain_part):
            def body(i, kind, v=None):
                steps = {"mix": 3 * MIX_EACH, "chain": STEPS, "plain": 0}[kind]
                for q, todo in enumerate(body_slots(steps)):
                    k = q // 3
                    block_part(eng, q % 3, i, k)
                    for step in todo:
                        if kind == "mix":
                            mix_part(eng, step % 3, i * MIX_EACH + step // 3, step // 3)
                        else:
                            if isinstance(i, int) and i == MIX_BODIES and step == 3:
                                mix_part(eng, 4, None)
                            chain_part(eng, step, v, parts_of(v), i * SLOTS + k + 1, i * (SLOTS * NG) - NG)

            body(0, "mix")
            with eng.Fori(1, MIX_BODIES) as i:
                body(i, "mix")
            mix_part(eng, 3, None)
            for v in range(3):
                body(MIX_BODIES + v, "chain", v)
            with eng.Fori(MIX_BODIES + 3, GAP_BODY) as i:
                body(i, "chain", i - MIX_BODIES)
            body(GAP_BODY, "plain")
            with eng.Fori(GAP_BODY + 1, BODIES - 1) as i:
                body(i, "chain", i - MIX_BODIES - 1)
            body(BODIES - 1, "chain", BODIES - MIX_BODIES - 2)
            block_part(eng, 3, None, None)
            for v in range(BODIES - MIX_BODIES - 1, ROUNDS):
                for step in range(STEPS):
                    chain_part(eng, step, v, parts_of(v), BLOCKS, GR)

        TURNED = (0, 1, 0, 1, 2)

        def passes(eng, *stages):
            def place(i, j, which):
                for k in which:
                    q = i - 1 if j < k else i
                    if not isinstance(q, int) or q >= 0:
                        n = (j - k) % PRE
                        stages[k](q, n, q * PRE + n)

            every = range(len(stages))
            for j in range(PRE):
                place(0, j, every)
            with eng.Fori(1, UNITS // PRE) as i:
                for j in range(PRE):
                    place(i, j, every)
            for j in range(len(stages) - 1):
                place(UNITS // PRE, j, every[j + 1:])

        def load_x(eng, u, j):
            eng.dma_start(x_u[:, j, :, :], x[bass.ds(u * UN, UN), :].rearrange("(t p) c -> p t c", p=P)).then_inc(s_x[j], 16)

        def nothing(eng, *rest):
            pass

        with nc.Block() as block:
            @block.sync
            def _(sp):
                for j in range(PRE):
                    for q in (s_xnt_out[j], s_rows_out[j]):
                        sp.sem_inc(q, 16)
                sp.sem_inc(c["base_out"], 16)

                sp.dma_start(wsum_s, wsum.rearrange("d f c -> f d c")).then_inc(s_w["wsum"], 16)
                sp.dma_start(attn_s, attn_t).then_inc(s_w["attn"], 16)
                for d in range(2):
                    sp.dma_start(wg_s[:, :, d, 0:F], wg[:, d * F:(d + 1) * F].rearrange("(k p) f -> p k f", p=P)).then_inc(s_w["wg"], 16)

                def keep(i, j):
                    u = i * PRE + j
                    c_rows.wait(sp, u + 1)
                    sp.sem_inc(hold_s, 1)
                    sp.dma_start(table_d[bass.ds(u * UN, UN), :].rearrange("(t p) r -> p t r", p=P),
                                 rows[:, j, :, :, :].rearrange("p t d r -> p t (d r)")).then_inc(s_rows_out[j], 16)
                    c_xnt.wait(sp, u + 1)
                    sp.sem_inc(hold_s, 1)
                    sp.dma_start(xnt_d[:, :, bass.ds(u * UN, UN)], xnt[:, j, :, :]).then_inc(s_xnt_out[j], 16)

                with sp.Fori(0, UNITS // PRE) as i:
                    for j in range(PRE):
                        keep(i, j)

                def part(eng, third, i, k):
                    if third == 0:
                        b = i * SLOTS + k
                        e_msg.wait(sp, b - SLOTS + 1)
                        sp.sem_inc(hold_s, 1)
                        sp.dma_start(idx[k][:, :], src_t[:, bass.ds(b * BT, BT)]).then_inc(s_idx[k], 16)
                        sp.dma_start(att[k][:, :, :], attr_t[:, bass.ds(b * BT, BT), :]).then_inc(s_att[k], 16)

                edge_bodies(sp, part, nothing, nothing)
                sp.wait_ge(c["base_out"], 16 * (UNITS + 1))
                for q, n in (("mix", 2), ("chain", 11), ("ff", 2)):
                    sp.wait_ge(s_w[q], 16 * n)

            @block.gpsimd
            def _(pool):
                pool.dma_start(dst_i, dst_t).then_inc(s_w["dst"], 16)
                for j in range(PRE):
                    load_x(pool, j, j)
                pool.dma_start(attr, attr_t).then_inc(s_w["attr"], 16)
                pool.memset(ident[:, :], 0.0).then_inc(s_const, 1)
                pool.memset(ones[:, :], 1.0).then_inc(s_const, 1)
                pool.memset(eps_col[:, :], LN_EPS).then_inc(s_const, 1)
                pool.iota(iota_i[:, :], pattern=[[1, WIN]], base=0, channel_multiplier=0).then_inc(s_const, 1)
                pool.memset(valid[:, :], 1.0).then_inc(s_const, 1)
                pool.memset(heads, 0.0).then_inc(s_const, 1)
                for part, first, n, done in ((limit_i[:, 0:early], 0, GAP_BODY + 1, -MIX_BODIES - 1),
                                             (limit_i[:, early:], GAP_BODY + 1, BODIES - GAP_BODY, -MIX_BODIES - 2)):
                    pool.iota(part.rearrange("p (b g) -> p b g", g=SLOTS * NG), pattern=[[UN, n], [0, SLOTS * NG]],
                              base=UN * (first + done), channel_multiplier=0).then_inc(s_const, 1)
                pool.wait_ge(s_const, 8)
                pool.affine_select(out=ident[:, :], in_=ident[:, :], compare_op=ALU.not_equal, fill=1.0, base=0,
                                   pattern=[[-1, P]], channel_multiplier=1).then_inc(s_const, 1)
                pool.affine_select(out=valid[:, :], in_=valid[:, :], compare_op=ALU.is_gt, fill=0.0, base=N,
                                   pattern=[[-P, NT]], channel_multiplier=-1).then_inc(s_const, 1)
                pool.wait_ge(s_const, 10)
                for g in range(P // HD):
                    pool.memset(heads[g * HD:(g + 1) * HD, g * HD:(g + 1) * HD], 1.0).then_inc(s_const, 1)
                pool.wait_ge(s_const, 14)
                pool.memset(acc_w[:, :], 0.0).then_inc(s_zero, 1)
                pool.memset(smax[:, :, :], LOW).then_inc(s_zero, 1)
                pool.memset(low[:, :, :], 1.0e30).then_inc(s_zero, 1)
                pool.memset(kv_sum, 0.0).then_inc(s_zero, 1)
                pool.memset(flat[:, scratch:], 0.0).then_inc(s_zero, 1)
                with pool.Fori(0, UNITS // PRE - 1) as i:
                    for j in range(PRE):
                        c_xn.wait(pool, i * PRE + j + 1)
                        pool.sem_inc(hold_p, 1)
                        load_x(pool, (i + 1) * PRE + j, j)
                pool.wait_ge(s_found, 1)
                for j in range(PRE):
                    pool.wait_ge(s_rows_out[j], 16 * (UNITS // PRE + 1))

                def part(eng, third, i, k):
                    if third == 0:
                        b = i * SLOTS + k
                        pool.wait_ge(s_idx[k], (i + 1) * 16)
                        pool.sem_inc(hold_p, 1)
                        e_msg.wait(pool, b - SLOTS + 1)
                        pool.sem_inc(hold_p, 1)
                        for t in range(BT):
                            pool.indirect_dma_start(got[k][:, t, :, :].rearrange("p d r -> p (d r)"), None, table_d,
                                                    bass.IndirectOffsetOnAxis(ap=idx[k][:, t:t + 1], axis=0)).then_inc(s_got[k], 16)
                edge_bodies(pool, part, nothing, nothing)

            @block.vector
            def _(dve):
                link = linker(dve, s_dv)
                dve.sem_inc(e_msg.sem, SLOTS)
                dve.sem_inc(e_merge.sem, NG + 1)
                dve.sem_inc(m_sum.sem, 1)
                for k in range(3):
                    c[f"V{k}"].open(dve)
                dve.wait_ge(s_w["dst"], 16)
                link(dve.tensor_copy(dst_rel[:, :], dst_i))
                link(dve.memset(gmin, PAD_NODE))
                link(dve.memset(gmax, 0.0))
                db = dst_rel[:, :].rearrange("p (b t) -> p b t", t=BT)
                gv = gmin[:, 0:GR].rearrange("p (b g) -> p b g", g=NG)
                xv = gmax[:, 0:GR].rearrange("p (b g) -> p b g", g=NG)
                for g, (a, z) in enumerate(GROUPS):
                    link(dve.tensor_reduce(gv[:, :, g], db[:, :, a:z], AX, ALU.min))
                link(dve.tensor_scalar(dst_real, dst_rel[:, :], 0.5 * PAD_NODE, None, ALU.is_lt))
                link(dve.tensor_tensor(dst_real, dst_real, dst_rel[:, :], ALU.mult))
                dr = dst_real.rearrange("p (b t) -> p b t", t=BT)
                for g, (a, z) in enumerate(GROUPS):
                    link(dve.tensor_reduce(xv[:, :, g], dr[:, :, a:z], AX, ALU.max))
                dve.sem_inc(s_found, 1)
                dve.wait_ge(s_w["wg"], 32)
                dve.wait_ge(s_score_w, 1)
                dve.tensor_copy(wg_s[:, :, :, F:ROW], bank[7][:, 0:KC * 2 * H].rearrange("p (k d h) -> p k d h", k=KC, d=2))\
                    .then_inc(s_score_c, 1)
                def moments(i, n, u):
                    dve.wait_ge(s_x[n], (i + 1) * 16)
                    for t in range(UT):
                        ins = dve.bn_stats(stats[:, n, t, :], x_u[:, n, t, :])
                    ins.then_inc(c_stats.sem, 1)
                    c_stats.wait(dve, u + 1)
                    dve.sem_inc(hold_v, 1)
                    for t in range(UT):
                        ins = dve.bn_aggr(mv[:, n, t, :], stats[:, n, t, :])
                    ins.then_inc(c_mv.sem, 1)

                def normalise(i, n, u):
                    c_sd.wait(dve, u + 1)
                    dve.reciprocal(rstd[:, n, :], sd[:, n, :]).then_inc(c_rstd.sem, 1)
                    c_rstd.wait(dve, u + 1)
                    for t in range(UT):
                        ins = dve.tensor_scalar(xn[:, n, t, :], x_u[:, n, t, :], mv[:, n, t, 0:1], rstd[:, n, t:t + 1],
                                                ALU.subtract, ALU.mult)
                    ins.then_inc(c_xn.sem, 1)
                    dve.tensor_scalar(res_scale[:, bass.ds(u * UT, UT)], rstd[:, n, :], 1.0, None, ALU.add)
                    dve.scalar_tensor_tensor(out=res_offset[:, bass.ds(u * UT, UT)], in0=mv[:, n, :, 0], scalar=-1.0,
                                             in1=rstd[:, n, :], op0=ALU.mult, op1=ALU.mult).then_inc(c_res.sem, 1)

                passes(dve, moments, normalise)
                dve.wait_ge(s_w["attr"], 16)
                for d in range(2):
                    link(dve.tensor_reduce(ext[:, d:d + 1], attr[:, :, d], AX, ALU.max))
                    link(dve.tensor_reduce(ext[:, 2 + d:3 + d], attr[:, :, d], AX, ALU.min))
                dve.sem_inc(s_ask, 1)
                dve.wait_ge(s_given, 1)
                for k in range(GC):
                    link(dve.tensor_reduce(bcol[:, k:k + 1], bank[0][:, k * P:(k + 1) * P], AX, ALU.min))
                    link(dve.tensor_reduce(mcol[:, k:k + 1], bank[1][:, k * P:(k + 1) * P], AX, ALU.max))
                link(dve.tensor_scalar(bcol, bcol, float(NP - WIN), None, ALU.min))
                link(dve.tensor_tensor(mcol, mcol, bcol, ALU.subtract))
                link(dve.tensor_reduce(verdict[:, 0:1], mcol, AX, ALU.max))
                link(dve.tensor_scalar(verdict[:, 0:1], verdict[:, 0:1], WIN - 0.5, None, ALU.subtract))
                dve.sem_inc(s_ask, 1)
                dve.wait_ge(s_given, 2)
                link(dve.tensor_copy(gmin[0:GC, 0:P], bank[2][0:GC, 0:P]))
                dve.sem_inc(s_first, 1)

                def spread(n, dst):
                    dve.wait_ge(s_given, 1 + 2 * n)
                    link(dve.tensor_reduce(v4[:, :], bank[0][0:4, 0:P], AX, ALU.max))
                    link(dve.tensor_scalar(vd[:, :], ident[0:4, 0:4], v4[:, 0:1], None, ALU.mult))
                    dve.sem_inc(s_ask, 1)
                    dve.wait_ge(s_given, 2 + 2 * n)
                    link(dve.tensor_copy(dst, bank[0][:, P:P + 4]))

                link(dve.tensor_scalar(ext[:, 2:4], ext[:, 2:4], -1.0, None, ALU.mult))
                dve.sem_inc(s_ask, 1)
                spread(1, ext_bc)
                link(dve.tensor_scalar(ext_bc[:, 2:4], ext_bc[:, 2:4], -1.0, None, ALU.mult))
                c_scores.wait(dve, UNITS)
                for d in range(2):
                    link(dve.tensor_scalar(p_lo[:, :, d, :], p_all[:, :, d, :], ext_bc[:, 2 + d:3 + d], None, ALU.mult))
                    link(dve.scalar_tensor_tensor(out=p_lo[:, :, d, :], in0=p_all[:, :, d, :], scalar=ext_bc[:, d:d + 1],
                                                  in1=p_lo[:, :, d, :], op0=ALU.mult, op1=ALU.max))
                link(dve.tensor_tensor(p_lo[:, :, 0, :], p_lo[:, :, 0, :], p_lo[:, :, 1, :], ALU.add))
                link(dve.tensor_reduce(ext, p_lo[:, :, 0, :].rearrange("p t h -> p h t"), AX, ALU.max))
                dve.sem_inc(s_ask, 1)
                spread(2, ext_bc)
                link(dve.scalar_tensor_tensor(out=bound[:, :], in0=ext_bc, scalar=SLOPE, in1=ext_bc, op0=ALU.mult, op1=ALU.max))
                dve.wait_ge(s_first_in, 16)
                lim = limit[:, 0:GR]
                link(dve.tensor_copy(lim, limit_i[:, NG:GR + NG]))
                link(dve.tensor_tensor(lim, lim, first_bc[:, 0:GR], ALU.subtract))
                link(dve.tensor_reduce(verdict[:, 1:2], lim, AX, ALU.max))
                link(dve.tensor_scalar(lim, lim, 0.0, None, ALU.max))
                link(dve.tensor_tensor(first_bc[:, 0:GR], first_bc[:, 0:GR], lim, ALU.add))
                bb = first_bc[:, 0:GR].rearrange("p (b g) -> p b g", g=NG)
                db = dst_rel[:, :].rearrange("p (b t) -> p b t", t=BT)
                for g, (a, z) in enumerate(GROUPS):
                    link(dve.tensor_tensor(db[:, :, a:z], db[:, :, a:z],
                                           bb[:, :, g:g + 1].to_broadcast([P, BLOCKS, z - a]), ALU.subtract))
                link(dve.tensor_copy(first_i[:, :], first_bc[0:1, :]))
                link(dve.tensor_copy(iota[:, :], iota_i[:, :]))
                dve.wait_ge(s_zero, 5)
                link(dve.memset(flat[:, 0:scratch], 0.0))
                for j in range(PRE):
                    for q in (s_xnt_out[j], s_rows_out[j]):
                        dve.wait_ge(q, 16 * (UNITS // PRE + 1))
                dve.sem_inc(s_begin, 1)

                def merge(n, w, blocks):
                    firsts = [dve.value_load(first_i[0:1, bass.ds(n + g, 1)], min_val=0, max_val=NP - WIN) for g in range(NG)]
                    e_grp.wait(dve, blocks)
                    for g, first in enumerate(firsts):
                        ps = bank[w][:, g * 3 * WIN:(g + 1) * 3 * WIN]
                        e_merge.wait(dve, n + g)
                        a = acc[:, :, bass.ds(first, WIN)]
                        dve.tensor_tensor(a, a, ps[:, 0:2 * WIN].rearrange("p (h w) -> p h w", h=2), ALU.add).then_inc(e_acc.sem, 1)
                        a = acc_w[:, bass.ds(first, WIN)]
                        dve.tensor_tensor(a, a, ps[0:H, 2 * WIN:3 * WIN], ALU.add).then_inc(e_merge.sem, 1)

                def part(eng, third, i, k):
                    if third == 3:
                        merge((BLOCKS - 1) * NG, (BLOCKS - 1) % 2, BLOCKS)
                        return
                    b = i * SLOTS + k
                    w = k % 2
                    if third == 0:
                        dve.wait_ge(s_att[k], (i + 1) * 16)
                        dve.wait_ge(s_got[k], (i + 1) * (16 * BT))
                        dve.tensor_tensor(got[k][:, :, :, :], got[k][:, :, :, :],
                                          att[k][:, :, :].rearrange("p t (d o) -> p t d o", o=1).to_broadcast([P, BT, 2, ROW]),
                                          ALU.mult).then_inc(e_prod.sem, 1)
                        e_prod.wait(dve, b + 1)
                        e_scat.wait(dve, b - 1)
                        dve.tensor_tensor(msg[:, w, :, :], got[k][:, :, 0, :], got[k][:, :, 1, :], ALU.add).then_inc(e_msg.sem, 1)
                        dve.tensor_tensor(onehot[:, w, :, :],
                                          dst_rel[:, bass.ds(b * BT, BT)].rearrange("p (t o) -> p t o", o=1).to_broadcast([P, BT, WIN]),
                                          iota[:, :].rearrange("p (o w) -> p o w", o=1).to_broadcast([P, BT, WIN]),
                                          ALU.is_equal).then_inc(e_onehot.sem, 1)
                        e_msg.wait(dve, b + 1)
                        sc = msg[:, w, :, F:ROW]
                        dve.scalar_tensor_tensor(out=lrelu[:, :, :], in0=sc, scalar=SLOPE, in1=sc, op0=ALU.mult, op1=ALU.max)\
                            .then_inc(e_lrelu.sem, 1)
                        dve.tensor_tensor(smax[:, :, :], smax[:, :, :], sc, ALU.max).then_inc(e_max.sem, 1)
                        e_lrelu.wait(dve, b + 1)
                        e_wgt.wait(dve, b - 1)
                        dve.tensor_tensor(score[:, w, :, :], lrelu[:, :, :],
                                          bound[:, :].rearrange("p (o h) -> p o h", o=1).to_broadcast([P, BT, H]), ALU.subtract)\
                            .then_inc(e_score.sem, 1)
                    if third == 1:
                        e_onehot.wait(dve, b + 1)
                        e_wgt.wait(dve, b + 1)
                        dve.tensor_tensor(woh[:, w, :, :, :],
                                          onehot[:, w, :, :].rearrange("p t (o w) -> p t o w", o=1).to_broadcast([P, BT, H, WIN]),
                                          wgt[:, w, :, :].rearrange("p t (h o) -> p t h o", o=1).to_broadcast([P, BT, H, WIN]),
                                          ALU.mult).then_inc(e_woh.sem, 1)
                        if k or not isinstance(i, int) or i:
                            merge(i * (SLOTS * NG) + (k - 1) * NG, (k - 1) % 2, b)

                def key_features(v):
                    m_exp.wait(dve, v + 1)
                    m_v.wait(dve, v + 1)
                    for t in range(UT):
                        ins = dve.scalar_tensor_tensor(out=T2[:, t * C:(t + 1) * C], in0=bank[2 + t][:, 0:C], scalar=0.0,
                                                       in1=T1[:, t * C:(t + 1) * C], op0=ALU.max, op1=ALU.add)
                    ins.then_inc(m_k.sem, 1)

                def add_unit(v):
                    m_kv.wait(dve, v + 1)
                    m_sum.wait(dve, v)
                    dve.tensor_tensor(kv_sum, kv_sum, bank[4][:, 0:KC * (P + 1)].rearrange("p (j n) -> p j n", j=KC), ALU.add)\
                        .then_inc(m_sum.sem, 1)

                def mix(eng, step, v, place=0):
                    later = not isinstance(v, int) or v > 0
                    if step == 0 and later:
                        key_features(v - 1)
                    if step == 2:
                        m_proj.wait(dve, v + 1)
                        for t in range(UT):
                            ins = dve.tensor_scalar(T0[:, t * C:(t + 1) * C], bank[2 + t][:, 0:C], 0.0, None, ALU.min)
                        ins.then_inc(m_min.sem, 1)
                        if later:
                            add_unit(v - 1)
                    if step == 3:
                        key_features(UNITS - 1)
                    if step == 4:
                        dve.wait_ge(s_w["chain"], 16 * 11)
                        add_unit(UNITS - 1)
                        m_sum.wait(dve, UNITS)
                        for j in range(KC):
                            dve.scalar_tensor_tensor(out=kv[:, j, :], in0=kv_sum[:, j, 0:P], scalar=1.0 / N, in1=heads,
                                                     op0=ALU.mult, op1=ALU.mult)
                            ins = dve.tensor_scalar(ksum[:, j, :], heads, kv_sum[:, j, P:P + 1], None, ALU.mult)
                        ins.then_inc(s_kv, 1)

                def chain(eng, step, v, parts, seen, groups):
                    vector_round(dve, s, c, step, v, parts, seen, s_last if isinstance(v, int) and v == UNITS + 1 else s_full)

                edge_bodies(dve, part, mix, chain)
                link(dve.tensor_tensor(verdict[:, 3:4], verdict[:, 0:1], verdict[:, 1:2], ALU.max))
                c["V2"].wait(dve, "low", UNITS)
                link(dve.tensor_scalar(vb[:, :], small["gap"][:, :], -1.0, -GAP_MAX, ALU.mult, ALU.add))
                link(dve.tensor_reduce(verdict[:, 1:2], vb[:, :], AX, ALU.max))
                for t in range(UT):
                    link(dve.tensor_tensor(tol[:, t, :], small["guard"][:, :], low[:, t, :], ALU.subtract))
                link(dve.tensor_reduce(verdict[:, 2:3], tol[:, :, :].rearrange("p t h -> p (t h)"), AX, ALU.max))
                dve.sem_inc(s_ask, 1)
                spread(3, vb[:, :])
                link(dve.tensor_reduce(v_one[:, :], vb[:, :], AX, ALU.max))
                link(dve.tensor_scalar(v_one[:, :], v_one[:, :], 0.0, None, ALU.is_gt))
                link(dve.tensor_copy(flag_i[:, :], v_one[:, :]))

            @block.scalar
            def _(act):
                act.sem_inc(e_wgt.sem, 2)
                for k in range(3):
                    c[f"A{k}"].open(act)
                act.wait_ge(s_const, 3)
                def deviation(i, n, u):
                    c_mv.wait(act, u + 1)
                    act.activation(sd[:, n, :], mv[:, n, :, 1], ACT.Sqrt, bias=eps_col[:, 0:1]).then_inc(c_sd.sem, 1)

                def keep_turned(i, n, u):
                    c_tr.wait(act, u + 1)
                    act.wait_ge(s_xnt_out[n], (i + 1) * 16)
                    act.activation(xnt[:, n, :, :], bank[TURNED[n]][:, :].rearrange("p (k n) -> p k n", k=KC), ACT.Copy)\
                        .then_inc(c_xnt.sem, 1)

                def keep_rows(i, n, u):
                    c_tab.wait(act, u + 1)
                    act.wait_ge(s_rows_out[n], (i + 1) * 16)
                    act.activation(rows[:, n, :, :, :],
                                   bank[3 + n][:, 0:UT * 2 * ROW].rearrange("p (t d r) -> p t d r", t=UT, d=2),
                                   ACT.Copy).then_inc(c_rows.sem, 1)
                    act.activation(p_all[:, bass.ds(u * UT, UT), :, :],
                                   bank[3 + n][:, 0:UT * 2 * ROW].rearrange("p (t d r) -> p t d r", t=UT, d=2)[:, :, :, F:ROW],
                                   ACT.Copy).then_inc(c_scores.sem, 1)

                passes(act, deviation, keep_turned, keep_rows)
                for j in range(PRE):
                    act.wait_ge(s_xnt_out[j], 16 * (UNITS // PRE + 1))
                act.wait_ge(s_first, 1)
                act.dma_start(first_d.rearrange("(c p) -> c p", c=GC), gmin[0:GC, 0:P]).then_inc(s_first_out, 16)
                act.wait_ge(s_first_out, 16)
                act.dma_start(first_bc, first_d.rearrange("(a n) -> a n", a=1).to_broadcast([P, GC * P])).then_inc(s_first_in, 16)
                for dst, src, q in ((wkv, wkv_d, "mix"), (wq, wq_d, "mix"), (wm, wm_d, "chain"), (w1, w1_d, "chain"),
                                    (w2, w2_d, "chain"), (f2, f2_d, "ff")):
                    act.dma_start(dst if dst is wkv else dst[:, :, :], src.rearrange("(k p) c -> p k c", p=P)).then_inc(s_w[q], 16)
                for dst, src in ((g1, g1_d), (b1, b1_d), (fb1, fb1_d)):
                    act.dma_start(dst[:, :], src).then_inc(s_w["chain"], 16)
                for dst, src in ((g2, g2_d), (b2, b2_d), (fb2, fb2_d), (wr, wr_d), (br, br_d)):
                    act.dma_start(dst[:, :], src.rearrange("(a n) -> a n", a=1).to_broadcast([P, src.shape[0]])).then_inc(s_w["chain"], 16)

                def part(eng, third, i, k):
                    if third == 0:
                        b = i * SLOTS + k
                        e_score.wait(act, b + 1)
                        e_scat.wait(act, b - 1)
                        act.activation(wgt[:, k % 2, :, :], score[:, k % 2, :, :], ACT.Exp).then_inc(e_wgt.sem, 1)

                def mix(eng, step, v, place=0):
                    later = not isinstance(v, int) or v > 0
                    if step == 0 and place == 0:
                        if later:
                            m_proj.wait(act, v)
                        act.dma_start(T4[:, :, :], xnt_d[:, :, bass.ds(v * UN, UN)]).then_inc(m_x, 16)
                    if step == 2:
                        if later:
                            m_k.wait(act, v)
                        m_min.wait(act, v + 1)
                        act.activation(T1[:, :], T0[:, :], ACT.Exp).then_inc(m_exp.sem, 1)
                        if place < MIX_EACH - 1:
                            act.dma_start(T4[:, :, :], xnt_d[:, :, bass.ds((v + 1) * UN, UN)]).then_inc(m_x, 16)
                        if later:
                            m_kv.wait(act, v)
                        for t in range(UT):
                            ins = act.activation(T3[:, t * C:(t + 1) * C], bank[2 + t][:, C:2 * C], ACT.Copy)
                        ins.then_inc(m_v.sem, 1)
                    if step == 3:
                        m_proj.wait(act, UNITS)
                        act.dma_start(f1[:, :, :], f1_d.rearrange("(k p) c -> p k c", p=P)).then_inc(s_w["ff"], 16)
                    if step == 4:
                        act.wait_ge(s_w["chain"], 16 * 11)

                def chain(eng, step, v, parts, seen, groups):
                    scalar_round(act, s, c, step, v, parts, lambda a: e_merge.wait(a, groups))

                edge_bodies(act, part, mix, chain)

            @block.tensor
            def _(pe):
                pe.sem_inc(e_scat.sem, 2)
                for k in range(3):
                    c[f"P{k}"].open(pe)
                pe.wait_ge(s_const, 14)
                pe.wait_ge(s_w["wsum"], 16)
                pe.wait_ge(s_w["attn"], 16)
                for k in range(KC):
                    for d in range(2):
                        c0 = (k * 2 + d) * H
                        ins = pe.matmul(bank[7][:, c0:c0 + H], wsum_s[:, d, k * P:(k + 1) * P], attn_s, start=True, stop=True)
                ins.then_inc(s_score_w, 1)
                pe.wait_ge(s_score_c, 1)
                def turn(i, n, u):
                    c_xn.wait(pe, u + 1)
                    for t in range(UT):
                        for k in range(KC):
                            ins = pe.transpose(bank[TURNED[n]][:, k * UN + t * P:k * UN + (t + 1) * P],
                                               xn[:, n, t, k * P:(k + 1) * P], ident[:, :])
                    ins.then_inc(c_tr.sem, 1)

                def table(i, n, u):
                    c_xnt.wait(pe, u + 1)
                    for t in range(UT):
                        for k in range(KC):
                            ins = pe.matmul(bank[3 + n][:, t * 2 * ROW:(t + 1) * 2 * ROW], xnt[:, n, k, t * P:(t + 1) * P],
                                            wg_s[:, k, :, :].rearrange("p d r -> p (d r)"), start=(k == 0), stop=(k == KC - 1))
                    ins.then_inc(c_tab.sem, 1)

                passes(pe, turn, table)
                pe.wait_ge(s_ask, 1)
                for b, g in ((0, gmin), (1, gmax)):
                    for k in range(GC):
                        ins = pe.transpose(bank[b][:, k * P:(k + 1) * P], g[:, k * P:(k + 1) * P], ident[:, :])
                ins.then_inc(s_given, 1)
                pe.wait_ge(s_ask, 2)
                pe.transpose(bank[2][0:GC, 0:P], bcol, ident[:, :]).then_inc(s_given, 1)

                def spread(n, cols):
                    pe.wait_ge(s_ask, 1 + 2 * n)
                    pe.transpose(bank[0][0:4, 0:P], cols, ident[:, :]).then_inc(s_given, 1)
                    pe.wait_ge(s_ask, 2 + 2 * n)
                    pe.matmul(bank[0][:, P:P + 4], ones[0:4, :], vd[:, :], start=True, stop=True).then_inc(s_given, 1)

                spread(1, ext)
                spread(2, ext)
                pe.wait_ge(s_begin, 1)
                pe.wait_ge(s_w["mix"], 32)

                def part(eng, third, i, k):
                    if third != 2:
                        return
                    b = i * SLOTS + k
                    w = k % 2
                    e_woh.wait(pe, b + 1)
                    e_merge.wait(pe, (b - 1) * NG)
                    for g, (a, z) in enumerate(GROUPS):
                        ps = bank[w][:, g * 3 * WIN:(g + 1) * 3 * WIN]
                        for half in range(2):
                            for t in range(a, z):
                                pe.matmul(ps[half * F:(half + 1) * F, 0:2 * WIN], msg[:, w, t, 0:F],
                                          woh[:, w, t, 2 * half:2 * half + 2, :].rearrange("p h w -> p (h w)"),
                                          start=(t == a), stop=(t == z - 1))
                        for t in range(a, z):
                            ins = pe.matmul(ps[0:H, 2 * WIN:3 * WIN], wgt[:, w, t, :], onehot[:, w, t, :], start=(t == a), stop=(t == z - 1))
                    ins.then_inc(e_grp.sem, 1)
                    e_grp.wait(pe, b + 1)
                    pe.sem_inc(e_scat.sem, 1)

                def keys_by_values(v):
                    m_v.wait(pe, v + 1)
                    m_k.wait(pe, v + 1)
                    m_sum.wait(pe, v)
                    for j in range(KC):
                        to = j * (P + 1)
                        for t in range(UT):
                            cols = slice(t * C + j * P, t * C + (j + 1) * P)
                            pe.matmul(bank[4][:, to:to + P], T2[:, cols], T3[:, cols], start=(t == 0), stop=(t == UT - 1))
                        for t in range(UT):
                            cols = slice(t * C + j * P, t * C + (j + 1) * P)
                            ins = pe.matmul(bank[4][:, to + P:to + P + 1], T2[:, cols], valid[:, bass.ds(v * UT + t, 1)],
                                            start=(t == 0), stop=(t == UT - 1))
                    ins.then_inc(m_kv.sem, 1)

                def mix(eng, step, v, place=0):
                    if step == 1:
                        pe.wait_ge(m_x, (v + 1) * 16)
                        if not isinstance(v, int) or v > 0:
                            m_v.wait(pe, v)
                            m_k.wait(pe, v)
                        for t in range(UT):
                            for k in range(KC):
                                ins = pe.matmul(bank[2 + t][:, :], T4[:, k, t * P:(t + 1) * P], wkv[:, k, :], start=(k == 0), stop=(k == KC - 1))
                        ins.then_inc(m_proj.sem, 1)
                        if not isinstance(v, int) or v > 0:
                            keys_by_values(v - 1)
                    if step == 3:
                        keys_by_values(UNITS - 1)
                    if step == 4:
                        pe.wait_ge(s_kv, 1)
                        pe.wait_ge(s_w["chain"], 16 * 11)
                        pe.wait_ge(s_w["ff"], 32)

                def chain(eng, step, v, parts, seen, groups):
                    tensor_round(pe, s, c, step, v, parts)

                edge_bodies(pe, part, mix, chain)
                spread(3, verdict[:, :])

        idx_g, dst_gi, att_g, got_g = idx[0], idx[1], att[0], got[0]
        dst_g = dst_rel[:, 0:BT]
        s_gen = sem("s_gen")
        s_gdst = sem("s_gdst")
        idx_n, att_n, got_n = BODIES * 16, BODIES * 16, BODIES * 16 * BT
        g_prod, g_msg = Count(e_prod.sem, BLOCKS), Count(e_msg.sem, SLOTS + BLOCKS)
        g_lrelu, g_score, g_wgt = Count(e_lrelu.sem, BLOCKS), Count(e_score.sem, BLOCKS), Count(e_wgt.sem, BLOCKS + e_wgt.credit)
        g_onehot, g_woh = Count(e_onehot.sem, BLOCKS), Count(e_woh.sem, BLOCKS)
        g_grp, g_merge = Count(e_grp.sem, BLOCKS), Count(e_merge.sem, GR + e_merge.credit)
        g_dst = count("g_dst", 1); g_rel = count("g_rel", 1)
        g_acc = Count(e_acc.sem, GR)
        cg = once_more(c)

        def way(eng):
            return eng.value_load(flag_i[0:1, 0:1], min_val=0, max_val=1)

        def again(eng, chain):
            def run(v):
                for step in range(STEPS):
                    chain(step, v, parts_of(v))

            for v in range(3):
                run(v)
            with eng.Fori(3, UNITS - 1) as v:
                run(v)
            for v in range(UNITS - 1, ROUNDS):
                run(v)

        with nc.Block() as block:
            @block.sync
            def _(sp):
                with sp.If(way(sp) > 0):
                    with sp.Fori(0, BLOCKS) as b:
                        g_merge.wait(sp, b * WINS)
                        sp.sem_inc(hold_s, 1)
                        sp.dma_start(idx_g[:, :], src_t[:, bass.ds(b * BT, BT)]).then_inc(s_idx[0], 16)
                        sp.dma_start(att_g[:, :, :], attr_t[:, bass.ds(b * BT, BT), :]).then_inc(s_att[0], 16)
                        sp.dma_start(dst_gi[:, :], dst_t[:, bass.ds(b * BT, BT)]).then_inc(s_gdst, 16)
                    sp.sem_inc(hold_s, 1)

            @block.gpsimd
            def _(pool):
                with pool.If(way(pool) > 0):
                    pool.memset(acc[:, :, :], 0.0).then_inc(s_zero, 1)
                    pool.wait_ge(s_zero, 6)
                    pool.memset(acc_w[:, :], 0.0).then_inc(s_zero, 1)
                    with pool.Fori(0, BLOCKS) as b:
                        pool.wait_ge(s_idx[0], b * 16 + (idx_n + 16))
                        pool.sem_inc(hold_p, 1)
                        g_merge.wait(pool, b * WINS)
                        pool.sem_inc(hold_p, 1)
                        for t in range(BT):
                            pool.indirect_dma_start(got_g[:, t, :, :].rearrange("p d r -> p (d r)"), None, table_d,
                                                    bass.IndirectOffsetOnAxis(ap=idx_g[:, t:t + 1], axis=0)).then_inc(s_got[0], 16)
                    pool.sem_inc(hold_p, 1)

            @block.vector
            def _(dve):
                with dve.If(way(dve) > 0):
                    dve.sem_inc(g_dst.sem, 1)
                    dve.sem_inc(g_rel.sem, 1)
                    dve.tensor_copy(bound[:, :], small["lead"][:, :]).then_inc(s_gen, 1)
                    dve.wait_ge(s_gen, 1)
                    dve.wait_ge(s_zero, 7)
                    with dve.Fori(0, BLOCKS) as b:
                        dve.wait_ge(s_gdst, (b + 1) * 16)
                        g_rel.wait(dve, b * WINS)
                        dve.tensor_scalar(dst_g, dst_gi[:, :], 1.0, float(WIN), ALU.mult, ALU.add).then_inc(g_dst.sem, 1)
                        dve.wait_ge(s_att[0], b * 16 + (att_n + 16))
                        dve.wait_ge(s_got[0], b * (16 * BT) + (got_n + 16 * BT))
                        dve.tensor_tensor(got_g[:, :, :, :], got_g[:, :, :, :],
                                          att_g[:, :, :].rearrange("p t (d o) -> p t d o", o=1).to_broadcast([P, BT, 2, ROW]),
                                          ALU.mult).then_inc(g_prod.sem, 1)
                        g_prod.wait(dve, b + 1)
                        g_grp.wait(dve, b * WINS)
                        dve.tensor_tensor(msg[:, 0, :, :], got_g[:, :, 0, :], got_g[:, :, 1, :], ALU.add).then_inc(g_msg.sem, 1)
                        g_msg.wait(dve, b + 1)
                        sc = msg[:, 0, :, F:ROW]
                        dve.scalar_tensor_tensor(out=lrelu[:, :, :], in0=sc, scalar=SLOPE, in1=sc, op0=ALU.mult, op1=ALU.max)\
                            .then_inc(g_lrelu.sem, 1)
                        g_lrelu.wait(dve, b + 1)
                        dve.tensor_tensor(score[:, 0, :, :], lrelu[:, :, :],
                                          bound[:, :].rearrange("p (o h) -> p o h", o=1).to_broadcast([P, BT, H]), ALU.subtract)\
                            .then_inc(g_score.sem, 1)
                        g_dst.wait(dve, b + 1)
                        g_wgt.wait(dve, b + 1)
                        dve.sem_inc(hold_v, 1)
                        with dve.Fori(0, WINS) as w:
                            n = b * WINS + w
                            g_onehot.wait(dve, n)
                            dve.tensor_scalar(dst_g, dst_g, float(WIN), None, ALU.subtract).then_inc(g_rel.sem, 1)
                            g_rel.wait(dve, n + 1)
                            g_grp.wait(dve, n)
                            dve.tensor_tensor(onehot[:, 0, :, :],
                                              dst_g.rearrange("p (t o) -> p t o", o=1).to_broadcast([P, BT, WIN]),
                                              iota[:, :].rearrange("p (o w) -> p o w", o=1).to_broadcast([P, BT, WIN]),
                                              ALU.is_equal).then_inc(g_onehot.sem, 1)
                            g_onehot.wait(dve, n + 1)
                            dve.tensor_tensor(woh[:, 0, :, :, :],
                                              onehot[:, 0, :, :].rearrange("p t (o w) -> p t o w", o=1).to_broadcast([P, BT, H, WIN]),
                                              wgt[:, 0, :, :].rearrange("p t (h o) -> p t h o", o=1).to_broadcast([P, BT, H, WIN]),
                                              ALU.mult).then_inc(g_woh.sem, 1)
                            g_grp.wait(dve, n + 1)
                            g_merge.wait(dve, n)
                            a = acc[:, :, bass.ds(w * WIN, WIN)]
                            dve.tensor_tensor(a, a, bank[0][:, 0:2 * WIN].rearrange("p (h w) -> p h w", h=2), ALU.add).then_inc(g_acc.sem, 1)
                            a = acc_w[:, bass.ds(w * WIN, WIN)]
                            dve.tensor_tensor(a, a, bank[0][0:H, 2 * WIN:3 * WIN], ALU.add).then_inc(g_merge.sem, 1)
                        dve.sem_inc(hold_v, 1)
                    dve.sem_inc(hold_v, 1)
                    again(dve, lambda step, v, parts: vector_round(dve, s, cg, step, v, parts, BLOCKS, s_full))
                    dve.sem_inc(hold_v, 1)

            @block.scalar
            def _(act):
                with act.If(way(act) > 0):
                    with act.Fori(0, BLOCKS) as b:
                        g_score.wait(act, b + 1)
                        g_grp.wait(act, b * WINS)
                        act.activation(wgt[:, 0, :, :], score[:, 0, :, :], ACT.Exp).then_inc(g_wgt.sem, 1)
                    act.sem_inc(hold_a, 1)
                    again(act, lambda step, v, parts: scalar_round(act, s, cg, step, v, parts, lambda a: g_merge.wait(a, BLOCKS * WINS)))
                    act.wait_ge(c["base_out"], 16 * (2 * UNITS + 1))

            @block.tensor
            def _(pe):
                with pe.If(way(pe) > 0):
                    with pe.Fori(0, BLOCKS) as b:
                        with pe.Fori(0, WINS) as w:
                            n = b * WINS + w
                            g_woh.wait(pe, n + 1)
                            g_merge.wait(pe, n)
                            for half in range(2):
                                for t in range(BT):
                                    pe.matmul(bank[0][half * F:(half + 1) * F, 0:2 * WIN], msg[:, 0, t, 0:F],
                                              woh[:, 0, t, 2 * half:2 * half + 2, :].rearrange("p h w -> p (h w)"),
                                              start=(t == 0), stop=(t == BT - 1))
                            for t in range(BT):
                                ins = pe.matmul(bank[0][0:H, 2 * WIN:3 * WIN], wgt[:, 0, t, :], onehot[:, 0, t, :],
                                                start=(t == 0), stop=(t == BT - 1))
                            ins.then_inc(g_grp.sem, 1)
                        pe.sem_inc(hold_t, 1)
                    pe.sem_inc(hold_t, 1)
                    again(pe, lambda step, v, parts: tensor_round(pe, s, cg, step, v, parts))
                    pe.sem_inc(hold_t, 1)

        work.close()
        edge.close()

        last = ExitStack()
        base = sb("base", [P, NT, C], F32, last)
        before = sb("before", [P, P], F32, last)
        wv = sb("wv", [P, NT], F32, last)
        hit = sb("hit", [P, DIGIT, NT], F32, last)
        above = sb("above", [P, NT], F32, last)
        level = sb("level", [P, NT], F32, last)
        pick = sb("pick", [P, NT], F32, last)
        cnt = sb("cnt", [P, 1], F32, last)
        need = sb("need", [P, 1], F32, last)
        by_tile_sum = sb("by_tile_sum", [NT, P], F32, last)
        counts = sb("counts", [P, DIGIT], F32, last)
        yes = sb("yes", [P, DIGIT + 1], F32, last)
        top_digit = sb("top_digit", [P, DIGIT], F32, last)
        part = sb("part", [P, DIGIT], F32, last)
        chosen = sb("chosen", [P, 1], F32, last)
        key = {n: sb(f"key_{n}", [P, DIGIT], I32, last) for n in ("digit", "try", "a", "b", "code", "sign", "shift", "shift28")}
        key.update({n: sb(f"key_{n}", [P, 1], I32, last) for n in ("found", "minus", "c31", "chosen")})
        l_in = [sem(f"l_in{j}") for j in range(OUT_CHUNKS)]
        l_out = sem("l_out"); l_key = sem("l_key"); l_step = sem("l_step"); l_v = sem("l_v"); l_p = sem("l_p");
        l_done = sem("l_done"); l_before = sem("l_before")
        l_try = count("l_try"); l_a = count("l_a"); l_b = count("l_b"); l_code = count("l_code"); l_cnt = count("l_cnt")
        l_sum = count("l_sum"); l_hit = count("l_hit"); l_top = count("l_top"); l_chosen = count("l_chosen"); l_yes = count("l_yes"); l_add = count("l_add"); l_found = count("l_found", 1)
        CT = NT // OUT_CHUNKS

        with nc.Block() as block:
            @block.sync
            def _(sp):
                for j in range(OUT_CHUNKS):
                    sp.dma_start(base[:, j * CT:(j + 1) * CT, :], base_d[j * CT * P:(j + 1) * CT * P, :].rearrange("(t p) c -> p t c", p=P))\
                        .then_inc(l_in[j], 16)
                for j in range(OUT_CHUNKS):
                    full = min((j + 1) * CT, N // P)
                    sp.wait_ge(l_done, j + 1)
                    sp.dma_start(out[j * CT * P:full * P, :].rearrange("(t p) c -> p t c", p=P), base[:, j * CT:full, :]).then_inc(l_out, 16)
                sp.dma_start(out[N // P * P:N, :], base[0:N % P, N // P, :]).then_inc(l_out, 16)
                sp.wait_ge(l_out, 16 * (OUT_CHUNKS + 1))

            @block.gpsimd
            def _(pool):
                for name, value in (("found", 0), ("sign", -2 ** 31), ("minus", -1), ("c31", 31), ("shift", BITS), ("shift28", 32 - BITS)):
                    pool.iota(key[name][:, :], pattern=[[0, key[name].shape[1]]], base=value, channel_multiplier=0).then_inc(l_key, 1)
                pool.iota(key["digit"][:, :], pattern=[[1, DIGIT]], base=0, channel_multiplier=0).then_inc(l_key, 1)
                pool.memset(before[:, :], 1.0).then_inc(l_before, 1)
                pool.wait_ge(l_before, 1)
                pool.affine_select(out=before[:, :], in_=before[:, :], compare_op=ALU.is_gt, fill=0.0, base=0,
                                   pattern=[[1, P]], channel_multiplier=-1).then_inc(l_before, 1)

            @block.vector
            def _(dve):
                n = [0]

                def link(ins):
                    n[0] += 1
                    ins.then_inc(l_v, 1)
                    dve.wait_ge(l_v, n[0])

                dve.sem_inc(l_found.sem, 1)
                link(dve.tensor_scalar(level[:, :], valid[:, :], 1.0, -LOW, ALU.subtract, ALU.mult))
                link(dve.tensor_tensor(wv[:, :], w_all[:, :], valid[:, :], ALU.mult))
                link(dve.tensor_tensor(wv[:, :], wv[:, :], level[:, :], ALU.add))
                dve.wait_ge(l_key, 7)
                k = {name: tile[:, :] for name, tile in key.items()}

                def code_of(source, n, r):
                    a, b, code = (k[name][:, 0:n] for name in ("a", "b", "code"))
                    dve.tensor_scalar(a, source, k["c31"], k["minus"], ALU.arith_shift_right, ALU.bitwise_xor).then_inc(l_a.sem, 1)
                    l_a.wait(dve, r)
                    dve.tensor_tensor(b, a, k["sign"][:, 0:n], ALU.bitwise_or).then_inc(l_b.sem, 1)
                    l_b.wait(dve, r)
                    dve.tensor_tensor(code, b, source, ALU.bitwise_xor).then_inc(l_code.sem, 1)
                    l_code.wait(dve, r)

                link(dve.memset(yes[:, 0:1], 1.0))
                link(dve.memset(yes[:, DIGIT:DIGIT + 1], 0.0))
                link(dve.tensor_tensor(k["digit"], k["digit"], k["shift28"], ALU.logical_shift_left))
                with dve.Fori(0, 32 // BITS) as i:
                    l_found.wait(dve, i)
                    dve.tensor_tensor(k["try"], k["digit"], k["found"].to_broadcast([P, DIGIT]), ALU.bitwise_or).then_inc(l_try.sem, 1)
                    l_try.wait(dve, i + 1)
                    code_of(k["try"], DIGIT, i + 1)
                    dve.tensor_tensor(hit[:, 1:, :], wv[:, :].rearrange("p (o t) -> p o t", o=1).to_broadcast([P, DIGIT - 1, NT]),
                                      k["code"][:, 1:].bitcast(F32).rearrange("p (d o) -> p d o", o=1).to_broadcast([P, DIGIT - 1, NT]),
                                      ALU.is_ge).then_inc(l_hit.sem, 1)
                    l_hit.wait(dve, i + 1)
                    dve.tensor_reduce(counts[:, 1:], hit[:, 1:, :], AX, ALU.add).then_inc(l_cnt.sem, 1)
                    l_sum.wait(dve, i + 1)
                    dve.tensor_scalar(yes[:, 1:DIGIT], bank[0][:, 1:DIGIT], TOP - 0.5, None, ALU.is_gt).then_inc(l_yes.sem, 1)
                    l_yes.wait(dve, i + 1)
                    dve.tensor_tensor(top_digit[:, :], yes[:, 0:DIGIT], yes[:, 1:DIGIT + 1], ALU.subtract).then_inc(l_top.sem, 1)
                    l_top.wait(dve, i + 1)
                    dve.tensor_tensor(part[:, :], top_digit[:, :], k["digit"], ALU.mult).then_inc(l_add.sem, 1)
                    l_add.wait(dve, i + 1)
                    dve.tensor_reduce(chosen[:, :], part[:, :], AX, ALU.add).then_inc(l_chosen.sem, 1)
                    l_chosen.wait(dve, 2 * i + 1)
                    dve.tensor_copy(k["chosen"], chosen[:, :]).then_inc(l_chosen.sem, 1)
                    l_chosen.wait(dve, 2 * i + 2)
                    dve.tensor_tensor(k["found"], k["found"], k["chosen"], ALU.bitwise_or)
                    dve.tensor_tensor(k["digit"], k["digit"], k["shift"], ALU.logical_shift_right).then_inc(l_found.sem, 1)
                l_found.wait(dve, 32 // BITS)
                code_of(k["found"], 1, 32 // BITS + 1)
                thr = k["code"][:, 0:1].bitcast(F32)
                link(dve.tensor_scalar(above[:, :], wv[:, :], thr, None, ALU.is_gt, ALU.add, accum_out=cnt[:, :]))
                link(dve.tensor_scalar(level[:, :], wv[:, :], thr, None, ALU.is_equal))
                dve.sem_inc(l_step, 1)
                dve.wait_ge(l_p, 1)
                link(dve.tensor_copy(by_tile_sum[:, :], bank[1][0:NT, 0:P]))
                link(dve.tensor_scalar(need[:, :], bank[2][:, 0:1], -1.0, float(TOP), ALU.mult, ALU.add))
                dve.sem_inc(l_step, 1)
                dve.wait_ge(l_p, 2)
                link(dve.tensor_scalar(pick[:, :], bank[3][:, 0:NT], need[:, 0:1], None, ALU.is_lt))
                link(dve.tensor_tensor(pick[:, :], pick[:, :], level[:, :], ALU.mult))
                link(dve.tensor_tensor(pick[:, :], pick[:, :], above[:, :], ALU.add))
                for j in range(OUT_CHUNKS):
                    dve.wait_ge(l_in[j], 16)
                    for t in range(j * CT, (j + 1) * CT):
                        ins = dve.scalar_tensor_tensor(out=base[:, t, :], in0=acc[:, t % UT, t // UT * UN:t // UT * UN + C],
                                                       scalar=pick[:, t:t + 1], in1=base[:, t, :], op0=ALU.mult, op1=ALU.add)
                    ins.then_inc(l_done, 1)

            @block.tensor
            def _(pe):
                with pe.Fori(0, 32 // BITS) as i:
                    l_cnt.wait(pe, i + 1)
                    pe.matmul(bank[0][:, 1:DIGIT], ones[:, :], counts[:, 1:], start=True, stop=True).then_inc(l_sum.sem, 1)
                pe.wait_ge(l_step, 1)
                pe.matmul(bank[1][0:NT, 0:P], level[:, :], ones[:, :], start=True, stop=True)
                pe.matmul(bank[2][:, 0:1], ones[:, :], cnt[:, :], start=True, stop=True).then_inc(l_p, 1)
                pe.wait_ge(l_step, 2)
                pe.wait_ge(l_before, 2)
                pe.matmul(bank[3][:, 0:NT], before[:, :], level[:, :], start=True, stop=False)
                pe.matmul(bank[3][:, 0:NT], by_tile_sum[:, :], before[0:NT, 0:NT], start=False, stop=True).then_inc(l_p, 1)
        last.close()


def kernel(**inputs):
    import numpy as np
    import concourse.bacc as bacc
    from concourse.bass_utils import run_bass_kernel_spmd

    def by_tile(a, fill):
        a = np.concatenate([a, fill[:ET * P - E]], axis=0)
        return np.ascontiguousarray(np.moveaxis(a.reshape((ET, P) + a.shape[1:]), 0, 1))

    def by_partition(a):
        return np.ascontiguousarray(a.reshape(-1, P).T)

    a = {k: np.asarray(v) for k, v in inputs.items()}
    x, src, dst, attr = a["x"], a["src"], a["dst"], a["edge_attr_2"]
    wf, wr = a["L0_gnn_W_forward"], a["L0_gnn_W_reverse"]
    arrays = {
        "x": np.concatenate([x, np.zeros((NP - N, C), x.dtype)], axis=0),
        "src_t": by_tile(src, src),
        "dst_t": by_tile(dst, np.full((P,), int(PAD_NODE), dst.dtype)),
        "attr_t": by_tile(attr, attr),
        "wg": np.ascontiguousarray(np.concatenate([wf.T, wr.T], axis=1)),
        "wsum": np.stack([wf, wr]),
        "attn_t": np.ascontiguousarray(a["L0_gnn_attn_forward"][0].T),
        "wkv_d": np.concatenate([a["L0_mix_Wk"], a["L0_mix_Wv"]], axis=1),
        "wq_d": a["L0_mix_Wq"],
        "wm_d": a["L0_mix_Wm"],
        "w1_d": a["L0_mix_W1"],
        "w2_d": a["L0_mix_W2"],
        "g1_d": by_partition(a["L0_mix_g1"]),
        "b1_d": by_partition(a["L0_mix_b1"]),
        "g2_d": a["L0_mix_g2"],
        "b2_d": a["L0_mix_b2"],
        "f1_d": a["L0_ffn_w1"],
        "f2_d": a["L0_ffn_w2"],
        "fb1_d": by_partition(a["L0_ffn_b1"]),
        "fb2_d": a["L0_ffn_b2"],
        "wr_d": np.ascontiguousarray(a["L0_ffn_wr"][:, 0]),
        "br_d": a["L0_ffn_br"],
    }
    nc = bacc.Bacc("TRN2", target_bir_lowering=False, num_devices=1)
    args = {k: nc.dram_tensor(f"in_{k}", v.shape, mybir.dt.from_np(v.dtype), kind="ExternalInput").ap() for k, v in arrays.items()}
    out = nc.dram_tensor("out_0", (N, C), F32, kind="ExternalOutput").ap()
    build_program(nc, out=out, **args)
    r = run_bass_kernel_spmd(nc, [{f"in_{k}": v for k, v in arrays.items()}], core_ids=[0])
    return r.results[0]["out_0"]
```
